# Optimizing a Trainium2 kernel written in Bass

```python
import numpy as np
import jax
import jax.numpy as jnp

def _softmax(x, axis=-1):
    return jax.nn.softmax(x, axis=axis)

def _gelu(x):
    return jax.nn.gelu(x, approximate=True)

def _silu(x):
    return jax.nn.silu(x)

def _sigmoid(x):
    return jax.nn.sigmoid(x)

def _layernorm(x, axis=-1, eps=1e-05):
    m = jnp.mean(x, axis=axis, keepdims=True)
    v = jnp.var(x, axis=axis, keepdims=True)
    return (x - m) / jnp.sqrt(v + eps)

def _scatter_add(tgt, idx, src, axis=0):
    return tgt.at[idx].add(src)

def _segment_sum(src, seg, n):
    return jax.ops.segment_sum(src, seg, n)
kernel_name = 'mk_xattn_ffn_d1_seqx_r4_44fa94'

def setup_inputs(seed: int=0):
    np.random.seed(seed)
    _w = jnp.asarray

    def _rec_inputs():
        import jax
        import jax.numpy as jnp
        _rk = jax.random.key(seed)
        x = 7.22e-05 + 1 * jax.random.normal(jax.random.fold_in(_rk, 1), (32, 128, 256), jnp.float32)
        _lenS = 128 - jax.random.randint(jax.random.fold_in(_rk, 7), (32,), 0, max(1, 128 // 4) + 1, jnp.int32)
        _lenS2 = 128 - jax.random.randint(jax.random.fold_in(_rk, 8), (32,), 0, max(1, 128 // 4) + 1, jnp.int32)
        _ctx_1024P = jax.random.normal(jax.random.fold_in(_rk, 11), (32, 16, 256), jnp.float32)
        _ctx_1024c = jax.random.dirichlet(jax.random.fold_in(_rk, 511), 0.3 * jnp.ones((16,), jnp.float32), (32, 128))
        _ctx_1024t = jnp.einsum('bsk,bkd->bsd', _ctx_1024c, _ctx_1024P)
        _ctx_1024t = _ctx_1024t * jax.lax.rsqrt(jnp.mean(jnp.square(_ctx_1024t)) + 1e-12) * 0.953939
        ctx_1024 = 4.13588e-05 + 0.999923 * (_ctx_1024t + 0.3 * jax.random.normal(jax.random.fold_in(_rk, 611), (32, 128, 256), jnp.float32))
        return (x, ctx_1024)
    x, ctx_1024 = _rec_inputs()

    def _L0_xattn_setup():
        import jax, jax.numpy as jnp
        import numpy as np
        DIM = 256
        NUM_HEADS = 8
        SCALE = (DIM // NUM_HEADS) ** (-0.5)
        key = jax.random.key(seed)
        ks = jax.random.split(key, 7)
        B, N, C = (4, 512, DIM)
        s = C ** (-0.5)
        return {'m_q': jax.random.normal(ks[0], (B, N, C), jnp.float32), 'm_kv': jax.random.normal(ks[1], (B, N, C), jnp.float32), 'Wq': jax.random.normal(ks[2], (C, C), jnp.float32) * s, 'Wk': jax.random.normal(ks[3], (C, C), jnp.float32) * s, 'Wv': jax.random.normal(ks[4], (C, C), jnp.float32) * s, 'Wp': jax.random.normal(ks[5], (C, C), jnp.float32) * s, 'bp': jax.random.normal(ks[6], (C,), jnp.float32) * 0.01}
    _L0_xattn_all = _L0_xattn_setup()
    _L0_xattn_in = {k: v for k, v in _L0_xattn_all.items() if k in ('Wq', 'Wk', 'Wv', 'Wp', 'bp')}
    del _L0_xattn_all

    def _L0_ffn_setup():
        import jax, jax.numpy as jnp
        import numpy as np
        D_MODEL = 256
        FFN = 256
        N_EXPERTS = 8
        N_SHARED = 1
        TOP_K = 2
        B, S = (2, 512)

        def _swiglu(h):
            a, b = jnp.split(h, 2, axis=-1)
            return jax.nn.silu(a) * b
        key = jax.random.key(seed)
        ks = jax.random.split(key, 12)
        sc = 0.02
        return {'x': jax.random.normal(ks[0], (B, S, D_MODEL), dtype=jnp.float32), 'gate_w': jax.random.normal(ks[1], (D_MODEL, N_EXPERTS), dtype=jnp.float32) * sc, 'gate_b': jnp.zeros((N_EXPERTS,), dtype=jnp.float32), 'sw1': jax.random.normal(ks[2], (N_SHARED, D_MODEL, 2 * FFN), dtype=jnp.float32) * sc, 'sb1': jnp.zeros((N_SHARED, 2 * FFN), dtype=jnp.float32), 'sw2': jax.random.normal(ks[3], (N_SHARED, FFN, D_MODEL), dtype=jnp.float32) * sc, 'sb2': jnp.zeros((N_SHARED, D_MODEL), dtype=jnp.float32), 'rw1': jax.random.normal(ks[4], (N_EXPERTS, D_MODEL, 2 * FFN), dtype=jnp.float32) * sc, 'rb1': jnp.zeros((N_EXPERTS, 2 * FFN), dtype=jnp.float32), 'rw2': jax.random.normal(ks[5], (N_EXPERTS, FFN, D_MODEL), dtype=jnp.float32) * sc, 'rb2': jnp.zeros((N_EXPERTS, D_MODEL), dtype=jnp.float32)}
    _L0_ffn_all = _L0_ffn_setup()
    _L0_ffn_in = {k: v for k, v in _L0_ffn_all.items() if k in ('gate_w', 'gate_b', 'sw1', 'sb1', 'sw2', 'sb2', 'rw1', 'rb1', 'rw2', 'rb2')}
    del _L0_ffn_all
    return {'x': x, 'ctx_1024': ctx_1024, 'L0_xattn_Wq': _L0_xattn_in['Wq'], 'L0_xattn_Wk': _L0_xattn_in['Wk'], 'L0_xattn_Wv': _L0_xattn_in['Wv'], 'L0_xattn_Wp': _L0_xattn_in['Wp'], 'L0_xattn_bp': _L0_xattn_in['bp'], 'L0_ffn_gate_w': _L0_ffn_in['gate_w'], 'L0_ffn_gate_b': _L0_ffn_in['gate_b'], 'L0_ffn_sw1': _L0_ffn_in['sw1'], 'L0_ffn_sb1': _L0_ffn_in['sb1'], 'L0_ffn_sw2': _L0_ffn_in['sw2'], 'L0_ffn_sb2': _L0_ffn_in['sb2'], 'L0_ffn_rw1': _L0_ffn_in['rw1'], 'L0_ffn_rb1': _L0_ffn_in['rb1'], 'L0_ffn_rw2': _L0_ffn_in['rw2'], 'L0_ffn_rb2': _L0_ffn_in['rb2']}

def reference(x, ctx_1024, L0_xattn_Wq, L0_xattn_Wk, L0_xattn_Wv, L0_xattn_Wp, L0_xattn_bp, L0_ffn_gate_w, L0_ffn_gate_b, L0_ffn_sw1, L0_ffn_sb1, L0_ffn_sw2, L0_ffn_sb2, L0_ffn_rw1, L0_ffn_rb1, L0_ffn_rw2, L0_ffn_rb2):
    import jax
    import jax.numpy as jnp

    def _L0_xattn_ref(m_q, m_kv, Wq, Wk, Wv, Wp, bp):
        import jax, jax.numpy as jnp
        import numpy as np
        DIM = 256
        NUM_HEADS = 8
        SCALE = (DIM // NUM_HEADS) ** (-0.5)
        B, N, C = m_q.shape
        q = m_q @ Wq
        k = m_kv @ Wk
        v = m_kv @ Wv
        attn = jnp.einsum('bnc,bmc->bnm', q, k) * SCALE
        attn = jax.nn.softmax(attn, axis=-1)
        x = jnp.einsum('bnm,bmc->bnc', attn, v)
        x = jnp.swapaxes(x, 1, 2).reshape(B, N, C)
        return x @ Wp + bp

    def _L0_ffn_ref(x, gate_w, gate_b, sw1, sb1, sw2, sb2, rw1, rb1, rw2, rb2):
        import jax, jax.numpy as jnp
        import numpy as np
        D_MODEL = 256
        FFN = 256
        N_EXPERTS = 8
        N_SHARED = 1
        TOP_K = 2
        B, S = (2, 512)

        def _swiglu(h):
            a, b = jnp.split(h, 2, axis=-1)
            return jax.nn.silu(a) * b
        hs = jnp.einsum('bsd,ndf->nbsf', x, sw1) + sb1[:, None, None, :]
        shared_out = jnp.einsum('nbsf,nfd->bsd', _swiglu(hs), sw2) + sb2.sum(0)
        probs = jax.nn.softmax(x @ gate_w + gate_b, axis=-1)
        topk_probs, topk_idx = jax.lax.top_k(probs, TOP_K)
        cw = jnp.sum(jax.nn.one_hot(topk_idx, N_EXPERTS, dtype=x.dtype) * topk_probs[..., None], axis=2)
        hr = jnp.einsum('bsd,edf->ebsf', x, rw1) + rb1[:, None, None, :]
        out_e = jnp.einsum('ebsf,efd->ebsd', _swiglu(hr), rw2) + rb2[:, None, None, :]
        routed_out = jnp.einsum('ebsd,bse->bsd', out_e, cw)
        return shared_out + routed_out
    x = x + _L0_xattn_ref(_layernorm(x, axis=-1), ctx_1024, L0_xattn_Wq, L0_xattn_Wk, L0_xattn_Wv, L0_xattn_Wp, L0_xattn_bp)
    x = x + _L0_ffn_ref(_layernorm(x, axis=-1), L0_ffn_gate_w, L0_ffn_gate_b, L0_ffn_sw1, L0_ffn_sb1, L0_ffn_sw2, L0_ffn_sb2, L0_ffn_rw1, L0_ffn_rb1, L0_ffn_rw2, L0_ffn_rb2)
    return x

_drawn_inputs = setup_inputs


def setup_inputs(seed=0):
    import zlib

    import numpy as np

    out = dict(_drawn_inputs(seed))
    spreads = {'L0_ffn_gate_b': (0.0, 0.725),
     'L0_ffn_sb1': (0.0, 0.8),
     'L0_ffn_sb2': (0.0, 0.535),
     'L0_ffn_rb1': (0.0, 0.8),
     'L0_ffn_rb2': (0.0, 0.399)}
    factors = {'L0_xattn_bp': 7.01,
     'L0_ffn_gate_w': 3.47,
     'L0_ffn_sw1': 4.035,
     'L0_ffn_sw2': 3.967,
     'L0_ffn_rw1': 8.0,
     'L0_ffn_rw2': 8.0}
    for name, (base, spread) in spreads.items():
        noise = np.random.default_rng([zlib.crc32(name.encode()), seed]).standard_normal(out[name].shape)
        drawn = base * np.exp(spread * noise) if base else spread * noise
        out[name] = jnp.asarray(drawn.astype(out[name].dtype))
    for name, factor in factors.items():
        out[name] = (out[name] * factor).astype(out[name].dtype)
    return out
```

```python
import concourse.bass as bass
from concourse import mybir
from contextlib import ExitStack


def cross_attention_moe_kernel(nc, x, ctx, wq, wk, wv, wp, bp, gate_w, gate_b,
                               sw1, sb1, sw2, sb2, rw1, rb1, rw2, rb2, out):
    f32, f32r, bf16 = mybir.dt.float32, mybir.dt.float32r, mybir.dt.bfloat16
    i32, u32 = mybir.dt.int32, mybir.dt.uint32
    ALU, ACT, AX = mybir.AluOpType, mybir.ActivationFunctionType, mybir.AxisListType.X

    P = 128
    B, N, C = x.shape
    E = gate_w.shape[1]
    F = rw2.shape[1]
    TOPK = 2
    KC = C // P
    KF = F // P
    PAIRS = B // 2
    EPS = 1e-5
    SCALE = float(C) ** -0.5 * 8 ** 0.5
    BR = 2 * P
    CAP = B * N + BR
    BLOCKS = TOPK * B * N // BR + E - 1
    SPARE = E - 1
    ROWS = E * CAP + SPARE * BR
    POOL_MADE, TABLE_LINKS = 20, 14
    assert N == P and F == C and C == 2 * P

    x_t = x.rearrange("b n c -> n b c")
    ctx_t = ctx.rearrange("b n c -> n b c")
    out_t = out.rearrange("b n c -> n b c")
    rw1_t = rw1.rearrange("e (k p) f -> p (e k) f", p=P)
    rw2_t = rw2.rearrange("e (k p) f -> p (e k) f", p=P)

    sorted_x = nc.dram_tensor("sorted_x", (ROWS, C), f32, kind="Internal").ap()
    block_y = nc.dram_tensor("block_y", (BLOCKS * BR, C), f32, kind="Internal").ap()

    with ExitStack() as stack:
        def sb(name, shape, dt):
            return stack.enter_context(nc.sbuf_tensor(name, shape, dt))

        def pb(name, shape, dt):
            return stack.enter_context(nc.psum_tensor(name, shape, dt))

        def sem(name):
            return stack.enter_context(nc.semaphore(name))

        ident = sb("ident", [P, P], f32)
        below = sb("below", [P, P], bf16)
        ones = sb("ones", [P, P], bf16)
        sel = sb("sel", [P, E + 3, P], bf16)
        bias = sb("bias", [P, 3 * C], bf16)
        minus_half = sb("minus_half", [P, 2], f32)
        eps = sb("eps", [P, 2], f32)
        expert_of = sb("expert_of", [P, E], f32)
        wqk = sb("wqk", [P, KC, C], f32)
        wv_s = sb("wv_s", [P, KC, C], f32)
        wp_s = sb("wp_s", [P, KC, C], f32)
        gw_s = sb("gw_s", [P, KC, E], f32)
        with ExitStack() as prologue:
            braw = prologue.enter_context(nc.sbuf_tensor("braw", [P, 3 * C], f32))
            brest = prologue.enter_context(nc.sbuf_tensor("brest", [P, 3 * C], f32))
            bpart = prologue.enter_context(nc.sbuf_tensor("bpart", [P, 3 * C], bf16))
        sw1h = sb("sw1h", [P, KC, 2 * F], f32r)
        sw1l = sb("sw1l", [P, KC, 2 * F], f32r)
        sw2h = sb("sw2h", [P, KF, C], f32r)
        sw2l = sb("sw2l", [P, KF, C], f32r)
        rw1h = sb("rw1h", [P, E * KC, 2 * F], f32r)
        rw1l = sb("rw1l", [P, E * KC, 2 * F], f32r)
        rw2h = sb("rw2h", [P, E * KF, C], f32r)
        rw2l = sb("rw2l", [P, E * KF, C], f32r)
        wstage = sb("wstage", [P, 2, 3 * C], f32)

        xs = sb("xs", [P, B, C], f32)
        keep = sb("keep", [P, PAIRS, 8], f32)
        slots = sb("slots", [P, PAIRS, 2 * TOPK], f32)
        y_rows = sb("y_rows", [P, PAIRS, 2 * TOPK], i32)
        counts = sb("counts", [P, E], f32)
        zeros = sb("zeros", [P, C], f32)
        block_expert = sb("block_expert", [1, BLOCKS], i32)
        block_row = sb("block_row", [1, BLOCKS], i32)
        pad_row = sb("pad_row", [1, E], i32)

        iota_e = sb("iota_e", [P, E], i32)
        iota_blocks = sb("iota_blocks", [1, BLOCKS], i32)

        with ExitStack() as phase_a:
            def sa(name, shape, dt):
                return phase_a.enter_context(nc.sbuf_tensor(name, shape, dt))

            cx = sa("cx", [P, 2, 2, C], f32)
            xn = sa("xn", [P, 2, 2, C], f32)
            xnT = sa("xnT", [P, 2, KC, 2 * P], f32)
            cT = sa("cT", [P, 2, KC, 2 * P], f32)
            tT = sa("tT", [P, 2, KC, 2 * P], f32)
            v = sa("v", [P, 2, 2, C], f32)
            prob = sa("prob", [P, 2, 2, P], f32)
            pT = sa("pT", [P, 2, 2 * P], f32)
            y = sa("y", [P, 2, 2, C], f32)
            xn2 = sa("xn2", [P, 2, 2, C], f32)
            xn2T = sa("xn2T", [P, 2, KC, 2 * P], f32)
            bn = sa("bn", [P, 2, 2, 6], f32)
            mv = sa("mv", [P, 2, 2, 2], f32)
            var = sa("var", [P, 2, 2], f32)
            bn2 = sa("bn2", [P, 2, 2, 6], f32)
            mv2 = sa("mv2", [P, 2, 2, 2], f32)
            var2 = sa("var2", [P, 2, 2], f32)
            nmax = sa("nmax", [P, 2, 2], f32)
            esum = sa("esum", [P, 2, 2], f32)
            rinv = sa("rinv", [P, 2, 2], f32)
            gmax = sa("gmax", [P, 2], f32)
            glog = sa("glog", [P, 2, E], f32)
            gexp = sa("gexp", [P, 2, E], f32)
            gsum = sa("gsum", [P, 2], f32)
            ginv = sa("ginv", [P, 2], f32)
            gprob = sa("gprob", [P, 2, E], f32)
            top8 = sa("top8", [P, 2, 8], f32)
            topi = sa("topi", [P, 2, 8], u32)
            topf = sa("topf", [P, 2, 8], f32)
            hot = sa("hot", [P, 2, TOPK, E], f32)
            both = sa("both", [P, 2, E], bf16)
            place = sa("place", [P, 2, E], f32)
            hotplace = sa("hotplace", [P, 2, TOPK, E], f32)
            slotf = sa("slotf", [P, 2 * TOPK], f32)
            slot_ring = sa("slot_ring", [P, 2, 2 * TOPK], i32)
            t_base = sa("t_base", [P, E], f32)
            t_zero = sa("t_zero", [P, E], f32)
            t_n = sa("t_n", [P, E], f32)
            t_ni = sa("t_ni", [P, E], i32)
            t_nr = sa("t_nr", [P, E], i32)
            t_nb = sa("t_nb", [P, E], f32)
            t_cum = sa("t_cum", [P, E], f32)
            t_start = sa("t_start", [P, E], f32)
            t_delta = sa("t_delta", [P, E], f32)
            t_step = sa("t_step", [P, E], f32)
            t_past = sa("t_past", [P, PAIRS * 2 * TOPK, E - 1], f32)
            t_moved = sa("t_moved", [P, PAIRS * 2 * TOPK], f32)
            t_j = sa("t_j", [1, BLOCKS], f32)
            t_ge = sa("t_ge", [1, BLOCKS, E], f32)
            t_e = sa("t_e", [1, BLOCKS], f32)
            t_before = sa("t_before", [1, BLOCKS], f32)
            t_in = sa("t_in", [1, BLOCKS], f32)
            t_in2 = sa("t_in2", [1, BLOCKS], f32)
            t_row = sa("t_row", [1, BLOCKS], f32)

        xg = sb("xg", [P, 2, 2, C], f32)
        xgh, xgl = sb("xgh", [P, 2, KC, BR], f32r), sb("xgl", [P, 2, KC, BR], f32r)
        assert F == C and KF == KC == 2
        th, gate_a, hid = sb("th", [P, 2, F], f32), sb("gate_a", [P, 2, F], f32), sb("hid", [P, 2, F], f32)
        hidh, hidl = sb("hidh", [P, 2, KF, BR], f32r), sb("hidl", [P, 2, KF, BR], f32r)
        yb = sb("yb", [P, 2, 2, C], f32)
        ckeep, cw = sb("ckeep", [P, 2, 8], f32), sb("cw", [P, 2, 2 * TOPK], f32)
        cxn, cxh, cxl = xg, xgh, xgl
        cth, cgate, chid = th, gate_a, hid
        chidh, chidl = hidh[:, 0], hidl[:, 0]
        cslot = sb("cslot", [P, 2, 2 * TOPK], i32)
        yg = sb("yg", [P, 2, 2 * TOPK, C], f32)
        acc = sb("acc", [P, 2, 2, C], f32)

        banks = [stack.enter_context(nc.psum_tensor(f"bank{i}", [P, 512], f32)) for i in range(8)]
        B_XT, B_CT, B_TT, B_V, B_S, B_Y, B_Z, B_R = banks
        B_ROWS, B_H, B_HT, B_YB = banks[0:2], (banks[2:4], banks[4:6]), banks[6], banks[7]
        C_XT, C_A, C_B, C_Y = banks[0], banks[2:4], banks[4:6], banks[6]

        def flat(t):
            return t.rearrange("p a b -> p (a b)")

        names = """attn_w_loaded small_loaded bias_loaded shared_loaded braw_zeroed pool_made bias_split
            prep_ps prep_sb w_hi w_lo shared_hi shared_lo
            bn_done mv_done var_done rstd_done xn_done xnT_ps cT_ps xnT_sb cT_sb tT_ps v_ps tT_sb v_sb
            s_ps max_done exp_done rinv_done pT_ps pT_sb y_ps y_sb z_ps x2_done bn2_done mv2_done var2_done
            rstd2_done xn2_done stats_kept xn2T_ps xn2T_sb gate_ps gmax_done glog_done gexp_done route_link
            hot_done place_ps counted place_link slots_done table_link table_done padded spare_zeroed
            rowsT_ps rows_hi rows_lo h_ps tanh_done gated hid_done hidT_ps hid_hi hid_lo yb_ps yb_sb
            c_slot c_kept c_xn c_T_ps c_hi c_lo c_h_ps c_tanh c_gated c_hid c_hid_hi c_hid_lo c_y_ps c_base
            c_added c_out waited move_link""".split()
        S = {name: stack.enter_context(nc.semaphore(name)) for name in names}

        def by_parity(name, n=2):
            return [stack.enter_context(nc.semaphore(f"{name}{i}")) for i in range(n)]

        x_loaded, ctx_loaded, wstage_loaded = by_parity("x_loaded"), by_parity("ctx_loaded"), by_parity("wstage_loaded")
        scattered, y_stored = by_parity("scattered"), by_parity("y_stored")
        rows_loaded = by_parity("rows_loaded")
        y_gathered, out_stored = by_parity("y_gathered"), by_parity("out_stored")

        def wait(eng, semaphore, count):
            if not isinstance(count, int) or count > 0:
                eng.wait_ge(semaphore, count)

        def wait_apart(eng, semaphore, count):
            wait(eng, semaphore, count)
            if not isinstance(count, int):
                eng.sem_inc(S["waited"], 1)

        class At:

            def __init__(self, offset, r=None, unroll=2):
                self.offset, self.r, self.unroll = offset, r, unroll

            def __add__(self, n):
                return At(self.offset + n, self.r, self.unroll)

            def __sub__(self, n):
                return self + (-n)

            def of(self, total):
                return self.r is not None or 0 <= self.offset < total

            def mod(self, n):
                return self.offset % n

            def div(self, n):
                return self.offset // n + (0 if self.r is None else self.r * (self.unroll // n))

            @property
            def v(self):
                return self.offset if self.r is None else self.unroll * self.r + self.offset

        def run_steps(eng, step, first, peel, total, last, unroll):
            loops = (total - peel) // unroll
            for s in range(first, peel):
                step(At(s))
            with eng.Fori(0, loops) as r:
                for u in range(unroll):
                    step(At(peel + u, r, unroll))
            for s in range(peel + loops * unroll, last + 1):
                step(At(s))

        def steps_a(eng, step):
            run_steps(eng, step, -2, 4, PAIRS - 2, PAIRS + 2, 2)

        def steps_b(eng, step):
            run_steps(eng, step, -1, 4, BLOCKS - 2, BLOCKS + 1, 2)

        def steps_c(eng, step):
            run_steps(eng, step, -2, 2, PAIRS - 2, PAIRS, 2)

        class Links:

            def __init__(self, eng, semaphore, per, q):
                self.eng, self.semaphore, self.left = eng, semaphore, per
                self.count = per * q

            def __call__(self, ins):
                self.count, self.left = self.count + 1, self.left - 1
                assert self.left >= 0
                ins.then_inc(self.semaphore, 1)
                wait_apart(self.eng, self.semaphore, self.count)

        def two(t, q):
            return t[:, bass.ds(2 * q.v, 2), :]

        def row_of(t, index):
            return t[:, bass.ds(index, 1), :].rearrange("p a f -> p (a f)")

        def in_halves(rows):
            return rows.rearrange("(p a) c -> p a c", a=2)

        zeros_block = zeros[:].unsqueeze(1).broadcast_to((P, 2, C))

        block = stack.enter_context(nc.Block())

        @block.sync
        def _(sp):
            for w, i in ((wq, 0), (wk, 1)):
                sp.dma_start(wstage[:, i, 0:KC * C].rearrange("p (k c) -> p k c", k=KC),
                             w.rearrange("(k p) c -> p k c", p=P)).then_inc(S["attn_w_loaded"], 16)
            for q in range(2):
                sp.dma_start(xs[:, 2 * q:2 * q + 2, :], x_t[:, 2 * q:2 * q + 2, :]).then_inc(x_loaded[q], 16)
                sp.dma_start(cx[:, q], ctx_t[:, 2 * q:2 * q + 2, :]).then_inc(ctx_loaded[q], 16)
            for dst, w in ((wv_s, wv), (wp_s, wp), (gw_s, gate_w)):
                sp.dma_start(dst[:], w.rearrange("(k p) c -> p k c", p=P)).then_inc(S["small_loaded"], 16)
            sp.wait_ge(S["braw_zeroed"], 1)
            for part in range(3):
                r0 = 32 * part
                for dst, b_dram in ((braw[r0:r0 + E, 0:2 * F], rb1), (braw[r0:r0 + E, 2 * F:2 * F + C], rb2),
                                    (braw[r0 + E:r0 + E + 1, 0:2 * F], sb1),
                                    (braw[r0 + E:r0 + E + 1, 2 * F:2 * F + C], sb2),
                                    (braw[r0 + E + 1:r0 + E + 2, 0:C], bp.rearrange("(a c) -> a c", a=1)),
                                    (braw[r0 + E + 2:r0 + E + 3, 0:E], gate_b.rearrange("(a c) -> a c", a=1))):
                    sp.dma_start(dst, b_dram).then_inc(S["bias_loaded"], 16)
            sp.wait_ge(S["pool_made"], POOL_MADE)
            for n in range(SPARE):
                sp.dma_start(in_halves(sorted_x[E * CAP + n * BR:E * CAP + (n + 1) * BR, :]), zeros_block)\
                    .then_inc(S["spare_zeroed"], 16)

            def step(s):
                if s.of(PAIRS - 2):
                    q = s + 2
                    wait(sp, S["cT_ps"], s.v + 1)
                    sp.dma_start(two(xs, q), x_t[:, bass.ds(2 * q.v, 2), :]).then_inc(x_loaded[q.mod(2)], 16)
                    sp.dma_start(cx[:, q.mod(2)], ctx_t[:, bass.ds(2 * q.v, 2), :])\
                        .then_inc(ctx_loaded[q.mod(2)], 16)
                if s.of(E * KC):
                    wait(sp, S["prep_ps"], 2)
                    wait(sp, S["w_lo"], s.v - 1)
                    for c0, c1, w in ((0, 2 * F, rw1_t), (2 * F, 2 * F + C, rw2_t)):
                        sp.dma_start(wstage[:, s.mod(2), c0:c1], row_of(w, s.v)).then_inc(wstage_loaded[s.mod(2)], 16)

            steps_a(sp, step)

            sp.wait_ge(S["w_lo"], E * KC)
            for k in range(KC):
                for c0, c1, w in ((0, 2 * F, sw1), (2 * F, 2 * F + C, sw2)):
                    sp.dma_start(wstage[:, k, c0:c1], w[0, k * P:(k + 1) * P, :]).then_inc(S["shared_loaded"], 16)

            sp.wait_ge(S["table_done"], 1)
            for e in range(E):
                row = sp.value_load(pad_row[0:1, e:e + 1], min_val=0, max_val=E * CAP - BR)
                sp.dma_start(in_halves(sorted_x[bass.ds(row, BR), :]), zeros_block).then_inc(S["padded"], 16)
            sp.wait_ge(S["padded"], 16 * E)
            sp.wait_ge(S["spare_zeroed"], 16 * SPARE)
            for i in range(2):
                sp.wait_ge(scattered[i], 16 * TOPK * B // 2)

            def rows_at(j):
                return bass.ds(sp.value_load(block_row[0:1, bass.ds(j.v, 1)], min_val=0, max_val=ROWS - BR), BR)

            def step(s):
                if (s + 2).of(BLOCKS):
                    j = s + 2
                    wait(sp, S["rowsT_ps"], j.v - 1)
                    sp.dma_start(xg[:, j.mod(2)], in_halves(sorted_x[rows_at(j), :]))\
                        .then_inc(rows_loaded[j.mod(2)], 16)
                if (s - 2).of(BLOCKS):
                    j = s - 2
                    sp.wait_ge(S["yb_sb"], j.v + 1)
                    sp.dma_start(in_halves(block_y[bass.ds(j.v * BR, BR), :]), yb[:, j.mod(2)])\
                        .then_inc(y_stored[j.mod(2)], 16)

            step(At(-2))
            steps_b(sp, step)

            def step(s):
                if (s - 1).of(PAIRS):
                    q = s - 1
                    sp.wait_ge(S["c_out"], q.v + 1)
                    sp.dma_start(out_t[:, bass.ds(2 * q.v, 2), :], acc[:, q.mod(2)]).then_inc(out_stored[q.mod(2)], 16)

            steps_c(sp, step)
            for i in range(2):
                sp.wait_ge(out_stored[i], 16 * PAIRS // 2)

        @block.gpsimd
        def _(pool):
            nc.gpsimd.memset(braw[:], 0.0).then_inc(S["braw_zeroed"], 1)
            made = Links(pool, S["pool_made"], POOL_MADE, 0)
            made(nc.gpsimd.memset(minus_half[:], -0.5))
            made(nc.gpsimd.memset(eps[:], EPS))
            made(nc.gpsimd.memset(ident[:], 0.0))
            made(nc.gpsimd.affine_select(out=ident[:], in_=ident[:], compare_op=ALU.not_equal, fill=1.0,
                                         base=0, pattern=[[-1, P]], channel_multiplier=1))
            made(nc.gpsimd.memset(zeros[:], 0.0))
            made(nc.gpsimd.memset(bias[:], 0.0))
            made(nc.gpsimd.memset(sel[:], 0.0))
            for part in range(3):
                made(nc.gpsimd.affine_select(out=sel[:], in_=sel[:], compare_op=ALU.not_equal, fill=1.0,
                                             base=-32 * part, pattern=[[-1, E + 3], [0, P]], channel_multiplier=1))
            made(nc.gpsimd.memset(ones[:], 1.0))
            made(nc.gpsimd.affine_select(out=below[:], in_=ones[:], compare_op=ALU.is_gt, fill=0.0,
                                         base=0, pattern=[[1, P]], channel_multiplier=-1))
            made(nc.gpsimd.iota(iota_e[:], [[1, E]], base=0, channel_multiplier=0))
            made(nc.gpsimd.tensor_copy(expert_of[:], iota_e[:]))
            made(nc.gpsimd.iota(iota_e[:], [[CAP, E]], base=0, channel_multiplier=0))
            made(nc.gpsimd.tensor_copy(counts[:], iota_e[:]))
            made(nc.gpsimd.tensor_copy(t_base[:], iota_e[:]))
            made(nc.gpsimd.iota(iota_blocks[:], [[1, BLOCKS]], base=0, channel_multiplier=0))
            made(nc.gpsimd.tensor_copy(t_j[:], iota_blocks[:]))
            made(nc.gpsimd.memset(t_zero[:], 0.0))
            assert made.left == 0

            def inverse_deviation(moments, room, moments_done, room_done, done, q):
                b = q.mod(2)
                pool.wait_ge(moments_done, q.v + 1)
                nc.gpsimd.tensor_tensor(room[:, b], moments[:, b, :, 1], eps[:], ALU.add).then_inc(room_done, 1)
                pool.wait_ge(room_done, q.v + 1)
                nc.gpsimd.tensor_tensor(moments[:, b, :, 1], room[:, b], minus_half[:], ALU.pow).then_inc(done, 1)

            def step(s):
                if (s + 2).of(PAIRS):
                    inverse_deviation(mv, var, S["mv_done"], S["var_done"], S["rstd_done"], s + 2)
                if (s - 3).of(PAIRS):
                    q = s - 3
                    wait_apart(pool, S["slots_done"], q.v + 1)
                    for n in range(2 * TOPK):
                        nc.gpsimd.indirect_dma_start(
                            out=sorted_x, out_offset=bass.IndirectOffsetOnAxis(
                                ap=slot_ring[:, q.mod(2), n:n + 1], axis=0),
                            in_=xn2[:, q.mod(2), n // TOPK, :], in_offset=None).then_inc(scattered[q.mod(2)], 16)
                if s.of(E * KC):
                    b = s.mod(2)
                    pool.wait_ge(S["w_hi"], s.v + 1)
                    nc.gpsimd.tensor_tensor(row_of(rw1l, s.v), wstage[:, b, 0:2 * F], row_of(rw1h, s.v), ALU.subtract)
                    nc.gpsimd.tensor_tensor(row_of(rw2l, s.v), wstage[:, b, 2 * F:2 * F + C], row_of(rw2h, s.v),
                                            ALU.subtract).then_inc(S["w_lo"], 1)
                if (s - 1).of(PAIRS):
                    inverse_deviation(mv2, var2, S["mv2_done"], S["var2_done"], S["rstd2_done"], s - 1)

            steps_a(pool, step)

            pool.wait_ge(S["shared_hi"], 1)
            for k in range(KC):
                nc.gpsimd.tensor_tensor(sw1l[:, k, :], wstage[:, k, 0:2 * F], sw1h[:, k, :], ALU.subtract)
                last = nc.gpsimd.tensor_tensor(sw2l[:, k, :], wstage[:, k, 2 * F:2 * F + C], sw2h[:, k, :],
                                               ALU.subtract)
            last.then_inc(S["shared_lo"], 1)

            pool.wait_ge(S["move_link"], 7)
            for i in range(2):
                pool.wait_ge(y_stored[i], 16 * ((BLOCKS + 1 - i) // 2))

            def step(s):
                if (s + 2).of(PAIRS):
                    q = s + 2
                    wait(pool, S["c_out"], q.v - 1)
                    nc.gpsimd.tensor_copy(cslot[:, q.mod(2)], row_of(y_rows, q.v)).then_inc(S["c_slot"], 1)
                    wait_apart(pool, S["c_slot"], q.v + 1)
                    for n in range(2 * TOPK):
                        nc.gpsimd.indirect_dma_start(
                            out=yg[:, q.mod(2), n, :], out_offset=None, in_=block_y,
                            in_offset=bass.IndirectOffsetOnAxis(ap=cslot[:, q.mod(2), n:n + 1], axis=0))\
                            .then_inc(y_gathered[q.mod(2)], 16)

            steps_c(pool, step)

        @block.scalar
        def _(act):
            nc.scalar.preload_act_table(ACT.Exp)

            def copy(dst, src, **kw):
                return nc.scalar.activation(dst, src, ACT.Copy, **kw)

            act.wait_ge(S["prep_ps"], 1)
            copy(flat(xnT[:, 0]), B_XT[:]).then_inc(S["prep_sb"], 1)
            act.wait_ge(S["prep_ps"], 2)
            copy(flat(cT[:, 0]), B_CT[:]).then_inc(S["prep_sb"], 1)
            act.wait_ge(S["prep_ps"], 3)
            copy(flat(wqk[:]), B_TT[:], scale=SCALE).then_inc(S["prep_sb"], 1)

            def step(s):
                b = s.mod(2)
                if s.of(PAIRS):
                    act.wait_ge(S["tT_ps"], s.v + 1)
                    wait(act, S["s_ps"], s.v - 1)
                    copy(flat(tT[:, b]), B_TT[:]).then_inc(S["tT_sb"], 1)
                if (s - 2).of(PAIRS):
                    q = s - 2
                    act.wait_ge(S["xn2T_ps"], q.v + 1)
                    wait(act, S["gate_ps"], q.v - 1)
                    copy(flat(xn2T[:, q.mod(2)]), B_XT[:]).then_inc(S["xn2T_sb"], 1)
                if s.of(PAIRS):
                    act.wait_ge(S["v_ps"], s.v + 1)
                    wait(act, S["y_ps"], s.v - 1)
                    copy(flat(v[:, b]), B_V[:]).then_inc(S["v_sb"], 1)
                if s.of(E * KC):
                    act.wait_ge(wstage_loaded[b], (s.div(2) + 1) * 32)
                    copy(row_of(rw1h, s.v), wstage[:, b, 0:2 * F])
                    copy(row_of(rw2h, s.v), wstage[:, b, 2 * F:2 * F + C]).then_inc(S["w_hi"], 1)
                if (s - 2).of(PAIRS):
                    q = s - 2
                    act.wait_ge(S["glog_done"], q.v + 1)
                    nc.scalar.activation(gexp[:], glog[:], ACT.Exp).then_inc(S["gexp_done"], 1)
                if s.of(PAIRS):
                    act.wait_ge(S["max_done"], s.v + 1)
                    wait(act, S["pT_ps"], s.v - 1)
                    for t in range(2):
                        last = nc.scalar.activation(prob[:, b, t, :], B_S[:, t * P:(t + 1) * P], ACT.Exp,
                                                    bias=nmax[:, b, t:t + 1], accum_out=esum[:, b, t:t + 1])
                    last.then_inc(S["exp_done"], 1)
                if (s + 1).of(PAIRS):
                    q = s + 1
                    act.wait_ge(S["xnT_ps"], q.v + 1)
                    wait(act, S["tT_ps"], q.v - 1)
                    copy(flat(xnT[:, q.mod(2)]), B_XT[:]).then_inc(S["xnT_sb"], 1)
                if s.of(PAIRS):
                    act.wait_ge(S["y_ps"], s.v + 1)
                    act.wait_ge(S["rinv_done"], s.v + 1)
                    wait(act, S["z_ps"], s.v - 1)
                    for t in range(2):
                        last = copy(y[:, b, t, :], B_Y[:, t * C:(t + 1) * C], scale=rinv[:, b, t:t + 1])
                    last.then_inc(S["y_sb"], 1)

            steps_a(act, step)

            act.wait_ge(S["shared_loaded"], 16 * 2 * KC)
            for k in range(KC):
                copy(sw1h[:, k, :], wstage[:, k, 0:2 * F])
                last = copy(sw2h[:, k, :], wstage[:, k, 2 * F:2 * F + C])
            last.then_inc(S["shared_hi"], 1)

            def step(s):
                if (s + 1).of(BLOCKS):
                    j = s + 1
                    act.wait_ge(S["rowsT_ps"], j.v + 1)
                    wait(act, S["h_ps"], (j.v - 1) * 2)
                    copy(flat(xgh[:, j.mod(2)]), B_ROWS[j.mod(2)][:]).then_inc(S["rows_hi"], 1)
                if s.of(BLOCKS):
                    for a in range(2):
                        act.wait_ge(S["h_ps"], s.v * 2 + a + 1)
                        if a == 0:
                            wait(act, S["gated"], s.v * 2)
                        nc.scalar.activation(th[:, a], B_H[s.mod(2)][a][:, 0:F], ACT.Tanh, scale=0.5)\
                            .then_inc(S["tanh_done"], 1)
                if (s - 1).of(BLOCKS):
                    j = s - 1
                    act.wait_ge(S["hidT_ps"], j.v + 1)
                    wait(act, S["yb_ps"], j.v - 1)
                    copy(flat(hidh[:, j.mod(2)]), B_HT[:]).then_inc(S["hid_hi"], 1)
                if (s - 2).of(BLOCKS):
                    j = s - 2
                    act.wait_ge(S["yb_ps"], j.v + 1)
                    wait(act, y_stored[j.mod(2)], j.div(2) * 16)
                    copy(flat(yb[:, j.mod(2)]), B_YB[:]).then_inc(S["yb_sb"], 1)

            steps_b(act, step)

            def step(s):
                if (s + 1).of(PAIRS):
                    q = s + 1
                    act.wait_ge(S["c_T_ps"], q.v + 1)
                    wait(act, S["c_h_ps"], q.v - 1)
                    copy(flat(cxh[:, q.mod(2)]), C_XT[:]).then_inc(S["c_hi"], 1)
                if s.of(PAIRS):
                    act.wait_ge(S["c_h_ps"], s.v + 1)
                    wait(act, S["c_gated"], s.v)
                    nc.scalar.activation(flat(cth[:]), C_A[s.mod(2)][:], ACT.Tanh, scale=0.5).then_inc(S["c_tanh"], 1)
                    act.wait_ge(S["c_hid"], s.v + 1)
                    wait(act, S["c_y_ps"], s.v)
                    copy(chidh[:], chid[:]).then_inc(S["c_hid_hi"], 1)

            steps_c(act, step)

        @block.vector
        def _(dve):
            def moments(src, stats6, out, stats_done, done, q):
                b = q.mod(2)
                for t in range(2):
                    last = nc.vector.bn_stats(stats6[:, b, t, :], row_of(src, q.v * 2 + t))
                last.then_inc(stats_done, 1)
                wait_apart(dve, stats_done, q.v + 1)
                for t in range(2):
                    last = nc.vector.bn_aggr(out[:, b, t, :], stats6[:, b, t, :])
                last.then_inc(done, 1)

            def normalise(dst, mom, q):
                b = q.mod(2)
                for t in range(2):
                    last = nc.vector.tensor_scalar(dst[:, b, t, :], row_of(xs, q.v * 2 + t), mom[:, t, 0:1],
                                                   mom[:, t, 1:2], ALU.subtract, ALU.mult)
                return last

            def split_bias():
                dve.wait_ge(S["bias_loaded"], 16 * 18)
                dve.wait_ge(S["pool_made"], POOL_MADE)
                link = Links(dve, S["bias_split"], 7, 0)
                link(nc.vector.tensor_copy(bias[0:E + 3, :], braw[0:E + 3, :]))
                link(nc.vector.tensor_copy(bpart[:], braw[:]))
                link(nc.vector.tensor_tensor(brest[:], braw[:], bpart[:], ALU.subtract))
                link(nc.vector.tensor_copy(bias[32:32 + E + 3, :], brest[32:32 + E + 3, :]))
                link(nc.vector.tensor_copy(bpart[:], brest[:]))
                link(nc.vector.tensor_tensor(braw[:], brest[:], bpart[:], ALU.subtract))
                link(nc.vector.tensor_copy(bias[64:64 + E + 3, :], braw[64:64 + E + 3, :]))

            def step(s):
                b = s.mod(2)
                if (s - 2).of(PAIRS):
                    q = s - 2
                    dve.wait_ge(S["rstd2_done"], q.v + 1)
                    if (q - 2).of(PAIRS):
                        dve.wait_ge(scattered[q.mod(2)], (q - 2).div(2) * (32 * TOPK) + 32 * TOPK)
                    normalise(xn2, mv2[:, q.mod(2)], q).then_inc(S["xn2_done"], 1)
                    nc.vector.tensor_copy(row_of(keep, q.v)[:, 0:4], mv2[:, q.mod(2)].rearrange("p a b -> p (a b)"))\
                        .then_inc(S["stats_kept"], 1)
                if (s - 3).of(PAIRS):
                    q = s - 3
                    dve.wait_ge(S["place_ps"], q.v + 1)
                    link = Links(dve, S["place_link"], 5, q.v)
                    nc.vector.tensor_tensor(place[:], B_R[:, 64:64 + 2 * E].rearrange("p (t e) -> p t e", t=2),
                                            counts[:].unsqueeze(1).broadcast_to((P, 2, E)), ALU.add)\
                        .then_inc(S["counted"], 1)
                    dve.wait_ge(S["counted"], q.v + 1)
                    link(nc.vector.tensor_tensor(counts[:], B_R[:, 64 + 2 * E:64 + 3 * E], counts[:], ALU.add))
                    link(nc.vector.tensor_tensor(hotplace[:], hot[:],
                                                 place[:].unsqueeze(2).broadcast_to((P, 2, TOPK, E)), ALU.mult))
                    link(nc.vector.tensor_reduce(slotf[:], hotplace[:].rearrange("p t k e -> p (t k) e"),
                                                 AX, ALU.add))
                    if (q - 2).of(PAIRS):
                        dve.wait_ge(scattered[q.mod(2)], (q - 2).div(2) * (32 * TOPK) + 32 * TOPK)
                    link(nc.vector.tensor_copy(row_of(slots, q.v), slotf[:]))
                    link(nc.vector.tensor_copy(slot_ring[:, q.mod(2)], slotf[:]))
                    nc.vector.tensor_copy(row_of(keep, q.v)[:, 4:8].rearrange("p (t k) -> p t k", t=2),
                                          top8[:, :, 0:TOPK]).then_inc(S["slots_done"], 1)
                if (s + 2).of(PAIRS):
                    q = s + 2
                    dve.wait_ge(x_loaded[q.mod(2)], q.div(2) * 16 + 16)
                    wait_apart(dve, S["xn_done"], q.v - 1)
                    moments(xs, bn, mv, S["bn_done"], S["mv_done"], q)
                if (s - 2).of(PAIRS):
                    q = s - 2
                    dve.wait_ge(S["gate_ps"], q.v + 1)
                    logits = B_R[:, 0:2 * E].rearrange("p (t e) -> p t e", t=2)
                    nc.vector.tensor_reduce(gmax[:], logits, AX, ALU.max).then_inc(S["gmax_done"], 1)
                    dve.wait_ge(S["gmax_done"], q.v + 1)
                    wait(dve, S["gexp_done"], q.v)
                    nc.vector.tensor_tensor(glog[:], logits, gmax[:].unsqueeze(2).broadcast_to((P, 2, E)),
                                            ALU.subtract).then_inc(S["glog_done"], 1)
                if (s + 2).of(PAIRS):
                    q = s + 2
                    dve.wait_ge(S["rstd_done"], q.v + 1)
                    wait(dve, S["xnT_ps"], q.v - 1)
                    normalise(xn, mv[:, q.mod(2)], q).then_inc(S["xn_done"], 1)
                if s.of(PAIRS):
                    dve.wait_ge(S["s_ps"], s.v + 1)
                    nc.vector.tensor_reduce(nmax[:, b, :], B_S[:, 0:2 * P].rearrange("p (t m) -> p t m", t=2),
                                            AX, ALU.max, negate=True).then_inc(S["max_done"], 1)
                if (s - 2).of(PAIRS):
                    q = s - 2
                    dve.wait_ge(S["gexp_done"], q.v + 1)
                    link = Links(dve, S["route_link"], 7, q.v)
                    link(nc.vector.tensor_reduce(gsum[:], gexp[:], AX, ALU.add))
                    link(nc.vector.reciprocal(ginv[:], gsum[:]))
                    link(nc.vector.tensor_tensor(gprob[:], gexp[:], ginv[:].unsqueeze(2).broadcast_to((P, 2, E)),
                                                 ALU.mult))
                    nc.vector.max(top8[:, 0, :], gprob[:, 0, :])
                    link(nc.vector.max(top8[:, 1, :], gprob[:, 1, :]))
                    nc.vector.max_index(topi[:, 0, :], top8[:, 0, :], gprob[:, 0, :])
                    link(nc.vector.max_index(topi[:, 1, :], top8[:, 1, :], gprob[:, 1, :]))
                    link(nc.vector.tensor_copy(topf[:], topi[:]))
                    link(nc.vector.tensor_tensor(
                        hot[:], expert_of[:].unsqueeze(1).unsqueeze(1).broadcast_to((P, 2, TOPK, E)),
                        topf[:, :, 0:TOPK].unsqueeze(3).broadcast_to((P, 2, TOPK, E)), ALU.is_equal))
                    nc.vector.tensor_tensor(both[:], hot[:, :, 0, :], hot[:, :, 1, :], ALU.add)\
                        .then_inc(S["hot_done"], 1)
                if s.of(PAIRS):
                    dve.wait_ge(S["exp_done"], s.v + 1)
                    wait(dve, S["y_sb"], s.v - 1)
                    nc.vector.reciprocal(rinv[:, b, :], esum[:, b, :]).then_inc(S["rinv_done"], 1)
                if (s - 1).of(PAIRS):
                    q = s - 1
                    dve.wait_ge(S["z_ps"], q.v + 1)
                    nc.vector.tensor_tensor(two(xs, q), B_Z[:].rearrange("p (t c) -> p t c", t=2), two(xs, q),
                                            ALU.add).then_inc(S["x2_done"], 1)
                    dve.wait_ge(S["x2_done"], q.v + 1)
                    wait_apart(dve, S["stats_kept"], q.v - 1)
                    moments(xs, bn2, mv2, S["bn2_done"], S["mv2_done"], q)
                if s.of(PAIRS):
                    dve.wait_ge(S["pT_ps"], s.v + 1)
                    wait(dve, S["y_ps"], s.v - 1)
                    nc.vector.tensor_copy(pT[:, b], B_S[:, 2 * P:4 * P]).then_inc(S["pT_sb"], 1)
                if (s + 1).of(PAIRS):
                    q = s + 1
                    dve.wait_ge(S["cT_ps"], q.v + 1)
                    wait(dve, S["s_ps"], q.v - 1)
                    nc.vector.tensor_copy(flat(cT[:, q.mod(2)]), B_CT[:]).then_inc(S["cT_sb"], 1)
                if s.r is None and s.offset == -1:
                    split_bias()

            steps_a(dve, step)

            dve.wait_ge(S["place_link"], 5 * PAIRS)
            link = Links(dve, S["table_link"], TABLE_LINKS, 0)
            link(nc.vector.tensor_tensor(t_n[:], counts[:], t_base[:], ALU.subtract))
            link(nc.vector.tensor_copy(pad_row[:], counts[0:1, :]))
            link(nc.vector.tensor_scalar(t_ni[:], t_n[:], float(BR - 1), None, ALU.add))
            link(nc.vector.tensor_scalar(t_nr[:], t_ni[:], BR.bit_length() - 1, None, ALU.arith_shift_right))
            link(nc.vector.tensor_copy(t_nb[:], t_nr[:]))
            link(nc.vector.tensor_tensor_scan(t_cum[:], t_nb[:], t_zero[:], 0.0, ALU.add, ALU.add))
            over = (1, BLOCKS, E)
            link(nc.vector.tensor_tensor(t_ge[:], t_cum[0:1, :].unsqueeze(1).broadcast_to(over),
                                         t_j[:].unsqueeze(2).broadcast_to(over), ALU.is_le))
            link(nc.vector.tensor_reduce(t_e[:], t_ge[:], AX, ALU.add))
            link(nc.vector.tensor_tensor(t_ge[:], t_ge[:], t_nb[0:1, :].unsqueeze(1).broadcast_to(over), ALU.mult))
            link(nc.vector.tensor_reduce(t_before[:], t_ge[:], AX, ALU.add))
            link(nc.vector.tensor_tensor(t_in[:], t_j[:], t_before[:], ALU.subtract))
            link(nc.vector.tensor_scalar(t_in2[:], t_in[:], float(BR), None, ALU.mult))
            link(nc.vector.scalar_tensor_tensor(t_row[:], t_e[:], float(CAP), t_in2[:], ALU.mult, ALU.add))
            link(nc.vector.tensor_scalar(block_expert[:], t_e[:], float(E - 1), None, ALU.min))
            assert link.left == 0
            nc.vector.tensor_copy(block_row[:], t_row[:]).then_inc(S["table_done"], 1)
            link = Links(dve, S["move_link"], 7, 0)
            link(nc.vector.tensor_tensor(t_start[:], t_cum[:], t_nb[:], ALU.subtract))
            link(nc.vector.scalar_tensor_tensor(t_delta[:], t_start[:], float(BR), t_base[:], ALU.mult, ALU.subtract))
            link(nc.vector.tensor_tensor(t_step[:, 1:E], t_delta[:, 1:E], t_delta[:, 0:E - 1], ALU.subtract))
            over = (P, PAIRS * 2 * TOPK, E - 1)
            link(nc.vector.tensor_tensor(t_past[:], flat(slots[:]).unsqueeze(2).broadcast_to(over),
                                         t_base[:, 1:E].unsqueeze(1).broadcast_to(over), ALU.is_ge))
            link(nc.vector.tensor_tensor(t_past[:], t_past[:], t_step[:, 1:E].unsqueeze(1).broadcast_to(over), ALU.mult))
            link(nc.vector.tensor_reduce(t_moved[:], t_past[:], AX, ALU.add))
            link(nc.vector.tensor_tensor(flat(y_rows[:]), flat(slots[:]), t_moved[:], ALU.add))

            def step(s):
                if (s + 1).of(BLOCKS):
                    j = s + 1
                    dve.wait_ge(S["rows_hi"], j.v + 1)
                    wait(dve, S["h_ps"], (j.v - 1) * 2)
                    nc.vector.tensor_tensor(flat(xgl[:, j.mod(2)]), B_ROWS[j.mod(2)][:],
                                            flat(xgh[:, j.mod(2)]), ALU.subtract).then_inc(S["rows_lo"], 1)
                if s.of(BLOCKS):
                    bank = B_H[s.mod(2)]
                    wait(dve, S["hid_done"], s.v)
                    for a in range(2):
                        dve.wait_ge(S["tanh_done"], s.v * 2 + a + 1)
                        nc.vector.scalar_tensor_tensor(gate_a[:, a], th[:, a], 1.0, bank[a][:, 0:F],
                                                       ALU.add, ALU.mult).then_inc(S["gated"], 1)
                    for a in range(2):
                        dve.wait_ge(S["gated"], s.v * 2 + a + 1)
                        if a == 0:
                            wait(dve, S["hidT_ps"], s.v)
                        last = nc.vector.scalar_tensor_tensor(hid[:, a], gate_a[:, a], 0.5, bank[a][:, F:2 * F],
                                                              ALU.mult, ALU.mult)
                    last.then_inc(S["hid_done"], 1)
                if (s - 1).of(BLOCKS):
                    j = s - 1
                    dve.wait_ge(S["hid_hi"], j.v + 1)
                    wait(dve, S["yb_ps"], j.v - 1)
                    nc.vector.tensor_tensor(flat(hidl[:, j.mod(2)]), B_HT[:], flat(hidh[:, j.mod(2)]), ALU.subtract)\
                        .then_inc(S["hid_lo"], 1)

            steps_b(dve, step)

            def step(s):
                if (s + 2).of(PAIRS):
                    q = s + 2
                    b = q.mod(2)
                    nc.vector.tensor_copy(ckeep[:, b, :], row_of(keep, q.v)).then_inc(S["c_kept"], 1)
                    dve.wait_ge(S["c_kept"], q.v + 1)
                    wait(dve, S["c_T_ps"], q.v - 1)
                    normalise(cxn, ckeep[:, b, 0:4].rearrange("p (t s) -> p t s", t=2), q).then_inc(S["c_xn"], 1)
                if (s + 1).of(PAIRS):
                    q = s + 1
                    dve.wait_ge(S["c_hi"], q.v + 1)
                    wait(dve, S["c_h_ps"], q.v - 1)
                    nc.vector.tensor_tensor(flat(cxl[:, q.mod(2)]), C_XT[:], flat(cxh[:, q.mod(2)]), ALU.subtract)\
                        .then_inc(S["c_lo"], 1)
                if s.of(PAIRS):
                    dve.wait_ge(S["c_tanh"], s.v + 1)
                    nc.vector.scalar_tensor_tensor(flat(cgate[:]), flat(cth[:]), 1.0, C_A[s.mod(2)][:],
                                                   ALU.add, ALU.mult).then_inc(S["c_gated"], 1)
                    dve.wait_ge(S["c_gated"], s.v + 1)
                    wait(dve, S["c_hid_hi"], s.v)
                    nc.vector.scalar_tensor_tensor(flat(chid[:]), flat(cgate[:]), 0.5, C_B[s.mod(2)][:],
                                                   ALU.mult, ALU.mult).then_inc(S["c_hid"], 1)
                    dve.wait_ge(S["c_hid_hi"], s.v + 1)
                    nc.vector.tensor_tensor(chidl[:], chid[:], chidh[:], ALU.subtract).then_inc(S["c_hid_lo"], 1)
                if (s - 1).of(PAIRS):
                    q = s - 1
                    b = q.mod(2)
                    dve.wait_ge(S["c_y_ps"], q.v + 1)
                    wait(dve, out_stored[b], q.div(2) * 16)
                    nc.vector.tensor_tensor(acc[:, b], C_Y[:].rearrange("p (t c) -> p t c", t=2), two(xs, q),
                                            ALU.add)
                    nc.vector.tensor_copy(cw[:, b, :], row_of(keep, q.v)[:, 4:8]).then_inc(S["c_base"], 1)
                    dve.wait_ge(S["c_base"], q.v + 1)
                    dve.wait_ge(y_gathered[b], q.div(2) * (32 * TOPK) + 32 * TOPK)
                    for k, done in ((0, S["c_added"]), (1, S["c_out"])):
                        for t in range(2):
                            n = 2 * t + k
                            last = nc.vector.scalar_tensor_tensor(acc[:, b, t, :], yg[:, b, n, :], cw[:, b, n:n + 1],
                                                                  acc[:, b, t, :], ALU.mult, ALU.add)
                        last.then_inc(done, 1)
                        if k == 0:
                            dve.wait_ge(S["c_added"], q.v + 1)

            steps_c(dve, step)

        @block.tensor
        def _(pe):
            def mm(out_, lhsT, rhs, first, last):
                return nc.tensor.matmul(out_, lhsT, rhs, start=first, stop=last)

            def mm3(out_, lh, ll, rh, rl, first, last):
                mm(out_, ll, rh, first, False)
                mm(out_, lh, rl, False, False)
                return mm(out_, lh, rh, False, last)

            def add_bias(out_, e, c0, c1):
                mm(out_, row_of(sel, e) if not isinstance(e, int) else sel[:, e, :], bias[:, c0:c1], True, False)

            pe.wait_ge(S["attn_w_loaded"], 32)
            pe.wait_ge(S["pool_made"], 4)
            for i, bank in ((0, B_XT), (1, B_CT)):
                for a in range(KC):
                    for k in range(KC):
                        last = nc.tensor.transpose(bank[:, k * C + a * P:k * C + (a + 1) * P],
                                                   wstage[:, i, a * C + k * P:a * C + (k + 1) * P], ident[:])
                last.then_inc(S["prep_ps"], 1)
            pe.wait_ge(S["prep_sb"], 2)
            for a in range(KC):
                for k in range(KC):
                    last = mm(B_TT[:, a * C:(a + 1) * C], xnT[:, 0, k, a * P:(a + 1) * P], cT[:, 0, k, :],
                              k == 0, k == KC - 1)
            last.then_inc(S["prep_ps"], 1)

            def transposes(bank, src):
                for t in range(2):
                    for k in range(KC):
                        last = nc.tensor.transpose(bank[:, k * 2 * P + t * P:k * 2 * P + (t + 1) * P],
                                                   src[:, t, k * P:(k + 1) * P], ident[:])
                return last

            def step(s):
                b = s.mod(2)
                if s.of(PAIRS):
                    wait(pe, S["prep_sb"], 3)
                    pe.wait_ge(S["xnT_sb"], s.v + 1)
                    wait(pe, S["tT_sb"], s.v)
                    for c in range(KC):
                        for k in range(KC):
                            last = mm(B_TT[:, c * 2 * P:(c + 1) * 2 * P], wqk[:, k, c * P:(c + 1) * P],
                                      xnT[:, b, k, :], k == 0, k == KC - 1)
                    last.then_inc(S["tT_ps"], 1)
                if (s - 2).of(PAIRS):
                    q = s - 2
                    pe.wait_ge(S["xn2_done"], q.v + 1)
                    transposes(B_XT, xn2[:, q.mod(2)]).then_inc(S["xn2T_ps"], 1)
                if s.of(PAIRS):
                    wait(pe, S["small_loaded"], 48)
                    pe.wait_ge(S["cT_sb"], s.v + 1)
                    wait(pe, S["v_sb"], s.v)
                    for t in range(2):
                        for k in range(KC):
                            last = mm(B_V[:, t * C:(t + 1) * C], cT[:, b, k, t * P:(t + 1) * P], wv_s[:, k, :],
                                      k == 0, k == KC - 1)
                    last.then_inc(S["v_ps"], 1)
                if (s - 2).of(PAIRS):
                    q = s - 2
                    pe.wait_ge(S["xn2T_sb"], q.v + 1)
                    wait(pe, S["slots_done"], q.v)
                    for t in range(2):
                        add_bias(B_R[:, t * E:(t + 1) * E], E + 2, 0, E)
                        for k in range(KC):
                            last = mm(B_R[:, t * E:(t + 1) * E], xn2T[:, q.mod(2), k, t * P:(t + 1) * P],
                                      gw_s[:, k, :], False, k == KC - 1)
                    last.then_inc(S["gate_ps"], 1)
                if s.of(PAIRS):
                    pe.wait_ge(S["tT_sb"], s.v + 1)
                    wait(pe, S["pT_sb"], s.v)
                    for t in range(2):
                        for k in range(KC):
                            last = mm(B_S[:, t * P:(t + 1) * P], tT[:, b, k, t * P:(t + 1) * P],
                                      cT[:, b, k, t * P:(t + 1) * P], k == 0, k == KC - 1)
                    last.then_inc(S["s_ps"], 1)
                if (s - 1).of(PAIRS):
                    q = s - 1
                    pe.wait_ge(S["bias_split"], 7)
                    pe.wait_ge(S["y_sb"], q.v + 1)
                    wait(pe, S["x2_done"], q.v)
                    for t in range(2):
                        add_bias(B_Z[:, t * C:(t + 1) * C], E + 1, 0, C)
                        for h in range(2):
                            last = mm(B_Z[:, t * C:(t + 1) * C],
                                      y[:, q.mod(2), t, :].rearrange("p (r h) -> p h r", h=2)[:, h, :],
                                      wp_s[:, h, :], False, h == 1)
                    last.then_inc(S["z_ps"], 1)
                if s.of(PAIRS):
                    pe.wait_ge(S["exp_done"], s.v + 1)
                    for t in range(2):
                        last = nc.tensor.transpose(B_S[:, (2 + t) * P:(3 + t) * P], prob[:, b, t, :], ident[:])
                    last.then_inc(S["pT_ps"], 1)
                if (s + 1).of(PAIRS):
                    q = s + 1
                    pe.wait_ge(S["xn_done"], q.v + 1)
                    wait(pe, S["xn2T_sb"], s.v - 1)
                    transposes(B_XT, xn[:, q.mod(2)]).then_inc(S["xnT_ps"], 1)
                    pe.wait_ge(ctx_loaded[q.mod(2)], q.div(2) * 16 + 16)
                    transposes(B_CT, cx[:, q.mod(2)]).then_inc(S["cT_ps"], 1)
                if s.of(PAIRS):
                    pe.wait_ge(S["pT_sb"], s.v + 1)
                    pe.wait_ge(S["v_sb"], s.v + 1)
                    wait(pe, S["y_sb"], s.v)
                    for t in range(2):
                        last = mm(B_Y[:, t * C:(t + 1) * C], pT[:, b, t * P:(t + 1) * P], v[:, b, t, :], True, True)
                    last.then_inc(S["y_ps"], 1)
                if (s - 2).of(PAIRS):
                    q = s - 2
                    pe.wait_ge(S["hot_done"], q.v + 1)
                    r0 = 64
                    mm(B_R[:, r0:r0 + E], below[:], both[:, 0, :], True, True)
                    mm(B_R[:, r0 + E:r0 + 2 * E], below[:], both[:, 1, :], True, False)
                    mm(B_R[:, r0 + E:r0 + 2 * E], ones[:], both[:, 0, :], False, True)
                    mm(B_R[:, r0 + 2 * E:r0 + 3 * E], ones[:], both[:, 0, :], True, False)
                    mm(B_R[:, r0 + 2 * E:r0 + 3 * E], ones[:], both[:, 1, :], False, True).then_inc(S["place_ps"], 1)

            steps_a(pe, step)

            def expert_of_block(j):
                return pe.value_load(block_expert[0:1, bass.ds(j.v, 1)], min_val=0, max_val=E - 1)

            pe.wait_ge(S["table_done"], 1)
            pe.wait_ge(S["w_lo"], E * KC)

            def step(s):
                if (s + 1).of(BLOCKS):
                    j = s + 1
                    i = j.mod(2)
                    pe.wait_ge(rows_loaded[i], j.div(2) * 16 + 16)
                    wait(pe, S["rows_lo"], j.v - 1)
                    transposes(B_ROWS[i], xg[:, i]).then_inc(S["rowsT_ps"], 1)
                if s.of(BLOCKS):
                    i = s.mod(2)
                    e = expert_of_block(s)
                    pe.wait_ge(S["rows_lo"], s.v + 1)
                    wait(pe, S["hid_done"], s.v - 1)
                    for a in range(2):
                        rows = slice(a * P, (a + 1) * P)
                        add_bias(B_H[i][a][:], e, 0, 2 * F)
                        for k in range(KC):
                            last = mm3(B_H[i][a][:], xgh[:, i, k, rows], xgl[:, i, k, rows],
                                       row_of(rw1h, e * KC + k), row_of(rw1l, e * KC + k), False, k == KC - 1)
                        last.then_inc(S["h_ps"], 1)
                if (s - 1).of(BLOCKS):
                    j = s - 1
                    pe.wait_ge(S["hid_done"], j.v + 1)
                    wait(pe, S["hid_lo"], j.v)
                    transposes(B_HT, hid).then_inc(S["hidT_ps"], 1)
                if (s - 2).of(BLOCKS):
                    j = s - 2
                    i = j.mod(2)
                    e = expert_of_block(j)
                    pe.wait_ge(S["hid_lo"], j.v + 1)
                    wait(pe, S["yb_sb"], j.v)
                    for a in range(2):
                        rows, o = slice(a * P, (a + 1) * P), B_YB[:, a * C:(a + 1) * C]
                        add_bias(o, e, 2 * F, 2 * F + C)
                        for k in range(KF):
                            last = mm3(o, hidh[:, i, k, rows], hidl[:, i, k, rows], row_of(rw2h, e * KF + k),
                                       row_of(rw2l, e * KF + k), False, k == KF - 1)
                    last.then_inc(S["yb_ps"], 1)

            steps_b(pe, step)

            pe.wait_ge(S["shared_lo"], 1)
            pe.wait_ge(S["yb_sb"], BLOCKS)

            def step(s):
                if (s + 1).of(PAIRS):
                    q = s + 1
                    pe.wait_ge(S["c_xn"], q.v + 1)
                    wait(pe, S["c_lo"], q.v)
                    transposes(C_XT, cxn[:, q.mod(2)]).then_inc(S["c_T_ps"], 1)
                if s.of(PAIRS):
                    b = s.mod(2)
                    pe.wait_ge(S["c_lo"], s.v + 1)
                    wait(pe, S["c_hid"], s.v - 1)
                    for half, bank in ((0, C_A[b]), (1, C_B[b])):
                        for f in range(KF):
                            o = bank[:, f * 2 * P:(f + 1) * 2 * P]
                            c0 = half * F + f * P
                            mm(o, bias[:, c0:c0 + P], sel[:, E, :].unsqueeze(1).broadcast_to((P, 2, P)), True, False)
                            for k in range(KC):
                                last = mm3(o, sw1h[:, k, c0:c0 + P], sw1l[:, k, c0:c0 + P], cxh[:, b, k, :],
                                           cxl[:, b, k, :], False, k == KC - 1)
                    last.then_inc(S["c_h_ps"], 1)
                if (s - 1).of(PAIRS):
                    q = s - 1
                    pe.wait_ge(S["c_hid_lo"], q.v + 1)
                    wait(pe, S["c_base"], q.v)
                    for t in range(2):
                        o = C_Y[:, t * C:(t + 1) * C]
                        add_bias(o, E, 2 * F, 2 * F + C)
                        for k in range(KF):
                            last = mm3(o, chidh[:, k, t * P:(t + 1) * P], chidl[:, k, t * P:(t + 1) * P],
                                       sw2h[:, k, :], sw2l[:, k, :], False, k == KF - 1)
                    last.then_inc(S["c_y_ps"], 1)

            steps_c(pe, step)


_INS = ['x', 'ctx_1024', 'L0_xattn_Wq', 'L0_xattn_Wk', 'L0_xattn_Wv', 'L0_xattn_Wp', 'L0_xattn_bp',
        'L0_ffn_gate_w', 'L0_ffn_gate_b', 'L0_ffn_sw1', 'L0_ffn_sb1', 'L0_ffn_sw2', 'L0_ffn_sb2',
        'L0_ffn_rw1', 'L0_ffn_rb1', 'L0_ffn_rw2', 'L0_ffn_rb2']


def kernel(**inputs):
    import numpy as _np
    import concourse.bacc as _bacc
    from concourse import mybir as _mybir
    from concourse.bass_utils import run_bass_kernel_spmd as _run

    nc = _bacc.Bacc("TRN2", target_bir_lowering=False, num_devices=1)
    arrays, args = {}, []
    for name in _INS:
        a = _np.ascontiguousarray(inputs[name])
        arrays[f"in_{name}"] = a
        args.append(nc.dram_tensor(f"in_{name}", a.shape, _mybir.dt.from_np(a.dtype), kind="ExternalInput").ap())
    shape = tuple(inputs['x'].shape)
    args.append(nc.dram_tensor("out_0", shape, _mybir.dt.float32, kind="ExternalOutput").ap())
    cross_attention_moe_kernel(nc, *args)
    r = _run(nc, [arrays], core_ids=[0])
    return r.results[0]["out_0"]
```

```python
import concourse.bass as bass
from concourse import mybir
from contextlib import ExitStack


def cross_attention_moe_kernel(nc, x, ctx, wq, wk, wv, wp, bp, gate_w, gate_b,
                               sw1, sb1, sw2, sb2, rw1, rb1, rw2, rb2, out):
    f32, f32r, bf16 = mybir.dt.float32, mybir.dt.float32r, mybir.dt.bfloat16
    i32, u32 = mybir.dt.int32, mybir.dt.uint32
    ALU, ACT, AX = mybir.AluOpType, mybir.ActivationFunctionType, mybir.AxisListType.X

    P = 128
    B, N, C = x.shape
    E = gate_w.shape[1]
    F = rw2.shape[1]
    TOPK = 2
    KC = C // P
    KF = F // P
    PAIRS = B // 2
    EPS = 1e-5
    SCALE = float(C) ** -0.5 * 8 ** 0.5
    BR = 2 * P
    CAP = B * N + BR
    BLOCKS = TOPK * B * N // BR + E - 1
    SPARE = E - 1
    ROWS = E * CAP + SPARE * BR
    POOL_MADE, TABLE_LINKS = 20, 14
    EARLY = 2
    assert N == P and F == C and C == 2 * P

    x_t = x.rearrange("b n c -> n b c")
    ctx_t = ctx.rearrange("b n c -> n b c")
    out_t = out.rearrange("b n c -> n b c")
    rw1_t = rw1.rearrange("e (k p) f -> p (e k) f", p=P)
    rw2_t = rw2.rearrange("e (k p) f -> p (e k) f", p=P)

    sorted_x = nc.dram_tensor("sorted_x", (ROWS, C), f32, kind="Internal").ap()
    block_y = nc.dram_tensor("block_y", (BLOCKS * BR, C), f32, kind="Internal").ap()

    with ExitStack() as stack:
        def sb(name, shape, dt):
            return stack.enter_context(nc.sbuf_tensor(name, shape, dt))

        def pb(name, shape, dt):
            return stack.enter_context(nc.psum_tensor(name, shape, dt))

        def sem(name):
            return stack.enter_context(nc.semaphore(name))

        ident = sb("ident", [P, P], f32)
        below = sb("below", [P, P], bf16)
        ones = sb("ones", [P, P], bf16)
        sel = sb("sel", [P, E + 3, P], bf16)
        bias = sb("bias", [P, 3 * C], bf16)
        minus_half = sb("minus_half", [P, 2], f32)
        eps = sb("eps", [P, 2], f32)
        expert_of = sb("expert_of", [P, E], f32)
        wqkh = sb("wqkh", [P, KC, C], f32r)
        wv_s = sb("wv_s", [P, KC, C], f32)
        wph = sb("wph", [P, KC, C], f32r)
        gw_s = sb("gw_s", [P, KC, E], f32)
        with ExitStack() as before_shared:
            def sx(stack_, name, shape, dt):
                return stack_.enter_context(nc.sbuf_tensor(name, shape, dt))

            with ExitStack() as prologue:
                braw = sx(prologue, "braw", [E + 3, 3 * C], f32)
                brest = sx(prologue, "brest", [E + 3, 3 * C], f32)
                bpart = sx(prologue, "bpart", [E + 3, 3 * C], bf16)
                wqkl = sx(prologue, "wqkl", [P, KC, C], f32r)
                xnTl = sx(prologue, "xnTl", [P, KC, 2 * P], f32r)
            wpl = sx(before_shared, "wpl", [P, KC, C], f32r)
            yl = sx(before_shared, "yl", [P, 2, 2, C], f32r)
        sw1h = sb("sw1h", [P, KC, 2 * F], f32r)
        sw1l = sb("sw1l", [P, KC, 2 * F], f32r)
        sw2h = sb("sw2h", [P, KF, C], f32r)
        sw2l = sb("sw2l", [P, KF, C], f32r)
        rw1h = sb("rw1h", [P, E * KC, 2 * F], f32r)
        rw1l = sb("rw1l", [P, E * KC, 2 * F], f32r)
        rw2h = sb("rw2h", [P, E * KF, C], f32r)
        rw2l = sb("rw2l", [P, E * KF, C], f32r)
        wstage = sb("wstage", [P, 2, 3 * C], f32)

        xs = sb("xs", [P, B, C], f32)
        keep = sb("keep", [P, PAIRS, 8], f32)
        slots = sb("slots", [P, PAIRS, 2 * TOPK], f32)
        y_rows = sb("y_rows", [P, PAIRS, 2 * TOPK], i32)
        slot_ring = sb("slot_ring", [P, 2, 2 * TOPK], i32)
        counts = sb("counts", [P, E], f32)
        zeros = sb("zeros", [P, C], f32)
        block_expert = sb("block_expert", [1, BLOCKS], i32)
        block_row = sb("block_row", [1, BLOCKS], i32)
        pad_row = sb("pad_row", [1, E], i32)

        iota_e = sb("iota_e", [P, E], i32)
        iota_blocks = sb("iota_blocks", [1, BLOCKS], i32)

        t_base = sb("t_base", [P, E], f32)
        t_zero = sb("t_zero", [P, E], f32)
        t_j = sb("t_j", [1, BLOCKS], f32)

        with ExitStack() as phase_a:
            def sa(name, shape, dt):
                return phase_a.enter_context(nc.sbuf_tensor(name, shape, dt))

            cx = sa("cx", [P, 2, 2, C], f32)
            xn = sa("xn", [P, 2, 2, C], f32)
            xnTh = sa("xnTh", [P, 2, KC, 2 * P], f32r)
            cT = sa("cT", [P, 2, KC, 2 * P], f32)
            tT = sa("tT", [P, 2, KC, 2 * P], f32)
            v = sa("v", [P, 2, 2, C], f32)
            prob = sa("prob", [P, 2, 2, P], f32)
            pT = sa("pT", [P, 2, 2 * P], f32)
            yh = sa("yh", [P, 2, 2, C], f32r)
            xn2 = sa("xn2", [P, 4, 2, C], f32)
            xn2T = sa("xn2T", [P, 2, KC, 2 * P], f32)
            bn = sa("bn", [P, 2, 2, 6], f32)
            mv = sa("mv", [P, 2, 2, 2], f32)
            var = sa("var", [P, 2, 2], f32)
            bn2 = sa("bn2", [P, 2, 2, 6], f32)
            mv2 = sa("mv2", [P, 2, 2, 2], f32)
            var2 = sa("var2", [P, 2, 2], f32)
            nmax = sa("nmax", [P, 2, 2], f32)
            esum = sa("esum", [P, 2, 2], f32)
            rinv = sa("rinv", [P, 2, 2], f32)
            gmax = sa("gmax", [P, 2], f32)
            glog = sa("glog", [P, 2, E], f32)
            gexp = sa("gexp", [P, 2, E], f32)
            gsum = sa("gsum", [P, 2], f32)
            ginv = sa("ginv", [P, 2], f32)
            gprob = sa("gprob", [P, 2, E], f32)
            top8 = sa("top8", [P, 2, 8], f32)
            topi = sa("topi", [P, 2, 8], u32)
            topf = sa("topf", [P, 2, 8], f32)
            hot = sa("hot", [P, 2, TOPK, E], f32)
            both = sa("both", [P, 2, E], bf16)
            place = sa("place", [P, 2, E], f32)
            hotplace = sa("hotplace", [P, 2, TOPK, E], f32)
            slotf = sa("slotf", [P, 2 * TOPK], f32)

        xg = sb("xg", [P, 2, 2, C], f32)
        xgh, xgl = sb("xgh", [P, 2, KC, BR], f32r), sb("xgl", [P, 2, KC, BR], f32r)
        assert F == C and KF == KC == 2
        th, gate_a, hid = sb("th", [P, 2, F], f32), sb("gate_a", [P, 2, F], f32), sb("hid", [P, 2, F], f32)
        hidh, hidl = sb("hidh", [P, 2, KF, BR], f32r), sb("hidl", [P, 2, KF, BR], f32r)
        yb = sb("yb", [P, 2, 2, C], f32)
        cxn, cxh, cxl = xg, xgh, xgl
        cth, cgate, chid = th, gate_a, hid
        chidh, chidl = hidh, hidl
        cslot = sb("cslot", [P, 2, 2 * TOPK], i32)
        yg = sb("yg", [P, 2, 2 * TOPK, C], f32)
        acc = sb("acc", [P, 2, 2, C], f32)
        t_n = sb("t_n", [P, E], f32)
        t_ni = sb("t_ni", [P, E], i32)
        t_nr = sb("t_nr", [P, E], i32)
        t_nb = sb("t_nb", [P, E], f32)
        t_cum = sb("t_cum", [P, E], f32)
        t_start = sb("t_start", [P, E], f32)
        t_delta = sb("t_delta", [P, E], f32)
        t_step = sb("t_step", [P, E], f32)
        t_past = sb("t_past", [P, PAIRS * 2 * TOPK, E - 1], f32)
        t_moved = sb("t_moved", [P, PAIRS * 2 * TOPK], f32)
        t_ge = sb("t_ge", [1, BLOCKS, E], f32)
        t_e = sb("t_e", [1, BLOCKS], f32)
        t_before = sb("t_before", [1, BLOCKS], f32)
        t_in = sb("t_in", [1, BLOCKS], f32)
        t_in2 = sb("t_in2", [1, BLOCKS], f32)
        t_row = sb("t_row", [1, BLOCKS], f32)

        banks = [stack.enter_context(nc.psum_tensor(f"bank{i}", [P, 512], f32)) for i in range(8)]
        B_XT, B_CT, B_TT, B_V, B_S, B_Y, B_Z, B_R = banks
        B_ROWS, B_H, B_HT, B_YB = banks[0:2], (banks[2:4], banks[4:6]), banks[6], banks[7]
        C_XT, C_H, C_Y = banks[0], (banks[2:4], banks[4:6]), banks[6:8]

        def flat(t):
            return t.rearrange("p a b -> p (a b)")

        names = """attn_w_loaded small_loaded bias_loaded shared_loaded braw_zeroed pool_made bias_split
            prep_ps prep_sb wqk_lo wp_hi wp_lo w_hi w_lo shared_hi shared_lo
            bn_done mv_done var_done rstd_done xn_done xnT_ps cT_ps xnT_sb xnT_lo cT_sb tT_ps v_ps tT_sb v_sb
            s_ps max_done exp_done rinv_done pT_ps pT_sb y_ps y_sb y_lo z_ps x2_done bn2_done mv2_done var2_done
            rstd2_done xn2_done stats_kept xn2T_ps xn2T_sb gate_ps gmax_done glog_done gexp_done gsum_made ginv_made gprob_made top_made topi_made topf_made hot_made
            hot_done place_ps counted counts_added hotplace_made slotf_made slots_done table_link table_done spare_zeroed
            rowsT_ps rows_hi rows_lo hid_done hidT_ps hid_hi hid_lo yb_ps yb_sb
            c_slot c_xn c_T_ps c_hi c_lo c_hid_lo c_y_ps c_base
            c_added c_out waited move_link""".split()
        S = {name: stack.enter_context(nc.semaphore(name)) for name in names}

        def by_parity(name, n=2):
            return [stack.enter_context(nc.semaphore(f"{name}{i}")) for i in range(n)]

        x_loaded, ctx_loaded, wstage_loaded = by_parity("x_loaded"), by_parity("ctx_loaded"), by_parity("wstage_loaded")
        scattered, y_stored = by_parity("scattered"), by_parity("y_stored")
        rows_loaded = by_parity("rows_loaded")
        padded = by_parity("padded")
        c_h_ps, c_tanh, c_gated = by_parity("c_h_ps"), by_parity("c_tanh"), by_parity("c_gated")
        c_hid, c_hid_hi = by_parity("c_hid"), by_parity("c_hid_hi")
        h_ps, tanh_done, gated = by_parity("h_ps"), by_parity("tanh_done"), by_parity("gated")
        y_gathered, out_stored = by_parity("y_gathered"), by_parity("out_stored")

        def wait(eng, semaphore, count):
            if not isinstance(count, int) or count > 0:
                eng.wait_ge(semaphore, count)

        def wait_apart(eng, semaphore, count):
            wait(eng, semaphore, count)
            if not isinstance(count, int):
                eng.sem_inc(S["waited"], 1)

        class At:

            def __init__(self, offset, r=None, unroll=2):
                self.offset, self.r, self.unroll = offset, r, unroll

            def __add__(self, n):
                return At(self.offset + n, self.r, self.unroll)

            def __sub__(self, n):
                return self + (-n)

            def of(self, total, first=0):
                return self.r is not None or first <= self.offset < total

            def mod(self, n):
                return self.offset % n

            def div(self, n):
                return self.offset // n + (0 if self.r is None else self.r * (self.unroll // n))

            @property
            def v(self):
                return self.offset if self.r is None else self.unroll * self.r + self.offset

        def run_steps(eng, step, first, peel, total, last, unroll):
            loops = (total - peel) // unroll
            for s in range(first, peel):
                step(At(s))
            with eng.Fori(0, loops) as r:
                for u in range(unroll):
                    step(At(peel + u, r, unroll))
            for s in range(peel + loops * unroll, last + 1):
                step(At(s))

        def steps_a(eng, step):
            run_steps(eng, step, -2, 5, PAIRS - 3, PAIRS + 3, 4)

        def steps_b(eng, step):
            run_steps(eng, step, -1, 4, BLOCKS - 3, BLOCKS + 1, 2)

        def steps_c(eng, step):
            run_steps(eng, lambda s: step(s, EARLY, PAIRS), EARLY - 2, EARLY + 2, PAIRS - 2, PAIRS + 1, 2)

        def steps_early(step, first=-2, end=EARLY + 2):
            for s in range(first, end):
                step(At(s), 0, EARLY)

        class Links:

            def __init__(self, eng, semaphore, per, q):
                self.eng, self.semaphore, self.left = eng, semaphore, per
                self.count = per * q

            def __call__(self, ins):
                self.count, self.left = self.count + 1, self.left - 1
                assert self.left >= 0
                ins.then_inc(self.semaphore, 1)
                wait_apart(self.eng, self.semaphore, self.count)

        def two(t, q):
            return t[:, bass.ds(2 * q.v, 2), :]

        def row_of(t, index):
            return t[:, bass.ds(index, 1), :].rearrange("p a f -> p (a f)")

        def in_halves(rows):
            return rows.rearrange("(p a) c -> p a c", a=2)

        def pad(eng, e):
            row = eng.value_load(pad_row[0:1, e:e + 1], min_val=0, max_val=E * CAP - BR)
            eng.dma_start(in_halves(sorted_x[bass.ds(row, BR), :]), zeros_block).then_inc(padded[e // (E // 2)], 16)

        zeros_block = zeros[:].unsqueeze(1).broadcast_to((P, 2, C))

        block = stack.enter_context(nc.Block())

        @block.sync
        def _(sp):
            for w, i in ((wq, 0), (wk, 1)):
                sp.dma_start(wstage[:, i, 0:KC * C].rearrange("p (k c) -> p k c", k=KC),
                             w.rearrange("(k p) c -> p k c", p=P)).then_inc(S["attn_w_loaded"], 16)
            for q in range(2):
                sp.dma_start(xs[:, 2 * q:2 * q + 2, :], x_t[:, 2 * q:2 * q + 2, :]).then_inc(x_loaded[q], 16)
                sp.dma_start(cx[:, q], ctx_t[:, 2 * q:2 * q + 2, :]).then_inc(ctx_loaded[q], 16)
            for dst, w in ((wv_s[:], wv), (xn2[:, 3], wp), (gw_s[:], gate_w)):
                sp.dma_start(dst, w.rearrange("(k p) c -> p k c", p=P)).then_inc(S["small_loaded"], 16)
            def load_biases():
                sp.wait_ge(S["braw_zeroed"], 1)
                for dst, b_dram in ((braw[0:E, 0:2 * F], rb1), (braw[0:E, 2 * F:2 * F + C], rb2),
                                    (braw[E:E + 1, 0:2 * F], sb1), (braw[E:E + 1, 2 * F:2 * F + C], sb2),
                                    (braw[E + 1:E + 2, 0:C], bp.rearrange("(a c) -> a c", a=1)),
                                    (braw[E + 2:E + 3, 0:E], gate_b.rearrange("(a c) -> a c", a=1))):
                    sp.dma_start(dst, b_dram).then_inc(S["bias_loaded"], 16)

            def step(s):
                if (s + 1).of(PAIRS - 2):
                    q = s + 3
                    sp.wait_ge(S["bn_done"], (s + 2).v)
                    sp.dma_start(two(xs, q), x_t[:, bass.ds(2 * q.v, 2), :]).then_inc(x_loaded[q.mod(2)], 16)
                if s.r is None and s.offset == 1:
                    load_biases()
                if s.of(PAIRS - 2):
                    q = s + 2
                    sp.wait_ge(S["cT_ps"], s.v + 1)
                    sp.dma_start(cx[:, q.mod(2)], ctx_t[:, bass.ds(2 * q.v, 2), :])\
                        .then_inc(ctx_loaded[q.mod(2)], 16)
                if s.of(E * KC):
                    wait(sp, S["prep_ps"], 2)
                    wait(sp, S["w_lo"], s.v - 1)
                    for c0, c1, w in ((0, 2 * F, rw1_t), (2 * F, 2 * F + C, rw2_t)):
                        sp.dma_start(wstage[:, s.mod(2), c0:c1], row_of(w, s.v)).then_inc(wstage_loaded[s.mod(2)], 16)

            steps_a(sp, step)

            sp.wait_ge(S["pool_made"], POOL_MADE)
            for n in range(SPARE):
                sp.dma_start(in_halves(sorted_x[E * CAP + n * BR:E * CAP + (n + 1) * BR, :]), zeros_block)\
                    .then_inc(S["spare_zeroed"], 16)

            sp.wait_ge(S["w_lo"], E * KC)
            for k in range(KC):
                for c0, c1, w in ((0, 2 * F, sw1), (2 * F, 2 * F + C, sw2)):
                    sp.dma_start(wstage[:, k, c0:c1], w[0, k * P:(k + 1) * P, :]).then_inc(S["shared_loaded"], 16)

            sp.wait_ge(S["table_done"], 1)
            for e in range(E // 2):
                pad(sp, e)
            for i in range(2):
                sp.wait_ge(padded[i], 16 * E // 2)
            sp.wait_ge(S["spare_zeroed"], 16 * SPARE)
            for i in range(2):
                sp.wait_ge(scattered[i], 16 * TOPK * B // 2)

            sp.wait_ge(S["c_T_ps"], EARLY)

            def rows_at(j):
                return bass.ds(sp.value_load(block_row[0:1, bass.ds(j.v, 1)], min_val=0, max_val=ROWS - BR), BR)

            def step(s):
                if (s + 3).of(BLOCKS):
                    j = s + 3
                    wait(sp, S["rowsT_ps"], j.v - 1)
                    sp.dma_start(xg[:, j.mod(2)], in_halves(sorted_x[rows_at(j), :]))\
                        .then_inc(rows_loaded[j.mod(2)], 16)
                if (s - 2).of(BLOCKS):
                    j = s - 2
                    sp.wait_ge(S["yb_sb"], j.v + 1)
                    sp.dma_start(in_halves(block_y[bass.ds(j.v * BR, BR), :]), yb[:, j.mod(2)])\
                        .then_inc(y_stored[j.mod(2)], 16)

            for s in (-3, -2):
                step(At(s))
            steps_b(sp, step)

            def step(s, lo, hi):
                if (s - 2).of(PAIRS):
                    q = s - 2
                    sp.wait_ge(S["c_out"], q.v + 1)
                    sp.dma_start(out_t[:, bass.ds(2 * q.v, 2), :], acc[:, q.mod(2)]).then_inc(out_stored[q.mod(2)], 16)

            steps_c(sp, step)
            for i in range(2):
                sp.wait_ge(out_stored[i], 16 * PAIRS // 2)

        @block.gpsimd
        def _(pool):
            made = Links(pool, S["pool_made"], POOL_MADE, 0)
            made(nc.gpsimd.memset(minus_half[:], -0.5))
            made(nc.gpsimd.memset(eps[:], EPS))
            made(nc.gpsimd.memset(ident[:], 0.0))
            made(nc.gpsimd.affine_select(out=ident[:], in_=ident[:], compare_op=ALU.not_equal, fill=1.0,
                                         base=0, pattern=[[-1, P]], channel_multiplier=1))

            nc.gpsimd.memset(braw[:], 0.0).then_inc(S["braw_zeroed"], 1)

            def more_constants():
                made(nc.gpsimd.memset(zeros[:], 0.0))
                made(nc.gpsimd.memset(bias[:], 0.0))
                made(nc.gpsimd.memset(sel[:], 0.0))
                for part in range(3):
                    made(nc.gpsimd.affine_select(out=sel[:], in_=sel[:], compare_op=ALU.not_equal, fill=1.0,
                                                 base=-32 * part, pattern=[[-1, E + 3], [0, P]], channel_multiplier=1))
                made(nc.gpsimd.memset(ones[:], 1.0))
                made(nc.gpsimd.affine_select(out=below[:], in_=ones[:], compare_op=ALU.is_gt, fill=0.0,
                                             base=0, pattern=[[1, P]], channel_multiplier=-1))
                made(nc.gpsimd.iota(iota_e[:], [[1, E]], base=0, channel_multiplier=0))
                made(nc.gpsimd.tensor_copy(expert_of[:], iota_e[:]))
                made(nc.gpsimd.iota(iota_e[:], [[CAP, E]], base=0, channel_multiplier=0))
                made(nc.gpsimd.tensor_copy(counts[:], iota_e[:]))
                made(nc.gpsimd.tensor_copy(t_base[:], iota_e[:]))
                made(nc.gpsimd.iota(iota_blocks[:], [[1, BLOCKS]], base=0, channel_multiplier=0))
                made(nc.gpsimd.tensor_copy(t_j[:], iota_blocks[:]))
                made(nc.gpsimd.memset(t_zero[:], 0.0))
                assert made.left == 0

            def inverse_deviation(moments, room, moments_done, room_done, done, q):
                b = q.mod(2)
                pool.wait_ge(moments_done, q.v + 1)
                nc.gpsimd.tensor_tensor(room[:, b], moments[:, b, :, 1], eps[:], ALU.add).then_inc(room_done, 1)
                pool.wait_ge(room_done, q.v + 1)
                nc.gpsimd.tensor_tensor(moments[:, b, :, 1], room[:, b], minus_half[:], ALU.pow).then_inc(done, 1)

            def step(s):
                if (s + 2).of(PAIRS):
                    inverse_deviation(mv, var, S["mv_done"], S["var_done"], S["rstd_done"], s + 2)
                if s.r is None and s.offset == 0:
                    more_constants()
                if (s - 4).of(PAIRS):
                    q = s - 4
                    wait_apart(pool, S["slots_done"], q.v + 1)
                    for n in range(2 * TOPK):
                        nc.gpsimd.indirect_dma_start(
                            out=sorted_x, out_offset=bass.IndirectOffsetOnAxis(
                                ap=slot_ring[:, q.mod(2), n:n + 1], axis=0),
                            in_=xn2[:, q.mod(4), n // TOPK, :], in_offset=None).then_inc(scattered[q.mod(2)], 16)
                if s.of(E * KC):
                    pool.wait_ge(S["w_hi"], s.v + 1)
                    nc.gpsimd.tensor_tensor(row_of(rw1l, s.v), wstage[:, s.mod(2), 0:2 * F], row_of(rw1h, s.v),
                                            ALU.subtract)
                    nc.gpsimd.tensor_tensor(row_of(rw2l, s.v), wstage[:, s.mod(2), 2 * F:2 * F + C],
                                            row_of(rw2h, s.v), ALU.subtract).then_inc(S["w_lo"], 1)
                if (s - 1).of(PAIRS):
                    inverse_deviation(mv2, var2, S["mv2_done"], S["var2_done"], S["rstd2_done"], s - 1)

            steps_a(pool, step)

            pool.wait_ge(S["table_done"], 1)
            for e in range(E // 2, E):
                pad(pool, e)

            pool.wait_ge(S["move_link"], 7)
            for i in range(2):
                pool.wait_ge(y_stored[i], 16 * ((BLOCKS + 1 - i) // 2))

            def step(s, lo, hi):
                if s.of(PAIRS):
                    q = s
                    wait(pool, S["c_out"], q.v - 1)
                    nc.gpsimd.tensor_copy(cslot[:, q.mod(2)], row_of(y_rows, q.v)).then_inc(S["c_slot"], 1)
                    wait_apart(pool, S["c_slot"], q.v + 1)
                    for n in range(2 * TOPK):
                        nc.gpsimd.indirect_dma_start(
                            out=yg[:, q.mod(2), n, :], out_offset=None, in_=block_y,
                            in_offset=bass.IndirectOffsetOnAxis(ap=cslot[:, q.mod(2), n:n + 1], axis=0))\
                            .then_inc(y_gathered[q.mod(2)], 16)

            steps_c(pool, step)

        @block.scalar
        def _(act):
            nc.scalar.preload_act_table(ACT.Exp)

            def copy(dst, src, **kw):
                return nc.scalar.activation(dst, src, ACT.Copy, **kw)

            act.wait_ge(S["prep_ps"], 1)
            copy(flat(tT[:, 0]), B_XT[:]).then_inc(S["prep_sb"], 1)
            act.wait_ge(S["prep_ps"], 2)
            copy(flat(cT[:, 0]), B_CT[:]).then_inc(S["prep_sb"], 1)
            act.wait_ge(S["prep_ps"], 3)
            copy(flat(wqkh[:]), B_TT[:], scale=SCALE).then_inc(S["prep_sb"], 1)

            def step(s):
                b = s.mod(2)
                if s.r is None and s.offset == PAIRS + 1:
                    act.wait_ge(S["shared_loaded"], 16 * 2 * KC)
                    act.wait_ge(S["z_ps"], PAIRS)
                    for k in range(KC):
                        copy(sw1h[:, k, :], wstage[:, k, 0:2 * F])
                        copy(sw2h[:, k, :], wstage[:, k, 2 * F:2 * F + C]).then_inc(S["shared_hi"], 1)
                if (s - 1).of(PAIRS):
                    q = s - 1
                    act.wait_ge(S["pT_ps"], q.v + 1)
                    wait(act, S["y_ps"], q.v - 1)
                    copy(pT[:, q.mod(2)], B_S[:, 2 * P:4 * P]).then_inc(S["pT_sb"], 1)
                if s.of(PAIRS):
                    act.wait_ge(S["tT_ps"], s.v + 1)
                    wait(act, S["s_ps"], s.v - 1)
                    copy(flat(tT[:, b]), B_TT[:]).then_inc(S["tT_sb"], 1)
                if (s + 1).of(PAIRS):
                    q = s + 1
                    act.wait_ge(S["xnT_ps"], q.v + 1)
                    wait(act, S["tT_ps"], q.v - 1)
                    copy(flat(xnTh[:, q.mod(2)]), B_XT[:]).then_inc(S["xnT_sb"], 1)
                if (s - 1).of(PAIRS):
                    q = s - 1
                    act.wait_ge(S["y_ps"], q.v + 1)
                    act.wait_ge(S["rinv_done"], q.v + 1)
                    wait(act, S["z_ps"], q.v - 1)
                    for t in range(2):
                        last = copy(yh[:, q.mod(2), t, :], B_Y[:, t * C:(t + 1) * C],
                                    scale=rinv[:, q.mod(2), t:t + 1])
                    last.then_inc(S["y_sb"], 1)
                if s.of(PAIRS):
                    act.wait_ge(S["v_ps"], s.v + 1)
                    wait(act, S["y_ps"], s.v - 1)
                    copy(flat(v[:, b]), B_V[:]).then_inc(S["v_sb"], 1)
                if s.of(E * KC):
                    act.wait_ge(wstage_loaded[b], (s.div(2) + 1) * 32)
                    copy(row_of(rw1h, s.v), wstage[:, b, 0:2 * F])
                    copy(row_of(rw2h, s.v), wstage[:, b, 2 * F:2 * F + C]).then_inc(S["w_hi"], 1)
                if (s - 2).of(PAIRS):
                    q = s - 2
                    act.wait_ge(S["xn2T_ps"], q.v + 1)
                    wait(act, S["gate_ps"], q.v - 1)
                    copy(flat(xn2T[:, q.mod(2)]), B_XT[:]).then_inc(S["xn2T_sb"], 1)
                if s.of(PAIRS):
                    act.wait_ge(S["max_done"], s.v + 1)
                    wait(act, S["pT_ps"], s.v - 1)
                    for t in range(2):
                        last = nc.scalar.activation(prob[:, b, t, :], B_S[:, t * P:(t + 1) * P], ACT.Exp,
                                                    bias=nmax[:, b, t:t + 1], accum_out=esum[:, b, t:t + 1])
                    last.then_inc(S["exp_done"], 1)
                if s.r is None and s.offset == 0:
                    act.wait_ge(S["small_loaded"], 48)
                    copy(flat(wph[:]), flat(xn2[:, 3])).then_inc(S["wp_hi"], 1)
                if (s - 2).of(PAIRS):
                    q = s - 2
                    act.wait_ge(S["glog_done"], q.v + 1)
                    nc.scalar.activation(gexp[:], glog[:], ACT.Exp).then_inc(S["gexp_done"], 1)
                if (s + 1).of(PAIRS):
                    q = s + 1
                    act.wait_ge(S["cT_ps"], q.v + 1)
                    wait(act, S["s_ps"], q.v - 1)
                    copy(flat(cT[:, q.mod(2)]), B_CT[:]).then_inc(S["cT_sb"], 1)

            steps_a(act, step)

            def shared_step(s, lo, hi):
                if (s + 1).of(hi, lo):
                    q = s + 1
                    act.wait_ge(S["c_T_ps"], q.v + 1)
                    wait(act, c_h_ps[1], q.v - 1)
                    copy(flat(cxh[:, q.mod(2)]), C_XT[:]).then_inc(S["c_hi"], 1)
                if (s + 2).of(hi, lo):
                    q = s + 2
                    wait(act, S["stats_kept"], min(q.offset + 1, PAIRS) if hi == EARLY else 0)
                    wait(act, S["c_T_ps"], q.v - 1)
                    for t in range(2):
                        last = nc.scalar.activation(cxn[:, q.mod(2), t, :], row_of(xs, q.v * 2 + t), ACT.Identity,
                                                    bias=row_of(keep, q.v)[:, t:t + 1],
                                                    scale=row_of(keep, q.v)[:, 2 + t:3 + t])
                    last.then_inc(S["c_xn"], 1)
                if s.of(hi, lo):
                    for f in range(KF):
                        act.wait_ge(c_h_ps[f], s.v + 1)
                        wait(act, c_gated[f], s.v)
                        nc.scalar.activation(cth[:, f], C_H[s.mod(2)][f][:, 0:2 * P], ACT.Tanh, scale=0.5)\
                            .then_inc(c_tanh[f], 1)
                    for f in range(KF):
                        act.wait_ge(c_hid[f], s.v + 1)
                        wait(act, S["c_y_ps"], s.v - 1)
                        copy(chidh[:, s.mod(2), f], chid[:, f]).then_inc(c_hid_hi[f], 1)

            steps_early(shared_step)

            def step(s):
                if (s + 1).of(BLOCKS):
                    j = s + 1
                    act.wait_ge(S["rowsT_ps"], j.v + 1)
                    wait(act, h_ps[1], j.v - 1)
                    copy(flat(xgh[:, j.mod(2)]), B_ROWS[j.mod(2)][:]).then_inc(S["rows_hi"], 1)
                if s.of(BLOCKS):
                    for a in range(2):
                        act.wait_ge(h_ps[a], s.v + 1)
                        wait(act, gated[a], s.v)
                        nc.scalar.activation(th[:, a], B_H[s.mod(2)][a][:, 0:F], ACT.Tanh, scale=0.5)\
                            .then_inc(tanh_done[a], 1)
                if (s - 1).of(BLOCKS):
                    j = s - 1
                    act.wait_ge(S["hidT_ps"], j.v + 1)
                    wait(act, S["yb_ps"], j.v - 1)
                    copy(flat(hidh[:, j.mod(2)]), B_HT[:]).then_inc(S["hid_hi"], 1)
                if (s - 2).of(BLOCKS):
                    j = s - 2
                    act.wait_ge(S["yb_ps"], j.v + 1)
                    wait(act, y_stored[j.mod(2)], j.div(2) * 16)
                    copy(flat(yb[:, j.mod(2)]), B_YB[:]).then_inc(S["yb_sb"], 1)

            steps_b(act, step)

            steps_c(act, shared_step)

        @block.vector
        def _(dve):
            def row_stats(src, stats6, done, q):
                for t in range(2):
                    last = nc.vector.bn_stats(stats6[:, q.mod(2), t, :], row_of(src, q.v * 2 + t))
                last.then_inc(done, 1)

            def moments(stats6, out, stats_done, done, q):
                wait_apart(dve, stats_done, q.v + 1)
                for t in range(2):
                    last = nc.vector.bn_aggr(out[:, q.mod(2), t, :], stats6[:, q.mod(2), t, :])
                last.then_inc(done, 1)

            def normalise(dst, mom, q):
                for t in range(2):
                    last = nc.vector.tensor_scalar(dst[:, t, :], row_of(xs, q.v * 2 + t), mom[:, t, 0:1],
                                                   mom[:, t, 1:2], ALU.subtract, ALU.mult)
                return last

            def split_shared(k):
                dve.wait_ge(S["shared_hi"], k + 1)
                nc.vector.tensor_tensor(sw1l[:, k, :], wstage[:, k, 0:2 * F], sw1h[:, k, :], ALU.subtract)
                nc.vector.tensor_tensor(sw2l[:, k, :], wstage[:, k, 2 * F:2 * F + C], sw2h[:, k, :],
                                        ALU.subtract).then_inc(S["shared_lo"], 1)

            def split_bias():
                dve.wait_ge(S["bias_loaded"], 16 * 6)
                dve.wait_ge(S["pool_made"], 6)
                link = Links(dve, S["bias_split"], 5, 0)
                rows = E + 3
                link(nc.vector.tensor_copy(bias[0:rows, :], braw[:]))
                link(nc.vector.tensor_tensor(brest[:], braw[:], bias[0:rows, :], ALU.subtract))
                link(nc.vector.tensor_copy(bpart[:], brest[:]))
                nc.vector.tensor_copy(bias[32:32 + rows, :], brest[:])
                link(nc.vector.tensor_tensor(braw[:], brest[:], bpart[:], ALU.subtract))
                link(nc.vector.tensor_copy(bias[64:64 + rows, :], braw[:]))

            def step(s):
                b = s.mod(2)
                r, x_next, last_q = s - 3, s + 2, s - 1
                routed, prepared = r.of(PAIRS), x_next.of(PAIRS)
                if last_q.of(PAIRS):
                    dve.wait_ge(S["exp_done"], s.v)
                    wait(dve, S["y_sb"], s.v - 2)
                    nc.vector.reciprocal(rinv[:, last_q.mod(2), :], esum[:, last_q.mod(2), :])\
                        .then_inc(S["rinv_done"], 1)
                if s.r is None and s.offset == 1:
                    split_bias()
                    dve.wait_ge(S["wp_hi"], 1)
                    nc.vector.tensor_tensor(flat(wpl[:]), flat(xn2[:, 3]), flat(wph[:]), ALU.subtract)\
                        .then_inc(S["wp_lo"], 1)
                if s.r is None and s.offset == 3:
                    dve.wait_ge(S["pool_made"], POOL_MADE)
                if routed:
                    dve.wait_ge(S["gexp_done"], r.v + 1)
                    nc.vector.tensor_reduce(gsum[:], gexp[:], AX, ALU.add).then_inc(S["gsum_made"], 1)
                if prepared:
                    i = x_next.mod(2)
                    wait_apart(dve, x_loaded[i], x_next.div(2) * 16 + 16)
                    nc.vector.bn_stats(bn[:, i, 0, :], row_of(xs, x_next.v * 2))
                if routed:
                    dve.wait_ge(S["gsum_made"], r.v + 1)
                    nc.vector.reciprocal(ginv[:], gsum[:]).then_inc(S["ginv_made"], 1)
                if prepared:
                    nc.vector.bn_stats(bn[:, i, 1, :], row_of(xs, x_next.v * 2 + 1)).then_inc(S["bn_done"], 1)
                if (s - 2).of(PAIRS):
                    q = s - 2
                    dve.wait_ge(S["rstd2_done"], q.v + 1)
                    if (q - 4).of(PAIRS):
                        dve.wait_ge(scattered[q.mod(2)], (q - 4).div(2) * (32 * TOPK) + 32 * TOPK)
                    normalise(xn2[:, q.mod(4)], mv2[:, q.mod(2)], q).then_inc(S["xn2_done"], 1)
                    m2 = mv2[:, q.mod(2)]
                    nc.vector.scalar_tensor_tensor(row_of(keep, q.v)[:, 0:2], m2[:, :, 0], -1.0, m2[:, :, 1],
                                                   ALU.mult, ALU.mult)
                    nc.vector.tensor_copy(row_of(keep, q.v)[:, 2:4], m2[:, :, 1]).then_inc(S["stats_kept"], 1)
                if routed:
                    dve.wait_ge(S["ginv_made"], r.v + 1)
                    nc.vector.tensor_tensor(gprob[:], gexp[:], ginv[:].unsqueeze(2).broadcast_to((P, 2, E)),
                                            ALU.mult).then_inc(S["gprob_made"], 1)
                if prepared:
                    wait(dve, S["xn_done"], x_next.v - 1)
                    moments(bn, mv, S["bn_done"], S["mv_done"], x_next)
                if routed:
                    wait_apart(dve, S["gprob_made"], r.v + 1)
                    nc.vector.max(top8[:, 0, :], gprob[:, 0, :])
                    nc.vector.max(top8[:, 1, :], gprob[:, 1, :]).then_inc(S["top_made"], 1)
                if s.r is None and s.offset == -1:
                    dve.wait_ge(S["prep_sb"], 3)
                    nc.vector.scalar_tensor_tensor(flat(wqkl[:]), B_TT[:], SCALE, flat(wqkh[:]), ALU.mult,
                                                   ALU.subtract).then_inc(S["wqk_lo"], 1)
                if (s + 1).of(PAIRS):
                    q = s + 1
                    dve.wait_ge(S["xnT_sb"], q.v + 1)
                    wait(dve, S["tT_ps"], q.v)
                    nc.vector.tensor_tensor(flat(xnTl[:]), B_XT[:], flat(xnTh[:, q.mod(2)]), ALU.subtract)\
                        .then_inc(S["xnT_lo"], 1)
                if routed:
                    wait_apart(dve, S["top_made"], r.v + 1)
                    nc.vector.max_index(topi[:, 0, :], top8[:, 0, :], gprob[:, 0, :])
                    nc.vector.max_index(topi[:, 1, :], top8[:, 1, :], gprob[:, 1, :]).then_inc(S["topi_made"], 1)
                    dve.wait_ge(S["topi_made"], r.v + 1)
                    nc.vector.tensor_copy(topf[:], topi[:]).then_inc(S["topf_made"], 1)
                if last_q.of(PAIRS):
                    i = last_q.mod(2)
                    dve.wait_ge(S["y_sb"], s.v)
                    wait(dve, S["z_ps"], s.v - 2)
                    for t in range(2):
                        last = nc.vector.scalar_tensor_tensor(yl[:, i, t, :], B_Y[:, t * C:(t + 1) * C],
                                                              rinv[:, i, t:t + 1], yh[:, i, t, :],
                                                              ALU.mult, ALU.subtract)
                    last.then_inc(S["y_lo"], 1)
                if routed:
                    dve.wait_ge(S["topf_made"], r.v + 1)
                    nc.vector.tensor_tensor(
                        hot[:], expert_of[:].unsqueeze(1).unsqueeze(1).broadcast_to((P, 2, TOPK, E)),
                        topf[:, :, 0:TOPK].unsqueeze(3).broadcast_to((P, 2, TOPK, E)), ALU.is_equal)\
                        .then_inc(S["hot_made"], 1)
                    dve.wait_ge(S["hot_made"], r.v + 1)
                    nc.vector.tensor_tensor(both[:], hot[:, :, 0, :], hot[:, :, 1, :], ALU.add)\
                        .then_inc(S["hot_done"], 1)
                if s.r is None and s.offset == PAIRS + 1:
                    split_shared(0)
                if prepared:
                    dve.wait_ge(S["rstd_done"], x_next.v + 1)
                    wait(dve, S["xnT_ps"], x_next.v - 1)
                    normalise(xn[:, x_next.mod(2)], mv[:, x_next.mod(2)], x_next).then_inc(S["xn_done"], 1)
                if routed:
                    dve.wait_ge(S["place_ps"], r.v + 1)
                    nc.vector.tensor_tensor(place[:], B_R[:, 64:64 + 2 * E].rearrange("p (t e) -> p t e", t=2),
                                            counts[:].unsqueeze(1).broadcast_to((P, 2, E)), ALU.add)\
                        .then_inc(S["counted"], 1)
                    dve.wait_ge(S["counted"], r.v + 1)
                    nc.vector.tensor_tensor(counts[:], B_R[:, 64 + 2 * E:64 + 3 * E], counts[:], ALU.add)\
                        .then_inc(S["counts_added"], 1)
                    nc.vector.tensor_tensor(hotplace[:], hot[:], place[:].unsqueeze(2).broadcast_to((P, 2, TOPK, E)),
                                            ALU.mult).then_inc(S["hotplace_made"], 1)
                if routed:
                    dve.wait_ge(S["hotplace_made"], r.v + 1)
                    nc.vector.tensor_reduce(slotf[:], hotplace[:].rearrange("p t k e -> p (t k) e"),
                                            AX, ALU.add).then_inc(S["slotf_made"], 1)
                if (s - 1).of(PAIRS):
                    q = s - 1
                    dve.wait_ge(S["z_ps"], q.v + 1)
                    nc.vector.tensor_tensor(two(xs, q), B_Z[:].rearrange("p (t c) -> p t c", t=2), two(xs, q),
                                            ALU.add).then_inc(S["x2_done"], 1)
                if s.of(PAIRS):
                    dve.wait_ge(S["s_ps"], s.v + 1)
                    nc.vector.tensor_reduce(nmax[:, b, :], B_S[:, 0:2 * P].rearrange("p (t m) -> p t m", t=2),
                                            AX, ALU.max, negate=True).then_inc(S["max_done"], 1)
                if (s - 1).of(PAIRS):
                    wait_apart(dve, S["x2_done"], q.v + 1)
                    row_stats(xs, bn2, S["bn2_done"], q)
                if routed:
                    if (r - 2).of(PAIRS):
                        dve.wait_ge(scattered[r.mod(2)], (r - 2).div(2) * (32 * TOPK) + 32 * TOPK)
                    wait_apart(dve, S["slotf_made"], r.v + 1)
                    nc.vector.tensor_copy(row_of(slots, r.v), slotf[:])
                    nc.vector.tensor_copy(slot_ring[:, r.mod(2)], slotf[:])
                    nc.vector.tensor_copy(row_of(keep, r.v)[:, 4:8].rearrange("p (t k) -> p t k", t=2),
                                          top8[:, :, 0:TOPK]).then_inc(S["slots_done"], 1)
                if (s - 1).of(PAIRS):
                    wait(dve, S["stats_kept"], q.v - 1)
                    moments(bn2, mv2, S["bn2_done"], S["mv2_done"], q)
                if s.r is None and s.offset == PAIRS + 1:
                    split_shared(1)
                if (s - 2).of(PAIRS):
                    q = s - 2
                    dve.wait_ge(S["gate_ps"], q.v + 1)
                    logits = B_R[:, 0:2 * E].rearrange("p (t e) -> p t e", t=2)
                    nc.vector.tensor_reduce(gmax[:], logits, AX, ALU.max).then_inc(S["gmax_done"], 1)
                    dve.wait_ge(S["gmax_done"], q.v + 1)
                    wait(dve, S["gexp_done"], q.v)
                    nc.vector.tensor_tensor(glog[:], logits, gmax[:].unsqueeze(2).broadcast_to((P, 2, E)),
                                            ALU.subtract).then_inc(S["glog_done"], 1)

            steps_a(dve, step)

            def shared_step(s, lo, hi):
                if (s - 2).of(hi, lo):
                    q = s - 2
                    dve.wait_ge(S["c_y_ps"], q.v + 1)
                    nc.vector.tensor_tensor(two(xs, q), C_Y[q.mod(2)][:].rearrange("p (t c) -> p t c", t=2),
                                            two(xs, q), ALU.add).then_inc(S["c_base"], 1)
                if (s + 1).of(hi, lo):
                    q = s + 1
                    dve.wait_ge(S["c_hi"], q.v + 1)
                    wait(dve, c_h_ps[1], q.v - 1)
                    nc.vector.tensor_tensor(flat(cxl[:, q.mod(2)]), C_XT[:], flat(cxh[:, q.mod(2)]), ALU.subtract)\
                        .then_inc(S["c_lo"], 1)
                if s.of(hi, lo):
                    i = s.mod(2)
                    for f in range(KF):
                        dve.wait_ge(c_tanh[f], s.v + 1)
                        wait(dve, c_hid[f], s.v)
                        nc.vector.scalar_tensor_tensor(cgate[:, f], cth[:, f], 1.0, C_H[i][f][:, 0:2 * P],
                                                       ALU.add, ALU.mult).then_inc(c_gated[f], 1)
                        dve.wait_ge(c_gated[f], s.v + 1)
                        wait(dve, c_hid_hi[f], s.v)
                        nc.vector.scalar_tensor_tensor(chid[:, f], cgate[:, f], 0.5, C_H[i][f][:, 2 * P:4 * P],
                                                       ALU.mult, ALU.mult).then_inc(c_hid[f], 1)
                    for f in range(KF):
                        dve.wait_ge(c_hid_hi[f], s.v + 1)
                        last = nc.vector.tensor_tensor(chidl[:, i, f], chid[:, f], chidh[:, i, f], ALU.subtract)
                    last.then_inc(S["c_hid_lo"], 1)
                if hi == PAIRS and (s - 2).of(PAIRS):
                    q = s - 2
                    b = q.mod(2)
                    wait(dve, S["c_base"], q.v + 1)
                    wait(dve, out_stored[b], q.div(2) * 16)
                    dve.wait_ge(y_gathered[b], q.div(2) * (32 * TOPK) + 32 * TOPK)
                    for k, done in ((0, S["c_added"]), (1, S["c_out"])):
                        for t in range(2):
                            n = 2 * t + k
                            base = row_of(xs, q.v * 2 + t) if k == 0 else acc[:, b, t, :]
                            last = nc.vector.scalar_tensor_tensor(acc[:, b, t, :], yg[:, b, n, :],
                                                                  row_of(keep, q.v)[:, 4 + n:5 + n], base,
                                                                  ALU.mult, ALU.add)
                        last.then_inc(done, 1)
                        if k == 0:
                            dve.wait_ge(S["c_added"], q.v + 1)

            steps_early(shared_step, -2, 0)

            dve.wait_ge(S["slots_done"], PAIRS)
            link = Links(dve, S["table_link"], TABLE_LINKS, 0)
            link(nc.vector.tensor_tensor(t_n[:], counts[:], t_base[:], ALU.subtract))
            link(nc.vector.tensor_copy(pad_row[:], counts[0:1, :]))
            link(nc.vector.tensor_scalar(t_ni[:], t_n[:], float(BR - 1), None, ALU.add))
            link(nc.vector.tensor_scalar(t_nr[:], t_ni[:], BR.bit_length() - 1, None, ALU.arith_shift_right))
            link(nc.vector.tensor_copy(t_nb[:], t_nr[:]))
            link(nc.vector.tensor_tensor_scan(t_cum[:], t_nb[:], t_zero[:], 0.0, ALU.add, ALU.add))
            over = (1, BLOCKS, E)
            link(nc.vector.tensor_tensor(t_ge[:], t_cum[0:1, :].unsqueeze(1).broadcast_to(over),
                                         t_j[:].unsqueeze(2).broadcast_to(over), ALU.is_le))
            link(nc.vector.tensor_reduce(t_e[:], t_ge[:], AX, ALU.add))
            link(nc.vector.tensor_tensor(t_ge[:], t_ge[:], t_nb[0:1, :].unsqueeze(1).broadcast_to(over), ALU.mult))
            link(nc.vector.tensor_reduce(t_before[:], t_ge[:], AX, ALU.add))
            link(nc.vector.tensor_tensor(t_in[:], t_j[:], t_before[:], ALU.subtract))
            link(nc.vector.tensor_scalar(t_in2[:], t_in[:], float(BR), None, ALU.mult))
            link(nc.vector.scalar_tensor_tensor(t_row[:], t_e[:], float(CAP), t_in2[:], ALU.mult, ALU.add))
            link(nc.vector.tensor_scalar(block_expert[:], t_e[:], float(E - 1), None, ALU.min))
            assert link.left == 0
            nc.vector.tensor_copy(block_row[:], t_row[:]).then_inc(S["table_done"], 1)

            steps_early(shared_step, 0, EARLY + 2)

            link = Links(dve, S["move_link"], 7, 0)
            link(nc.vector.tensor_tensor(t_start[:], t_cum[:], t_nb[:], ALU.subtract))
            link(nc.vector.scalar_tensor_tensor(t_delta[:], t_start[:], float(BR), t_base[:], ALU.mult, ALU.subtract))
            link(nc.vector.tensor_tensor(t_step[:, 1:E], t_delta[:, 1:E], t_delta[:, 0:E - 1], ALU.subtract))
            over = (P, PAIRS * 2 * TOPK, E - 1)
            link(nc.vector.tensor_tensor(t_past[:], flat(slots[:]).unsqueeze(2).broadcast_to(over),
                                         t_base[:, 1:E].unsqueeze(1).broadcast_to(over), ALU.is_ge))
            link(nc.vector.tensor_tensor(t_past[:], t_past[:], t_step[:, 1:E].unsqueeze(1).broadcast_to(over), ALU.mult))
            link(nc.vector.tensor_reduce(t_moved[:], t_past[:], AX, ALU.add))
            link(nc.vector.tensor_tensor(flat(y_rows[:]), flat(slots[:]), t_moved[:], ALU.add))

            def step(s):
                if (s + 1).of(BLOCKS):
                    j = s + 1
                    dve.wait_ge(S["rows_hi"], j.v + 1)
                    wait(dve, h_ps[1], j.v - 1)
                    nc.vector.tensor_tensor(flat(xgl[:, j.mod(2)]), B_ROWS[j.mod(2)][:],
                                            flat(xgh[:, j.mod(2)]), ALU.subtract).then_inc(S["rows_lo"], 1)
                if s.of(BLOCKS):
                    bank = B_H[s.mod(2)]
                    wait(dve, S["hid_done"], s.v)
                    for a in range(2):
                        dve.wait_ge(tanh_done[a], s.v + 1)
                        nc.vector.scalar_tensor_tensor(gate_a[:, a], th[:, a], 1.0, bank[a][:, 0:F],
                                                       ALU.add, ALU.mult).then_inc(gated[a], 1)
                    for a in range(2):
                        dve.wait_ge(gated[a], s.v + 1)
                        if a == 0:
                            wait(dve, S["hidT_ps"], s.v)
                        last = nc.vector.scalar_tensor_tensor(hid[:, a], gate_a[:, a], 0.5, bank[a][:, F:2 * F],
                                                              ALU.mult, ALU.mult)
                    last.then_inc(S["hid_done"], 1)
                if (s - 1).of(BLOCKS):
                    j = s - 1
                    dve.wait_ge(S["hid_hi"], j.v + 1)
                    wait(dve, S["yb_ps"], j.v - 1)
                    nc.vector.tensor_tensor(flat(hidl[:, j.mod(2)]), B_HT[:], flat(hidh[:, j.mod(2)]), ALU.subtract)\
                        .then_inc(S["hid_lo"], 1)

            steps_b(dve, step)

            steps_c(dve, shared_step)

        @block.tensor
        def _(pe):
            def mm(out_, lhsT, rhs, first, last):
                return nc.tensor.matmul(out_, lhsT, rhs, start=first, stop=last)

            def mm3(out_, lh, ll, rh, rl, first, last):
                mm(out_, ll, rh, first, False)
                mm(out_, lh, rl, False, False)
                return mm(out_, lh, rh, False, last)

            def add_bias(out_, e, c0, c1):
                mm(out_, row_of(sel, e) if not isinstance(e, int) else sel[:, e, :], bias[:, c0:c1], True, False)

            pe.wait_ge(S["attn_w_loaded"], 32)
            pe.wait_ge(S["pool_made"], 4)
            for i, bank in ((0, B_XT), (1, B_CT)):
                for a in range(KC):
                    for k in range(KC):
                        last = nc.tensor.transpose(bank[:, k * C + a * P:k * C + (a + 1) * P],
                                                   wstage[:, i, a * C + k * P:a * C + (k + 1) * P], ident[:])
                last.then_inc(S["prep_ps"], 1)
            pe.wait_ge(S["prep_sb"], 2)
            for a in range(KC):
                for k in range(KC):
                    last = mm(B_TT[:, a * C:(a + 1) * C], tT[:, 0, k, a * P:(a + 1) * P], cT[:, 0, k, :],
                              k == 0, k == KC - 1)
            last.then_inc(S["prep_ps"], 1)

            def transposes(bank, src):
                for t in range(2):
                    for k in range(KC):
                        last = nc.tensor.transpose(bank[:, k * 2 * P + t * P:k * 2 * P + (t + 1) * P],
                                                   src[:, t, k * P:(k + 1) * P], ident[:])
                return last

            def step(s):
                b = s.mod(2)
                if (s - 1).of(PAIRS):
                    q = s - 1
                    pe.wait_ge(S["exp_done"], q.v + 1)
                    for t in range(2):
                        last = nc.tensor.transpose(B_S[:, (2 + t) * P:(3 + t) * P], prob[:, q.mod(2), t, :], ident[:])
                    last.then_inc(S["pT_ps"], 1)
                if s.of(PAIRS):
                    wait(pe, S["wqk_lo"], 1)
                    pe.wait_ge(S["xnT_lo"], s.v + 1)
                    wait(pe, S["tT_sb"], s.v)
                    for c in range(KC):
                        cols = slice(c * P, (c + 1) * P)
                        for k in range(KC):
                            last = mm3(B_TT[:, c * 2 * P:(c + 1) * 2 * P], wqkh[:, k, cols], wqkl[:, k, cols],
                                       xnTh[:, b, k, :], xnTl[:, k, :], k == 0, k == KC - 1)
                    last.then_inc(S["tT_ps"], 1)
                if (s + 1).of(PAIRS):
                    q = s + 1
                    pe.wait_ge(S["xn_done"], q.v + 1)
                    wait(pe, S["xn2T_sb"], s.v - 2)
                    transposes(B_XT, xn[:, q.mod(2)]).then_inc(S["xnT_ps"], 1)
                if (s - 1).of(PAIRS):
                    q = s - 1
                    pe.wait_ge(S["pT_sb"], q.v + 1)
                    pe.wait_ge(S["v_sb"], q.v + 1)
                    wait(pe, S["y_lo"], q.v)
                    for t in range(2):
                        last = mm(B_Y[:, t * C:(t + 1) * C], pT[:, q.mod(2), t * P:(t + 1) * P],
                                  v[:, q.mod(2), t, :], True, True)
                    last.then_inc(S["y_ps"], 1)
                if s.of(PAIRS):
                    wait(pe, S["small_loaded"], 48)
                    pe.wait_ge(S["cT_sb"], s.v + 1)
                    wait(pe, S["v_sb"], s.v)
                    for t in range(2):
                        for k in range(KC):
                            last = mm(B_V[:, t * C:(t + 1) * C], cT[:, b, k, t * P:(t + 1) * P], wv_s[:, k, :],
                                      k == 0, k == KC - 1)
                    last.then_inc(S["v_ps"], 1)
                if (s - 2).of(PAIRS):
                    q = s - 2
                    pe.wait_ge(S["xn2_done"], q.v + 1)
                    if (s + 1).of(PAIRS):
                        pe.wait_ge(S["xnT_lo"], s.v + 2)
                    transposes(B_XT, xn2[:, q.mod(4)]).then_inc(S["xn2T_ps"], 1)
                if (s - 3).of(PAIRS):
                    q = s - 3
                    pe.wait_ge(S["hot_done"], q.v + 1)
                    r0 = 64
                    mm(B_R[:, r0:r0 + E], below[:], both[:, 0, :], True, True)
                    mm(B_R[:, r0 + E:r0 + 2 * E], below[:], both[:, 1, :], True, False)
                    mm(B_R[:, r0 + E:r0 + 2 * E], ones[:], both[:, 0, :], False, True)
                    mm(B_R[:, r0 + 2 * E:r0 + 3 * E], ones[:], both[:, 0, :], True, False)
                    mm(B_R[:, r0 + 2 * E:r0 + 3 * E], ones[:], both[:, 1, :], False, True).then_inc(S["place_ps"], 1)
                if (s - 1).of(PAIRS):
                    q = s - 1
                    if s.r is None:
                        pe.wait_ge(S["bias_split"], 5)
                        pe.wait_ge(S["pool_made"], POOL_MADE)
                        pe.wait_ge(S["wp_lo"], 1)
                    pe.wait_ge(S["y_lo"], q.v + 1)
                    wait(pe, S["x2_done"], q.v)
                    halves_h, halves_l = (t_[:, q.mod(2)].rearrange("p t (r h) -> p t h r", h=2) for t_ in (yh, yl))
                    for t in range(2):
                        add_bias(B_Z[:, t * C:(t + 1) * C], E + 1, 0, C)
                        for h in range(2):
                            last = mm3(B_Z[:, t * C:(t + 1) * C], halves_h[:, t, h, :], halves_l[:, t, h, :],
                                       wph[:, h, :], wpl[:, h, :], False, h == 1)
                    last.then_inc(S["z_ps"], 1)
                if s.of(PAIRS):
                    pe.wait_ge(S["tT_sb"], s.v + 1)
                    wait(pe, S["pT_sb"], s.v)
                    for t in range(2):
                        for k in range(KC):
                            last = mm(B_S[:, t * P:(t + 1) * P], tT[:, b, k, t * P:(t + 1) * P],
                                      cT[:, b, k, t * P:(t + 1) * P], k == 0, k == KC - 1)
                    last.then_inc(S["s_ps"], 1)
                if (s - 2).of(PAIRS):
                    q = s - 2
                    pe.wait_ge(S["xn2T_sb"], q.v + 1)
                    wait(pe, S["counts_added"], q.v)
                    for t in range(2):
                        add_bias(B_R[:, t * E:(t + 1) * E], E + 2, 0, E)
                        for k in range(KC):
                            last = mm(B_R[:, t * E:(t + 1) * E], xn2T[:, q.mod(2), k, t * P:(t + 1) * P],
                                      gw_s[:, k, :], False, k == KC - 1)
                    last.then_inc(S["gate_ps"], 1)
                if (s + 1).of(PAIRS):
                    q = s + 1
                    pe.wait_ge(ctx_loaded[q.mod(2)], q.div(2) * 16 + 16)
                    transposes(B_CT, cx[:, q.mod(2)]).then_inc(S["cT_ps"], 1)

            steps_a(pe, step)

            def shared_step(s, lo, hi):
                if (s + 1).of(hi, lo):
                    q = s + 1
                    pe.wait_ge(S["c_xn"], q.v + 1)
                    wait(pe, S["c_lo"], q.v)
                    transposes(C_XT, cxn[:, q.mod(2)]).then_inc(S["c_T_ps"], 1)
                if s.of(hi, lo):
                    b = s.mod(2)
                    pe.wait_ge(S["c_lo"], s.v + 1)
                    wait(pe, c_hid[1], s.v - 1)
                    for f in range(KF):
                        for half in range(2):
                            o = C_H[b][f][:, half * 2 * P:(half + 1) * 2 * P]
                            c0 = half * F + f * P
                            mm(o, bias[:, c0:c0 + P], sel[:, E, :].unsqueeze(1).broadcast_to((P, 2, P)), True, False)
                            for k in range(KC):
                                last = mm3(o, sw1h[:, k, c0:c0 + P], sw1l[:, k, c0:c0 + P], cxh[:, b, k, :],
                                           cxl[:, b, k, :], False, k == KC - 1)
                        last.then_inc(c_h_ps[f], 1)
                if (s - 1).of(hi, lo):
                    q = s - 1
                    b = q.mod(2)
                    pe.wait_ge(S["c_hid_lo"], q.v + 1)
                    wait(pe, S["c_base"], q.v - 1)
                    for t in range(2):
                        o = C_Y[b][:, t * C:(t + 1) * C]
                        add_bias(o, E, 2 * F, 2 * F + C)
                        for k in range(KF):
                            last = mm3(o, chidh[:, b, k, t * P:(t + 1) * P], chidl[:, b, k, t * P:(t + 1) * P],
                                       sw2h[:, k, :], sw2l[:, k, :], False, k == KF - 1)
                    last.then_inc(S["c_y_ps"], 1)

            pe.wait_ge(S["shared_lo"], KC)
            steps_early(shared_step)
            pe.wait_ge(S["c_base"], EARLY)

            def expert_of_block(j):
                return pe.value_load(block_expert[0:1, bass.ds(j.v, 1)], min_val=0, max_val=E - 1)

            pe.wait_ge(S["table_done"], 1)
            pe.wait_ge(S["w_lo"], E * KC)

            def step(s):
                if (s + 1).of(BLOCKS):
                    j = s + 1
                    i = j.mod(2)
                    pe.wait_ge(rows_loaded[i], j.div(2) * 16 + 16)
                    wait(pe, S["rows_lo"], j.v - 1)
                    transposes(B_ROWS[i], xg[:, i]).then_inc(S["rowsT_ps"], 1)
                if s.of(BLOCKS):
                    i = s.mod(2)
                    e = expert_of_block(s)
                    pe.wait_ge(S["rows_lo"], s.v + 1)
                    wait(pe, S["hid_done"], s.v - 1)
                    for a in range(2):
                        rows = slice(a * P, (a + 1) * P)
                        add_bias(B_H[i][a][:], e, 0, 2 * F)
                        for k in range(KC):
                            last = mm3(B_H[i][a][:], xgh[:, i, k, rows], xgl[:, i, k, rows],
                                       row_of(rw1h, e * KC + k), row_of(rw1l, e * KC + k), False, k == KC - 1)
                        last.then_inc(h_ps[a], 1)
                if (s - 1).of(BLOCKS):
                    j = s - 1
                    pe.wait_ge(S["hid_done"], j.v + 1)
                    wait(pe, S["hid_lo"], j.v)
                    transposes(B_HT, hid).then_inc(S["hidT_ps"], 1)
                if (s - 2).of(BLOCKS):
                    j = s - 2
                    i = j.mod(2)
                    e = expert_of_block(j)
                    pe.wait_ge(S["hid_lo"], j.v + 1)
                    wait(pe, S["yb_sb"], j.v)
                    for a in range(2):
                        rows, o = slice(a * P, (a + 1) * P), B_YB[:, a * C:(a + 1) * C]
                        add_bias(o, e, 2 * F, 2 * F + C)
                        for k in range(KF):
                            last = mm3(o, hidh[:, i, k, rows], hidl[:, i, k, rows], row_of(rw2h, e * KF + k),
                                       row_of(rw2l, e * KF + k), False, k == KF - 1)
                    last.then_inc(S["yb_ps"], 1)

            steps_b(pe, step)

            pe.wait_ge(S["yb_sb"], BLOCKS)
            steps_c(pe, shared_step)


_INS = ['x', 'ctx_1024', 'L0_xattn_Wq', 'L0_xattn_Wk', 'L0_xattn_Wv', 'L0_xattn_Wp', 'L0_xattn_bp',
        'L0_ffn_gate_w', 'L0_ffn_gate_b', 'L0_ffn_sw1', 'L0_ffn_sb1', 'L0_ffn_sw2', 'L0_ffn_sb2',
        'L0_ffn_rw1', 'L0_ffn_rb1', 'L0_ffn_rw2', 'L0_ffn_rb2']


def kernel(**inputs):
    import numpy as _np
    import concourse.bacc as _bacc
    from concourse import mybir as _mybir
    from concourse.bass_utils import run_bass_kernel_spmd as _run

    nc = _bacc.Bacc("TRN2", target_bir_lowering=False, num_devices=1)
    arrays, args = {}, []
    for name in _INS:
        a = _np.ascontiguousarray(inputs[name])
        arrays[f"in_{name}"] = a
        args.append(nc.dram_tensor(f"in_{name}", a.shape, _mybir.dt.from_np(a.dtype), kind="ExternalInput").ap())
    shape = tuple(inputs['x'].shape)
    args.append(nc.dram_tensor("out_0", shape, _mybir.dt.float32, kind="ExternalOutput").ap())
    cross_attention_moe_kernel(nc, *args)
    r = _run(nc, [arrays], core_ids=[0])
    return r.results[0]["out_0"]
```

```python
import concourse.bass as bass
from concourse import mybir
from contextlib import ExitStack


def cross_attention_moe_kernel(nc, x, ctx, wq, wk, wv, wp, bp, gate_w, gate_b,
                               sw1, sb1, sw2, sb2, rw1, rb1, rw2, rb2, out):
    f32, f32r, bf16 = mybir.dt.float32, mybir.dt.float32r, mybir.dt.bfloat16
    i32, u32 = mybir.dt.int32, mybir.dt.uint32
    ALU, ACT, AX = mybir.AluOpType, mybir.ActivationFunctionType, mybir.AxisListType.X

    P = 128
    B, N, C = x.shape
    E = gate_w.shape[1]
    F = rw2.shape[1]
    TOPK = 2
    KC = C // P
    KF = F // P
    PAIRS = B // 2
    EPS = 1e-5
    SCALE = float(C) ** -0.5 * 8 ** 0.5
    BR = 2 * P
    CAP = B * N + BR
    BLOCKS = TOPK * B * N // BR + E - 1
    SPARE = E - 1
    ROWS = E * CAP + SPARE * BR
    POOL_MADE, TABLE_LINKS = 25, 10
    EARLY = 2
    LAST = 3
    assert N == P and F == C and C == 2 * P

    x_t = x.rearrange("b n c -> n b c")
    ctx_t = ctx.rearrange("b n c -> n b c")
    out_t = out.rearrange("b n c -> n b c")
    rw1_t = rw1.rearrange("e (k p) f -> p (e k) f", p=P)
    rw2_t = rw2.rearrange("e (k p) f -> p (e k) f", p=P)

    CX = C + 2
    sorted_x = nc.dram_tensor("sorted_x", (ROWS, CX), f32, kind="Internal").ap()
    FILL = TOPK + BLOCKS * BR
    routed = nc.dram_tensor("routed", (FILL + TOPK * B * N, C), f32, kind="Internal").ap()
    routed_t = routed[FILL:, :].rearrange("(b n k) c -> n b (k c)", n=N, k=TOPK)
    assert TOPK == 2

    with ExitStack() as stack:
        def sb(name, shape, dt):
            return stack.enter_context(nc.sbuf_tensor(name, shape, dt))

        def pb(name, shape, dt):
            return stack.enter_context(nc.psum_tensor(name, shape, dt))

        def sem(name):
            return stack.enter_context(nc.semaphore(name))

        ident = sb("ident", [P, P], f32)
        below = sb("below", [P, P], bf16)
        ones = sb("ones", [P, P], bf16)
        sel = sb("sel", [P, E + 3, P], bf16)
        bias = sb("bias", [P, 3 * C], bf16)
        minus_half = sb("minus_half", [P, 2], f32)
        eps = sb("eps", [P, 2], f32)
        sb1_s = sb("sb1_s", [P, 2 * KF], f32)
        expert_of = sb("expert_of", [P, E], f32)
        with ExitStack() as after_attention:
            def st(name, shape, dt):
                return after_attention.enter_context(nc.sbuf_tensor(name, shape, dt))

            t_n = st("t_n", [P, E], f32)
            t_ni = st("t_ni", [P, E], i32)
            t_nr = st("t_nr", [P, E], i32)
            t_nb = st("t_nb", [P, E], f32)
            t_skip = st("t_skip", [P, E], f32)
            t_cum = st("t_cum", [P, E], f32)
            t_ge = st("t_ge", [1, BLOCKS, E], f32)
            t_e = st("t_e", [1, BLOCKS], f32)
            t_before = st("t_before", [1, BLOCKS], f32)
            y_bias = st("y_bias", [P, E, C], f32)
            shared_bias = st("shared_bias", [P, C], f32)
        wqkh = sb("wqkh", [P, KC, C], f32r)
        wv_s = sb("wv_s", [P, KC, C], f32)
        wph = sb("wph", [P, KC, C], f32r)
        gw_s = sb("gw_s", [P, KC, E], f32)
        wstage = sb("wstage", [P, 2, 3 * C], f32)
        with ExitStack() as before_shared:
            def sx(stack_, name, shape, dt):
                return stack_.enter_context(nc.sbuf_tensor(name, shape, dt))

            with ExitStack() as prologue:
                braw = sx(prologue, "braw", [E + 3, 3 * C], f32)
                brest = sx(prologue, "brest", [E + 3, 3 * C], f32)
                bpart = sx(prologue, "bpart", [E + 3, 3 * C], bf16)
                wqkl = sx(prologue, "wqkl", [P, KC, C], f32r)
                xnTl = sx(prologue, "xnTl", [P, KC, 2 * P], f32r)
            wpl = sx(before_shared, "wpl", [P, KC, C], f32r)
            yl = sx(before_shared, "yl", [P, 2, 2, C], f32r)
        sw1h = sb("sw1h", [P, KC, 2 * F], f32r)
        sw1l = sb("sw1l", [P, KC, 2 * F], f32r)
        sw2h = sb("sw2h", [P, KF, C], f32r)
        sw2l = sb("sw2l", [P, KF, C], f32r)
        with ExitStack() as after_experts:
            yg = after_experts.enter_context(nc.sbuf_tensor("yg", [P, PAIRS, 2 * TOPK, C], f32))
        rw1h = sb("rw1h", [P, E * KC, 2 * F], f32r)
        rw1l = sb("rw1l", [P, E * KC, 2 * F], f32r)
        rw2h = sb("rw2h", [P, E * KF, C], f32r)
        rw2l = sb("rw2l", [P, E * KF, C], f32r)

        xs = sb("xs", [P, B, C], f32)
        keep = sb("keep", [P, PAIRS, 8], f32)
        slot_ring = sb("slot_ring", [P, 2, 2 * TOPK], i32)
        first_result = sb("first_result", [P, PAIRS, 2], f32)
        fill_row = sb("fill_row", [P, BLOCKS, 2], i32)
        dest = sb("dest", [P, BLOCKS, 2], i32)
        tags = sb("tags", [P, 2, 2, 2], f32)
        dest_ring = sb("dest_ring", [P, 2, 2], i32)
        counts = sb("counts", [P, E], f32)
        zeros = sb("zeros", [P, CX], f32)
        block_expert = sb("block_expert", [1, BLOCKS], i32)
        block_row = sb("block_row", [1, BLOCKS], i32)
        pad_row = sb("pad_row", [1, E], i32)

        iota_rows = sb("iota_rows", [P, PAIRS, 2], i32)
        iota_e = sb("iota_e", [P, E], i32)
        iota_blocks = sb("iota_blocks", [1, BLOCKS], i32)

        t_base = sb("t_base", [P, E], f32)
        t_zero = sb("t_zero", [P, E], f32)
        t_j = sb("t_j", [1, BLOCKS], f32)
        t_j_row = sb("t_j_row", [1, BLOCKS], f32)

        with ExitStack() as phase_a:
            def sa(name, shape, dt):
                return phase_a.enter_context(nc.sbuf_tensor(name, shape, dt))

            cx = sa("cx", [P, 2, 2, C], f32)
            xn = sa("xn", [P, 2, 2, C], f32)
            xnTh = sa("xnTh", [P, 2, KC, 2 * P], f32r)
            cT = sa("cT", [P, 2, KC, 2 * P], f32)
            tT = sa("tT", [P, 2, KC, 2 * P], f32)
            v = sa("v", [P, 2, 2, C], f32)
            prob = sa("prob", [P, 2, 2, P], f32)
            pT = sa("pT", [P, 2, 2 * P], f32)
            xn2 = sa("xn2", [P, 4, 2, CX], f32)
            yh = sa("yh", [P, 2, 2, C], f32r)
            xn2T = sa("xn2T", [P, 2, KC, 2 * P], f32)
            bn = sa("bn", [P, 2, 2, 6], f32)
            mv = sa("mv", [P, 2, 2, 2], f32)
            var = sa("var", [P, 2, 2], f32)
            bn2 = sa("bn2", [P, 2, 2, 6], f32)
            mv2 = sa("mv2", [P, 2, 2, 2], f32)
            var2 = sa("var2", [P, 2, 2], f32)
            nmax = sa("nmax", [P, 2, 2], f32)
            esum = sa("esum", [P, 2, 2], f32)
            rinv = sa("rinv", [P, 2, 2], f32)
            gmax = sa("gmax", [P, 2], f32)
            glog = sa("glog", [P, 2, E], f32)
            gexp = sa("gexp", [P, 2, E], f32)
            gsum = sa("gsum", [P, 2], f32)
            ginv = sa("ginv", [P, 2], f32)
            gprob = sa("gprob", [P, 2, E], f32)
            top8 = sa("top8", [P, 2, 8], f32)
            topi = sa("topi", [P, 2, 8], u32)
            topf = sa("topf", [P, 2, 8], f32)
            hot = sa("hot", [P, 2, TOPK, E], f32)
            both = sa("both", [P, 2, E], bf16)
            place = sa("place", [P, 2, E], f32)
            hotplace = sa("hotplace", [P, 2, TOPK, E], f32)
            slotf = sa("slotf", [P, 2 * TOPK], f32)

        xg = sb("xg", [P, 2, 2, CX], f32)
        xgh, xgl = sb("xgh", [P, 2, KC, BR], f32r), sb("xgl", [P, 2, KC, BR], f32r)
        assert F == C and KF == KC == 2
        hb, hid = sb("hb", [P, 2, 2 * F], f32), sb("hid", [P, 2, F], f32)
        hidh, hidl = sb("hidh", [P, 2, KF, BR], f32r), sb("hidl", [P, 2, KF, BR], f32r)
        yb = sb("yb", [P, 2, 2, C], f32)
        h_bias = sb("h_bias", [P, E, 2 * F], f32)
        cxn, cxh, cxl = xg, xgh, xgl
        cgate, chid = hb[:, :, 0:F], hid
        chidh, chidl = hidh, hidl
        banks = [stack.enter_context(nc.psum_tensor(f"bank{i}", [P, 512], f32)) for i in range(8)]
        B_XT, B_CT, B_TT, B_V, B_S, B_Y, B_Z, B_R = banks
        B_ROWS, B_H, B_HT, B_YB = banks[0:2], (banks[2:4], banks[4:6]), banks[6], banks[7]
        C_XT, C_H, C_Y = banks[0], (banks[2:4], banks[4:6]), banks[6:8]

        def bias_bank(e):
            return B_H[e // 2 % 2][e % 2]

        y_bias_banks = banks[0:2] + banks[6:8]
        assert E // 2 == len(y_bias_banks)

        def flat(t):
            return t.rearrange("p a b -> p (a b)")

        names = """attn_w_loaded small_loaded hidden_bias_loaded bias_loaded shared_loaded braw_zeroed pool_made bias_split
            prep_ps prep_sb wqk_lo wp_hi wp_lo w_hi w_lo shared_hi shared_lo shared_lo2
            bn_done mv_done var_done rstd_done xn_done xnT_ps cT_ps xnT_sb xnT_lo cT_sb tT_ps v_ps tT_sb v_sb
            s_ps max_done exp_done rinv_done pT_ps pT_sb y_ps y_sb y_lo z_ps x2_done bn2_done mv2_done var2_done
            rstd2_done xn2_done stats_kept xn2T_ps xn2T_sb gate_ps gmax_done glog_done gexp_done gsum_made ginv_made gprob_made top_made topi_made topf_made hot_made
            hot_done place_ps counted counts_added hotplace_made slotf_made slots_done table_link table_done spare_zeroed
            rowsT_ps rows_hi rows_lo hid_done hidT_ps hid_hi hid_lo yb_ps yb_sb
            c_xn c_T_ps c_hi c_lo c_hid_lo c_y_ps c_base
            h_bias_ps h_bias_sb y_bias_ps y_bias_sb out_stored c_last_out c_weighted c_biased c_added c_out waited""".split()
        S = {name: stack.enter_context(nc.semaphore(name)) for name in names}

        def by_parity(name, n=2):
            return [stack.enter_context(nc.semaphore(f"{name}{i}")) for i in range(n)]

        x_loaded, ctx_loaded, wstage_loaded = by_parity("x_loaded"), by_parity("ctx_loaded"), by_parity("wstage_loaded")
        scattered, y_stored = by_parity("scattered"), by_parity("y_stored")
        rows_loaded = by_parity("rows_loaded")
        padded = by_parity("padded")
        c_h_ps, c_gated = by_parity("c_h_ps"), by_parity("c_gated")
        c_hid, c_hid_hi = by_parity("c_hid"), by_parity("c_hid_hi")
        h_ps, h_sb, gated = by_parity("h_ps"), by_parity("h_sb"), by_parity("gated")
        y_loaded = by_parity("y_loaded", 4)

        def expert_of_block(eng, j):
            return eng.value_load(block_expert[0:1, bass.ds(j.v, 1)], min_val=0, max_val=E - 1)

        def wait(eng, semaphore, count):
            if not isinstance(count, int) or count > 0:
                eng.wait_ge(semaphore, count)

        def wait_apart(eng, semaphore, count):
            wait(eng, semaphore, count)
            if not isinstance(count, int):
                eng.sem_inc(S["waited"], 1)

        class At:

            def __init__(self, offset, r=None, unroll=2):
                self.offset, self.r, self.unroll = offset, r, unroll

            def __add__(self, n):
                return At(self.offset + n, self.r, self.unroll)

            def __sub__(self, n):
                return self + (-n)

            def of(self, total, first=0):
                return self.r is not None or first <= self.offset < total

            def mod(self, n):
                return self.offset % n

            def div(self, n):
                return self.offset // n + (0 if self.r is None else self.r * (self.unroll // n))

            @property
            def v(self):
                return self.offset if self.r is None else self.unroll * self.r + self.offset

        def run_steps(eng, step, first, peel, total, last, unroll):
            loops = (total - peel) // unroll
            for s in range(first, peel):
                step(At(s))
            with eng.Fori(0, loops) as r:
                for u in range(unroll):
                    step(At(peel + u, r, unroll))
            for s in range(peel + loops * unroll, last + 1):
                step(At(s))

        def steps_a(eng, step):
            run_steps(eng, step, -2, 5, PAIRS - 3, PAIRS + 3, 4)

        def steps_b(eng, step):
            run_steps(eng, step, -1, 4, BLOCKS - 3, BLOCKS + 1, 2)

        def steps_c(eng, step, first=EARLY):
            run_steps(eng, lambda s: step(s, EARLY, PAIRS), first, 6, PAIRS - 2, PAIRS + 3, 4)

        def summed(s):
            if s.r is None and s.offset >= PAIRS:
                return [At(q) for q in {PAIRS: (PAIRS - 4, PAIRS - 3, PAIRS - 2), PAIRS + 1: (PAIRS - 1,)}
                        .get(s.offset, ())]
            return [s - 4] if (s - 4).of(PAIRS) else []

        def yg_of(q, k):
            return yg[:, bass.ds(q.v, 1)].rearrange("p a (t k) c -> p (a t) k c", k=TOPK)[:, :, k, :]

        def steps_early(step, first=-2, end=EARLY + 2):
            for s in range(first, end):
                step(At(s), 0, EARLY)

        class Links:

            def __init__(self, eng, semaphore, per, q):
                self.eng, self.semaphore, self.left = eng, semaphore, per
                self.count = per * q

            def __call__(self, ins):
                self.count, self.left = self.count + 1, self.left - 1
                assert self.left >= 0
                ins.then_inc(self.semaphore, 1)
                wait_apart(self.eng, self.semaphore, self.count)

        def two(t, q):
            return t[:, bass.ds(2 * q.v, 2), :]

        def row_of(t, index):
            return t[:, bass.ds(index, 1), :].rearrange("p a f -> p (a f)")

        def in_halves(rows):
            return rows.rearrange("(p a) c -> p a c", a=2)

        SP_PADS = E // 2

        def pad(eng, e):
            row = eng.value_load(pad_row[0:1, e:e + 1], min_val=0, max_val=E * CAP - BR)
            eng.dma_start(in_halves(sorted_x[bass.ds(row, BR), :]), zeros_block).then_inc(padded[0 if e < SP_PADS else 1], 16)

        zeros_block = zeros[:].unsqueeze(1).broadcast_to((P, 2, CX))

        block = stack.enter_context(nc.Block())

        @block.sync
        def _(sp):
            for w, i in ((wq, 0), (wk, 1)):
                sp.dma_start(wstage[:, i, 0:KC * C].rearrange("p (k c) -> p k c", k=KC),
                             w.rearrange("(k p) c -> p k c", p=P)).then_inc(S["attn_w_loaded"], 16)
            for q in range(2):
                sp.dma_start(xs[:, 2 * q:2 * q + 2, :], x_t[:, 2 * q:2 * q + 2, :]).then_inc(x_loaded[q], 16)
                sp.dma_start(cx[:, q], ctx_t[:, 2 * q:2 * q + 2, :]).then_inc(ctx_loaded[q], 16)
            for dst, w in ((wv_s[:], wv), (xn2[:, 3, :, 0:C], wp), (gw_s[:], gate_w)):
                sp.dma_start(dst, w.rearrange("(k p) c -> p k c", p=P)).then_inc(S["small_loaded"], 16)
            def load_biases():
                sp.dma_start(sb1_s[:], sb1.rearrange("a (c p) -> p (a c)", p=P),
                             allow_slow_non_contiguous=True).then_inc(S["hidden_bias_loaded"], 16)
                sp.wait_ge(S["braw_zeroed"], 1)
                for dst, b_dram in ((braw[0:E, 0:2 * F], rb1), (braw[0:E, 2 * F:2 * F + C], rb2),
                                    (braw[E:E + 1, 0:2 * F], sb1), (braw[E:E + 1, 2 * F:2 * F + C], sb2),
                                    (braw[E + 1:E + 2, 0:C], bp.rearrange("(a c) -> a c", a=1)),
                                    (braw[E + 2:E + 3, 0:E], gate_b.rearrange("(a c) -> a c", a=1))):
                    sp.dma_start(dst, b_dram).then_inc(S["bias_loaded"], 16)

            def step(s):
                if (s + 1).of(PAIRS - 2):
                    q = s + 3
                    sp.wait_ge(S["bn_done"], (s + 2).v)
                    sp.dma_start(two(xs, q), x_t[:, bass.ds(2 * q.v, 2), :]).then_inc(x_loaded[q.mod(2)], 16)
                if s.r is None and s.offset == 0:
                    load_biases()
                if s.of(PAIRS - 2):
                    q = s + 2
                    sp.wait_ge(S["cT_ps"], s.v + 1)
                    sp.dma_start(cx[:, q.mod(2)], ctx_t[:, bass.ds(2 * q.v, 2), :])\
                        .then_inc(ctx_loaded[q.mod(2)], 16)
                if s.of(E * KC):
                    wait(sp, S["prep_ps"], 2)
                    wait(sp, S["w_lo"], s.v - 1)
                    for c0, c1, w in ((0, 2 * F, rw1_t), (2 * F, 2 * F + C, rw2_t)):
                        sp.dma_start(wstage[:, s.mod(2), c0:c1], row_of(w, s.v)).then_inc(wstage_loaded[s.mod(2)], 16)

            steps_a(sp, step)

            sp.wait_ge(S["pool_made"], POOL_MADE)
            for n in range(SPARE):
                sp.dma_start(in_halves(sorted_x[E * CAP + n * BR:E * CAP + (n + 1) * BR, :]), zeros_block)\
                    .then_inc(S["spare_zeroed"], 16)

            sp.wait_ge(S["w_lo"], E * KC)
            for k in range(KC):
                for c0, c1, w in ((0, 2 * F, sw1), (2 * F, 2 * F + C, sw2)):
                    sp.dma_start(wstage[:, k, c0:c1], w[0, k * P:(k + 1) * P, :]).then_inc(S["shared_loaded"], 16)

            sp.wait_ge(S["table_done"], 1)
            for e in range(SP_PADS):
                pad(sp, e)
            def rows_at(j):
                return bass.ds(sp.value_load(block_row[0:1, bass.ds(j.v, 1)], min_val=0, max_val=ROWS - BR), BR)

            first_rows = [rows_at(At(j)) for j in range(2)]
            for i, n in enumerate((SP_PADS, E - SP_PADS)):
                sp.wait_ge(padded[i], 16 * n)
            sp.wait_ge(S["spare_zeroed"], 16 * SPARE)
            for i in range(2):
                sp.wait_ge(scattered[i], 16 * TOPK * B // 2)

            sp.wait_ge(S["c_T_ps"], EARLY)

            def step(s):
                if (s + 3).of(BLOCKS):
                    j = s + 3
                    wait(sp, S["rows_lo"], j.v - 1)
                    rows = first_rows[j.offset] if j.r is None and j.offset < 2 else rows_at(j)
                    sp.dma_start(xg[:, j.mod(2)], in_halves(sorted_x[rows, :]))\
                        .then_inc(rows_loaded[j.mod(2)], 16)

            for s in (-3, -2):
                step(At(s))
            steps_b(sp, step)

            for i in range(2):
                sp.wait_ge(y_stored[i], 32 * ((BLOCKS + 1 - i) // 2))

            def step(s, lo, hi):
                if (s + 2).of(PAIRS):
                    q = s + 2
                    wait(sp, y_loaded[q.mod(4)], q.div(4) * 16)
                    sp.dma_start(yg[:, bass.ds(q.v, 1)].rearrange("p a (t k) c -> p (a t) (k c)", k=TOPK),
                                 two(routed_t, q)).then_inc(y_loaded[q.mod(4)], 16)
                for q in summed(s):
                    if q.r is None and q.offset >= PAIRS - LAST:
                        sp.wait_ge(S["c_last_out"], q.offset + 1 - (PAIRS - LAST))
                    else:
                        sp.wait_ge(S["c_out"], q.v + 1)
                    sp.dma_start(out_t[:, bass.ds(2 * q.v, 2), :], yg_of(q, 0)).then_inc(S["out_stored"], 16)

            steps_c(sp, step, -2)
            sp.wait_ge(S["out_stored"], 16 * PAIRS)

        @block.gpsimd
        def _(pool):
            made = Links(pool, S["pool_made"], POOL_MADE, 0)
            made(nc.gpsimd.memset(minus_half[:], -0.5))
            made(nc.gpsimd.memset(eps[:], EPS))
            made(nc.gpsimd.memset(ident[:], 0.0))
            made(nc.gpsimd.affine_select(out=ident[:], in_=ident[:], compare_op=ALU.not_equal, fill=1.0,
                                         base=0, pattern=[[-1, P]], channel_multiplier=1))

            nc.gpsimd.memset(braw[:], 0.0).then_inc(S["braw_zeroed"], 1)

            def more_constants():
                made(nc.gpsimd.memset(bias[:], 0.0))
                made(nc.gpsimd.memset(sel[:], 0.0))
                for part in range(3):
                    made(nc.gpsimd.affine_select(out=sel[:], in_=sel[:], compare_op=ALU.not_equal, fill=1.0,
                                                 base=-32 * part, pattern=[[-1, E + 3], [0, P]], channel_multiplier=1))
                made(nc.gpsimd.memset(ones[:], 1.0))
                made(nc.gpsimd.affine_select(out=below[:], in_=ones[:], compare_op=ALU.is_gt, fill=0.0,
                                             base=0, pattern=[[1, P]], channel_multiplier=-1))

            def constants_of_routing():
                made(nc.gpsimd.iota(iota_e[:], [[1, E]], base=0, channel_multiplier=0))
                made(nc.gpsimd.tensor_copy(expert_of[:], iota_e[:]))
                made(nc.gpsimd.iota(iota_e[:], [[CAP, E]], base=0, channel_multiplier=0))
                made(nc.gpsimd.tensor_copy(counts[:], iota_e[:]))
                made(nc.gpsimd.tensor_copy(t_base[:], iota_e[:]))
                made(nc.gpsimd.iota(iota_blocks[:], [[1, BLOCKS]], base=0, channel_multiplier=0))
                made(nc.gpsimd.tensor_copy(t_j[:], iota_blocks[:]))
                made(nc.gpsimd.iota(iota_blocks[:], [[BR, BLOCKS]], base=0, channel_multiplier=0))
                made(nc.gpsimd.tensor_copy(t_j_row[:], iota_blocks[:]))
                made(nc.gpsimd.memset(t_zero[:], 0.0))
                made(nc.gpsimd.memset(zeros[:], 0.0))
                made(nc.gpsimd.iota(iota_rows[:], [[4 * N, PAIRS], [2 * N, 2]], base=FILL, channel_multiplier=2))
                made(nc.gpsimd.tensor_copy(first_result[:], iota_rows[:]))
                made(nc.gpsimd.iota(fill_row[:], [[BR, BLOCKS], [1, 2]], base=TOPK, channel_multiplier=2))
                assert made.left == 0

            def inverse_deviation(moments, room, moments_done, room_done, done, q):
                b = q.mod(2)
                pool.wait_ge(moments_done, q.v + 1)
                nc.gpsimd.tensor_tensor(room[:, b], moments[:, b, :, 1], eps[:], ALU.add).then_inc(room_done, 1)
                pool.wait_ge(room_done, q.v + 1)
                nc.gpsimd.tensor_tensor(moments[:, b, :, 1], room[:, b], minus_half[:], ALU.pow).then_inc(done, 1)

            def step(s):
                if (s + 2).of(PAIRS):
                    inverse_deviation(mv, var, S["mv_done"], S["var_done"], S["rstd_done"], s + 2)
                if s.r is None and s.offset == 0:
                    more_constants()
                if s.r is None and s.offset == 1:
                    constants_of_routing()
                if (s - 4).of(PAIRS):
                    q = s - 4
                    wait_apart(pool, S["slots_done"], q.v + 1)
                    for n in range(2 * TOPK):
                        nc.gpsimd.indirect_dma_start(
                            out=sorted_x, out_offset=bass.IndirectOffsetOnAxis(
                                ap=slot_ring[:, q.mod(2), n:n + 1], axis=0),
                            in_=xn2[:, q.mod(4), n // TOPK, :], in_offset=None).then_inc(scattered[q.mod(2)], 16)
                if s.of(E * KC):
                    pool.wait_ge(S["w_hi"], s.v + 1)
                    nc.gpsimd.tensor_tensor(row_of(rw1l, s.v), wstage[:, s.mod(2), 0:2 * F], row_of(rw1h, s.v),
                                            ALU.subtract)
                    nc.gpsimd.tensor_tensor(row_of(rw2l, s.v), wstage[:, s.mod(2), 2 * F:2 * F + C],
                                            row_of(rw2h, s.v), ALU.subtract).then_inc(S["w_lo"], 1)
                if (s - 1).of(PAIRS):
                    inverse_deviation(mv2, var2, S["mv2_done"], S["var2_done"], S["rstd2_done"], s - 1)

            steps_a(pool, step)

            pool.wait_ge(S["table_done"], 1)
            for e in range(SP_PADS, E):
                pad(pool, e)

            def step(s):
                if (s - 2).of(BLOCKS):
                    j = s - 2
                    wait_apart(pool, S["yb_sb"], j.v + 1)
                    for a in range(2):
                        nc.gpsimd.indirect_dma_start(
                            out=routed, out_offset=bass.IndirectOffsetOnAxis(
                                ap=dest_ring[:, j.mod(2), a:a + 1], axis=0),
                            in_=yb[:, j.mod(2), a, :], in_offset=None).then_inc(y_stored[j.mod(2)], 16)

            steps_b(pool, step)

            pool.wait_ge(S["y_bias_sb"], E // 2 + 1)

            def step(s, lo, hi):
                if s.of(PAIRS):
                    q = s
                    y1 = yg_of(q, 1)
                    weights = row_of(keep, q.v)[:, 4:8].rearrange("p (t k) -> p t k", k=TOPK)[:, :, 1:2]
                    pool.wait_ge(y_loaded[q.mod(4)], q.div(4) * 16 + 16)
                    nc.gpsimd.tensor_tensor(y1, y1, weights.broadcast_to((P, 2, C)), ALU.mult)\
                        .then_inc(S["c_weighted"], 1)
                    wait_apart(pool, S["c_weighted"], q.v + 1)
                    if q.of(PAIRS, EARLY):
                        nc.gpsimd.tensor_tensor(y1, y1, shared_bias[:].unsqueeze(1).broadcast_to((P, 2, C)), ALU.add)\
                            .then_inc(S["c_biased"], 1)
                for q in summed(s):
                    if q.r is None and q.offset >= PAIRS - LAST:
                        continue
                    wait(pool, S["c_biased"], q.v + 1 - EARLY)
                    pool.wait_ge(S["c_added"], q.v + 1)
                    nc.gpsimd.tensor_tensor(yg_of(q, 0), yg_of(q, 0), yg_of(q, 1), ALU.add).then_inc(S["c_out"], 1)

            steps_c(pool, step, 0)

        @block.scalar
        def _(act):
            nc.scalar.preload_act_table(ACT.Exp)

            def copy(dst, src, **kw):
                return nc.scalar.activation(dst, src, ACT.Copy, **kw)

            act.wait_ge(S["prep_ps"], 1)
            copy(flat(tT[:, 0]), B_XT[:]).then_inc(S["prep_sb"], 1)
            act.wait_ge(S["prep_ps"], 2)
            copy(flat(cT[:, 0]), B_CT[:]).then_inc(S["prep_sb"], 1)
            act.wait_ge(S["prep_ps"], 3)
            copy(flat(wqkh[:]), B_TT[:], scale=SCALE).then_inc(S["prep_sb"], 1)

            def step(s):
                b = s.mod(2)
                if s.r is None and s.offset == PAIRS + 1:
                    act.wait_ge(S["shared_loaded"], 16 * 2 * KC)
                    act.wait_ge(S["z_ps"], PAIRS)
                    for k in range(KC):
                        copy(sw1h[:, k, :], wstage[:, k, 0:2 * F])
                        copy(sw2h[:, k, :], wstage[:, k, 2 * F:2 * F + C]).then_inc(S["shared_hi"], 1)
                if (s - 1).of(PAIRS):
                    q = s - 1
                    act.wait_ge(S["pT_ps"], q.v + 1)
                    wait(act, S["y_ps"], q.v - 1)
                    copy(pT[:, q.mod(2)], B_S[:, 2 * P:4 * P]).then_inc(S["pT_sb"], 1)
                if s.of(PAIRS):
                    act.wait_ge(S["tT_ps"], s.v + 1)
                    wait(act, S["s_ps"], s.v - 1)
                    copy(flat(tT[:, b]), B_TT[:]).then_inc(S["tT_sb"], 1)
                if (s + 1).of(PAIRS):
                    q = s + 1
                    act.wait_ge(S["xnT_ps"], q.v + 1)
                    wait(act, S["tT_ps"], q.v - 1)
                    copy(flat(xnTh[:, q.mod(2)]), B_XT[:]).then_inc(S["xnT_sb"], 1)
                if (s - 1).of(PAIRS):
                    q = s - 1
                    act.wait_ge(S["y_ps"], q.v + 1)
                    act.wait_ge(S["rinv_done"], q.v + 1)
                    wait(act, S["z_ps"], q.v - 1)
                    for t in range(2):
                        last = copy(yh[:, q.mod(2), t, :], B_Y[:, t * C:(t + 1) * C],
                                    scale=rinv[:, q.mod(2), t:t + 1])
                    last.then_inc(S["y_sb"], 1)
                if s.of(PAIRS):
                    act.wait_ge(S["v_ps"], s.v + 1)
                    wait(act, S["y_ps"], s.v - 1)
                    copy(flat(v[:, b]), B_V[:]).then_inc(S["v_sb"], 1)
                if s.of(E * KC):
                    act.wait_ge(wstage_loaded[b], (s.div(2) + 1) * 32)
                    copy(row_of(rw1h, s.v), wstage[:, b, 0:2 * F])
                    copy(row_of(rw2h, s.v), wstage[:, b, 2 * F:2 * F + C]).then_inc(S["w_hi"], 1)
                if (s - 2).of(PAIRS):
                    q = s - 2
                    act.wait_ge(S["xn2T_ps"], q.v + 1)
                    wait(act, S["gate_ps"], q.v - 1)
                    copy(flat(xn2T[:, q.mod(2)]), B_XT[:]).then_inc(S["xn2T_sb"], 1)
                if s.of(PAIRS):
                    act.wait_ge(S["max_done"], s.v + 1)
                    wait(act, S["pT_ps"], s.v - 1)
                    for t in range(2):
                        last = nc.scalar.activation(prob[:, b, t, :], B_S[:, t * P:(t + 1) * P], ACT.Exp,
                                                    bias=nmax[:, b, t:t + 1], accum_out=esum[:, b, t:t + 1])
                    last.then_inc(S["exp_done"], 1)
                if s.r is None and s.offset == 0:
                    act.wait_ge(S["small_loaded"], 48)
                    copy(wph[:], xn2[:, 3, :, 0:C]).then_inc(S["wp_hi"], 1)
                if (s - 2).of(PAIRS):
                    q = s - 2
                    act.wait_ge(S["glog_done"], q.v + 1)
                    nc.scalar.activation(gexp[:], glog[:], ACT.Exp).then_inc(S["gexp_done"], 1)
                if (s + 1).of(PAIRS):
                    q = s + 1
                    act.wait_ge(S["cT_ps"], q.v + 1)
                    wait(act, S["s_ps"], q.v - 1)
                    copy(flat(cT[:, q.mod(2)]), B_CT[:]).then_inc(S["cT_sb"], 1)

            steps_a(act, step)

            def shared_step(s, lo, hi):
                if (s + 1).of(hi, lo):
                    q = s + 1
                    act.wait_ge(S["c_T_ps"], q.v + 1)
                    wait(act, c_h_ps[1], q.v - 1)
                    copy(flat(cxh[:, q.mod(2)]), C_XT[:]).then_inc(S["c_hi"], 1)
                if (s + 2).of(hi, lo):
                    q = s + 2
                    wait(act, S["stats_kept"], min(q.offset + 1, PAIRS) if hi == EARLY else 0)
                    wait(act, S["c_T_ps"], q.v - 1)
                    for t in range(2):
                        last = nc.scalar.activation(cxn[:, q.mod(2), t, 0:C], row_of(xs, q.v * 2 + t), ACT.Identity,
                                                    bias=row_of(keep, q.v)[:, t:t + 1],
                                                    scale=row_of(keep, q.v)[:, 2 + t:3 + t])
                    last.then_inc(S["c_xn"], 1)
                if s.of(hi, lo):
                    for f in range(KF):
                        act.wait_ge(c_h_ps[f], s.v + 1)
                        wait(act, c_hid[f], s.v)
                        nc.scalar.activation(cgate[:, f], C_H[s.mod(2)][f][:, 0:2 * P], ACT.Silu,
                                             bias=sb1_s[:, f:f + 1]).then_inc(c_gated[f], 1)
                    for f in range(KF):
                        act.wait_ge(c_hid[f], s.v + 1)
                        wait(act, S["c_y_ps"], s.v - 1)
                        if s.r is None and s.offset == EARLY:
                            act.wait_ge(S["yb_ps"], BLOCKS)
                        copy(chidh[:, s.mod(2), f], chid[:, f]).then_inc(c_hid_hi[f], 1)

            act.wait_ge(S["hidden_bias_loaded"], 16)
            nc.scalar.preload_act_table(ACT.Silu)
            steps_early(shared_step)

            for i in range(2):
                act.wait_ge(scattered[i], 16 * 2 * TOPK * PAIRS // 2)
            for e in range(E):
                act.wait_ge(S["h_bias_ps"], e + 1)
                copy(h_bias[:, e], bias_bank(e)[:]).then_inc(S["h_bias_sb"], 1)

            def step(s):
                if s.r is None and s.offset in (BLOCKS - 1, BLOCKS):
                    if s.offset == BLOCKS - 1:
                        act.wait_ge(S["rows_lo"], BLOCKS)
                    shared_step(At(s.offset - BLOCKS + 1), EARLY, PAIRS)
                if (s + 1).of(BLOCKS):
                    j = s + 1
                    act.wait_ge(S["rowsT_ps"], j.v + 1)
                    wait(act, h_ps[1], j.v - 1)
                    copy(flat(xgh[:, j.mod(2)]), B_ROWS[j.mod(2)][:]).then_inc(S["rows_hi"], 1)
                def gate(a):
                    act.wait_ge(h_sb[a], s.v + 1)
                    nc.scalar.activation(hb[:, a, 0:F], hb[:, a, 0:F], ACT.Silu).then_inc(gated[a], 1)

                if s.of(BLOCKS):
                    gate(0)
                if (s - 1).of(BLOCKS):
                    j = s - 1
                    act.wait_ge(S["hidT_ps"], j.v + 1)
                    wait(act, S["yb_ps"], j.v - 1)
                    copy(flat(hidh[:, j.mod(2)]), B_HT[:]).then_inc(S["hid_hi"], 1)
                if s.of(BLOCKS):
                    gate(1)

            steps_b(act, step)

            steps_c(act, shared_step)

        @block.vector
        def _(dve):
            def row_stats(src, stats6, done, q):
                for t in range(2):
                    last = nc.vector.bn_stats(stats6[:, q.mod(2), t, :], row_of(src, q.v * 2 + t))
                last.then_inc(done, 1)

            def moments(stats6, out, stats_done, done, q):
                wait_apart(dve, stats_done, q.v + 1)
                for t in range(2):
                    last = nc.vector.bn_aggr(out[:, q.mod(2), t, :], stats6[:, q.mod(2), t, :])
                last.then_inc(done, 1)

            def normalise(dst, mom, q):
                for t in range(2):
                    last = nc.vector.tensor_scalar(dst[:, t, 0:C], row_of(xs, q.v * 2 + t), mom[:, t, 0:1],
                                                   mom[:, t, 1:2], ALU.subtract, ALU.mult)
                return last

            def split_shared(k):
                dve.wait_ge(S["shared_hi"], k + 1)
                nc.vector.tensor_tensor(sw1l[:, k, :], wstage[:, k, 0:2 * F], sw1h[:, k, :], ALU.subtract)\
                    .then_inc(S["shared_lo"], 1)

            def split_bias():
                dve.wait_ge(S["bias_loaded"], 16 * 6)
                dve.wait_ge(S["pool_made"], 5)
                link = Links(dve, S["bias_split"], 5, 0)
                rows = E + 3
                link(nc.vector.tensor_copy(bias[0:rows, :], braw[:]))
                link(nc.vector.tensor_tensor(brest[:], braw[:], bias[0:rows, :], ALU.subtract))
                link(nc.vector.tensor_copy(bpart[:], brest[:]))
                nc.vector.tensor_copy(bias[32:32 + rows, :], brest[:])
                link(nc.vector.tensor_tensor(braw[:], brest[:], bpart[:], ALU.subtract))
                link(nc.vector.tensor_copy(bias[64:64 + rows, :], braw[:]))

            def step(s):
                b = s.mod(2)
                r, x_next, last_q = s - 3, s + 2, s - 1
                routed, prepared = r.of(PAIRS), x_next.of(PAIRS)
                if last_q.of(PAIRS):
                    dve.wait_ge(S["exp_done"], s.v)
                    wait(dve, S["y_sb"], s.v - 2)
                    nc.vector.reciprocal(rinv[:, last_q.mod(2), :], esum[:, last_q.mod(2), :])\
                        .then_inc(S["rinv_done"], 1)
                if s.r is None and s.offset == 1:
                    split_bias()
                    dve.wait_ge(S["wp_hi"], 1)
                    nc.vector.tensor_tensor(wpl[:], xn2[:, 3, :, 0:C], wph[:], ALU.subtract)\
                        .then_inc(S["wp_lo"], 1)
                if s.r is None and s.offset == 3:
                    dve.wait_ge(S["pool_made"], POOL_MADE)
                if routed:
                    dve.wait_ge(S["gexp_done"], r.v + 1)
                    nc.vector.tensor_reduce(gsum[:], gexp[:], AX, ALU.add).then_inc(S["gsum_made"], 1)
                if prepared:
                    i = x_next.mod(2)
                    wait_apart(dve, x_loaded[i], x_next.div(2) * 16 + 16)
                    nc.vector.bn_stats(bn[:, i, 0, :], row_of(xs, x_next.v * 2))
                if routed:
                    dve.wait_ge(S["gsum_made"], r.v + 1)
                    nc.vector.reciprocal(ginv[:], gsum[:]).then_inc(S["ginv_made"], 1)
                if prepared:
                    nc.vector.bn_stats(bn[:, i, 1, :], row_of(xs, x_next.v * 2 + 1)).then_inc(S["bn_done"], 1)
                if (s - 2).of(PAIRS):
                    q = s - 2
                    dve.wait_ge(S["rstd2_done"], q.v + 1)
                    if (q - 4).of(PAIRS):
                        dve.wait_ge(scattered[q.mod(2)], (q - 4).div(2) * (32 * TOPK) + 32 * TOPK)
                    normalise(xn2[:, q.mod(4)], mv2[:, q.mod(2)], q).then_inc(S["xn2_done"], 1)
                    m2 = mv2[:, q.mod(2)]
                    nc.vector.scalar_tensor_tensor(row_of(keep, q.v)[:, 0:2], m2[:, :, 0], -1.0, m2[:, :, 1],
                                                   ALU.mult, ALU.mult)
                    nc.vector.tensor_copy(row_of(keep, q.v)[:, 2:4], m2[:, :, 1]).then_inc(S["stats_kept"], 1)
                if routed:
                    dve.wait_ge(S["ginv_made"], r.v + 1)
                    nc.vector.tensor_tensor(gprob[:], gexp[:], ginv[:].unsqueeze(2).broadcast_to((P, 2, E)),
                                            ALU.mult).then_inc(S["gprob_made"], 1)
                if prepared:
                    wait(dve, S["xn_done"], x_next.v - 1)
                    moments(bn, mv, S["bn_done"], S["mv_done"], x_next)
                if routed:
                    wait_apart(dve, S["gprob_made"], r.v + 1)
                    nc.vector.max(top8[:, 0, :], gprob[:, 0, :])
                    nc.vector.max(top8[:, 1, :], gprob[:, 1, :]).then_inc(S["top_made"], 1)
                if s.r is None and s.offset == -1:
                    dve.wait_ge(S["prep_sb"], 3)
                    nc.vector.scalar_tensor_tensor(flat(wqkl[:]), B_TT[:], SCALE, flat(wqkh[:]), ALU.mult,
                                                   ALU.subtract).then_inc(S["wqk_lo"], 1)
                if (s + 1).of(PAIRS):
                    q = s + 1
                    dve.wait_ge(S["xnT_sb"], q.v + 1)
                    wait(dve, S["tT_ps"], q.v)
                    nc.vector.tensor_tensor(flat(xnTl[:]), B_XT[:], flat(xnTh[:, q.mod(2)]), ALU.subtract)\
                        .then_inc(S["xnT_lo"], 1)
                if routed:
                    wait_apart(dve, S["top_made"], r.v + 1)
                    nc.vector.max_index(topi[:, 0, :], top8[:, 0, :], gprob[:, 0, :])
                    nc.vector.max_index(topi[:, 1, :], top8[:, 1, :], gprob[:, 1, :]).then_inc(S["topi_made"], 1)
                    dve.wait_ge(S["topi_made"], r.v + 1)
                    nc.vector.tensor_copy(topf[:], topi[:]).then_inc(S["topf_made"], 1)
                if last_q.of(PAIRS):
                    i = last_q.mod(2)
                    dve.wait_ge(S["y_sb"], s.v)
                    wait(dve, S["z_ps"], s.v - 2)
                    for t in range(2):
                        last = nc.vector.scalar_tensor_tensor(yl[:, i, t, :], B_Y[:, t * C:(t + 1) * C],
                                                              rinv[:, i, t:t + 1], yh[:, i, t, :],
                                                              ALU.mult, ALU.subtract)
                    last.then_inc(S["y_lo"], 1)
                if routed:
                    dve.wait_ge(S["topf_made"], r.v + 1)
                    nc.vector.tensor_tensor(
                        hot[:], expert_of[:].unsqueeze(1).unsqueeze(1).broadcast_to((P, 2, TOPK, E)),
                        topf[:, :, 0:TOPK].unsqueeze(3).broadcast_to((P, 2, TOPK, E)), ALU.is_equal)\
                        .then_inc(S["hot_made"], 1)
                    dve.wait_ge(S["hot_made"], r.v + 1)
                    nc.vector.tensor_tensor(both[:], hot[:, :, 0, :], hot[:, :, 1, :], ALU.add)\
                        .then_inc(S["hot_done"], 1)
                if s.r is None and s.offset == PAIRS + 1:
                    split_shared(0)
                if prepared:
                    dve.wait_ge(S["rstd_done"], x_next.v + 1)
                    wait(dve, S["xnT_ps"], x_next.v - 1)
                    normalise(xn[:, x_next.mod(2)], mv[:, x_next.mod(2)], x_next).then_inc(S["xn_done"], 1)
                if routed:
                    dve.wait_ge(S["place_ps"], r.v + 1)
                    nc.vector.tensor_tensor(place[:], B_R[:, 64:64 + 2 * E].rearrange("p (t e) -> p t e", t=2),
                                            counts[:].unsqueeze(1).broadcast_to((P, 2, E)), ALU.add)\
                        .then_inc(S["counted"], 1)
                    dve.wait_ge(S["counted"], r.v + 1)
                    nc.vector.tensor_tensor(counts[:], B_R[:, 64 + 2 * E:64 + 3 * E], counts[:], ALU.add)\
                        .then_inc(S["counts_added"], 1)
                    nc.vector.tensor_tensor(hotplace[:], hot[:], place[:].unsqueeze(2).broadcast_to((P, 2, TOPK, E)),
                                            ALU.mult).then_inc(S["hotplace_made"], 1)
                if routed:
                    dve.wait_ge(S["hotplace_made"], r.v + 1)
                    nc.vector.tensor_reduce(slotf[:], hotplace[:].rearrange("p t k e -> p (t k) e"),
                                            AX, ALU.add).then_inc(S["slotf_made"], 1)
                if (s - 1).of(PAIRS):
                    q = s - 1
                    dve.wait_ge(S["z_ps"], q.v + 1)
                    nc.vector.tensor_tensor(two(xs, q), B_Z[:].rearrange("p (t c) -> p t c", t=2), two(xs, q),
                                            ALU.add).then_inc(S["x2_done"], 1)
                if s.of(PAIRS):
                    dve.wait_ge(S["s_ps"], s.v + 1)
                    nc.vector.tensor_reduce(nmax[:, b, :], B_S[:, 0:2 * P].rearrange("p (t m) -> p t m", t=2),
                                            AX, ALU.max, negate=True).then_inc(S["max_done"], 1)
                if (s - 1).of(PAIRS):
                    wait_apart(dve, S["x2_done"], q.v + 1)
                    row_stats(xs, bn2, S["bn2_done"], q)
                if routed:
                    if (r - 2).of(PAIRS):
                        dve.wait_ge(scattered[r.mod(2)], (r - 2).div(2) * (32 * TOPK) + 32 * TOPK)
                    wait_apart(dve, S["slotf_made"], r.v + 1)
                    nc.vector.tensor_copy(xn2[:, r.mod(4), :, C], row_of(first_result, r.v))
                    nc.vector.tensor_copy(xn2[:, r.mod(4), :, C + 1], topf[:, :, 0])
                    nc.vector.tensor_copy(slot_ring[:, r.mod(2)], slotf[:])
                    nc.vector.tensor_copy(row_of(keep, r.v)[:, 4:8].rearrange("p (t k) -> p t k", t=2),
                                          top8[:, :, 0:TOPK]).then_inc(S["slots_done"], 1)
                if (s - 1).of(PAIRS):
                    wait(dve, S["stats_kept"], q.v - 1)
                    moments(bn2, mv2, S["bn2_done"], S["mv2_done"], q)
                if s.r is None and s.offset == PAIRS + 1:
                    split_shared(1)
                if (s - 2).of(PAIRS):
                    q = s - 2
                    dve.wait_ge(S["gate_ps"], q.v + 1)
                    logits = B_R[:, 0:2 * E].rearrange("p (t e) -> p t e", t=2)
                    nc.vector.tensor_reduce(gmax[:], logits, AX, ALU.max).then_inc(S["gmax_done"], 1)
                    dve.wait_ge(S["gmax_done"], q.v + 1)
                    wait(dve, S["gexp_done"], q.v)
                    nc.vector.tensor_tensor(glog[:], logits, gmax[:].unsqueeze(2).broadcast_to((P, 2, E)),
                                            ALU.subtract).then_inc(S["glog_done"], 1)

            steps_a(dve, step)

            def shared_step(s, lo, hi):
                if (s - 2).of(hi, lo):
                    q = s - 2
                    dve.wait_ge(S["c_y_ps"], q.v + 1)
                    nc.vector.tensor_tensor(two(xs, q), C_Y[q.mod(2)][:].rearrange("p (t c) -> p t c", t=2),
                                            two(xs, q), ALU.add).then_inc(S["c_base"], 1)
                if (s + 1).of(hi, lo):
                    q = s + 1
                    dve.wait_ge(S["c_hi"], q.v + 1)
                    wait(dve, c_h_ps[1], q.v - 1)
                    nc.vector.tensor_tensor(flat(cxl[:, q.mod(2)]), C_XT[:], flat(cxh[:, q.mod(2)]), ALU.subtract)\
                        .then_inc(S["c_lo"], 1)
                if s.of(hi, lo):
                    i = s.mod(2)
                    for f in range(KF):
                        dve.wait_ge(c_gated[f], s.v + 1)
                        if f == 0:
                            wait(dve, S["c_hid_lo"], s.v)
                        nc.vector.scalar_tensor_tensor(chid[:, f], C_H[i][f][:, 2 * P:4 * P],
                                                       sb1_s[:, KF + f:KF + f + 1], cgate[:, f],
                                                       ALU.add, ALU.mult).then_inc(c_hid[f], 1)
                for q in summed(s) if hi == PAIRS else ():
                    wait(dve, S["c_base"], q.v + 1)
                    dve.wait_ge(y_loaded[q.mod(4)], q.div(4) * 16 + 16)
                    for t in range(2):
                        y0 = yg_of(q, 0)[:, t, :]
                        last = nc.vector.scalar_tensor_tensor(y0, y0, row_of(keep, q.v)[:, 4 + 2 * t:5 + 2 * t],
                                                              row_of(xs, q.v * 2 + t), ALU.mult, ALU.add)
                    last.then_inc(S["c_added"], 1)
                    if q.r is None and q.offset >= PAIRS - LAST:
                        dve.wait_ge(S["c_biased"], q.v + 1 - EARLY)
                        dve.wait_ge(S["c_added"], q.v + 1)
                        nc.vector.tensor_tensor(yg_of(q, 0), yg_of(q, 0), yg_of(q, 1), ALU.add)\
                            .then_inc(S["c_last_out"], 1)
                if s.of(hi, lo):
                    for f in range(KF):
                        dve.wait_ge(c_hid_hi[f], s.v + 1)
                        last = nc.vector.tensor_tensor(chidl[:, i, f], chid[:, f], chidh[:, i, f], ALU.subtract)
                    last.then_inc(S["c_hid_lo"], 1)

            steps_early(shared_step, -2, 0)

            dve.wait_ge(S["slots_done"], PAIRS)
            link = Links(dve, S["table_link"], TABLE_LINKS, 0)
            link(nc.vector.tensor_tensor(t_n[:], counts[:], t_base[:], ALU.subtract))
            link(nc.vector.tensor_copy(pad_row[:], counts[0:1, :]))
            link(nc.vector.tensor_scalar(t_ni[:], t_n[:], float(BR - 1), None, ALU.add))
            link(nc.vector.tensor_scalar(t_nr[:], t_ni[:], BR.bit_length() - 1, None, ALU.arith_shift_right))
            link(nc.vector.tensor_copy(t_nb[:], t_nr[:]))
            nc.vector.tensor_scalar(t_skip[:], t_nb[:], -float(BR), float(CAP), ALU.mult, ALU.add)
            link(nc.vector.tensor_tensor_scan(t_cum[:], t_nb[:], t_zero[:], 0.0, ALU.add, ALU.add))
            over = (1, BLOCKS, E)
            link(nc.vector.tensor_tensor(t_ge[:], t_cum[0:1, :].unsqueeze(1).broadcast_to(over),
                                         t_j[:].unsqueeze(2).broadcast_to(over), ALU.is_le))
            link(nc.vector.tensor_reduce(t_e[:], t_ge[:], AX, ALU.add))
            nc.vector.tensor_scalar(block_expert[:], t_e[:], float(E - 1), None, ALU.min)
            link(nc.vector.tensor_tensor(t_ge[:], t_ge[:], t_skip[0:1, :].unsqueeze(1).broadcast_to(over), ALU.mult))
            link(nc.vector.tensor_reduce(t_before[:], t_ge[:], AX, ALU.add))
            nc.vector.tensor_tensor(block_row[:], t_before[:], t_j_row[:], ALU.add).then_inc(S["table_done"], 1)
            assert link.left == 0

            nc.vector.tensor_tensor(sw2l[:], wstage[:, :, 2 * F:2 * F + C], sw2h[:], ALU.subtract)\
                .then_inc(S["shared_lo2"], 1)

            dve.wait_ge(S["hidden_bias_loaded"], 16)
            def y_biases(n0, n1):
                for n in range(n0, n1):
                    dve.wait_ge(S["y_bias_ps"], n + 1)
                    nc.vector.tensor_copy(flat(y_bias[:, 2 * n:2 * n + 2]), y_bias_banks[n][:])\
                        .then_inc(S["y_bias_sb"], 1)

            steps_early(shared_step, 0, EARLY + 1)
            y_biases(0, 2)
            steps_early(shared_step, EARLY + 1)
            y_biases(2, 4)
            dve.wait_ge(S["y_bias_ps"], E // 2 + 1)
            nc.vector.tensor_copy(shared_bias[:], y_bias_banks[2][:, 0:C]).then_inc(S["y_bias_sb"], 1)

            def step(s):
                if s.r is None and s.offset >= BLOCKS - 1:
                    shared_step(At(s.offset - BLOCKS + 1), EARLY, PAIRS)
                if (s + 1).of(BLOCKS):
                    j = s + 1
                    dve.wait_ge(S["rows_hi"], j.v + 1)
                    nc.vector.tensor_copy(tags[:, j.mod(2)], xg[:, j.mod(2), :, C:CX])
                    wait(dve, h_ps[1], j.v - 1)
                    nc.vector.tensor_tensor(flat(xgl[:, j.mod(2)]), B_ROWS[j.mod(2)][:],
                                            flat(xgh[:, j.mod(2)]), ALU.subtract).then_inc(S["rows_lo"], 1)
                if s.of(BLOCKS):
                    e = expert_of_block(dve, s)
                    for a in range(2):
                        dve.wait_ge(h_ps[a], s.v + 1)
                        if a == 0:
                            wait(dve, S["hid_done"], s.v)
                        nc.vector.tensor_tensor(hb[:, a], B_H[s.mod(2)][a][:], row_of(h_bias, e), ALU.add)\
                            .then_inc(h_sb[a], 1)
                        if a == 0:
                            i = s.mod(2)
                            nc.vector.scalar_tensor_tensor(row_of(dest, s.v), tags[:, i, :, 1],
                                                           expert_of[:, bass.ds(e, 1)], tags[:, i, :, 0],
                                                           ALU.not_equal, ALU.add)
                if (s - 1).of(BLOCKS):
                    j = s - 1
                    dve.wait_ge(S["hid_hi"], j.v + 1)
                    wait(dve, S["yb_ps"], j.v - 1)
                    nc.vector.tensor_tensor(flat(hidl[:, j.mod(2)]), B_HT[:], flat(hidh[:, j.mod(2)]), ALU.subtract)\
                        .then_inc(S["hid_lo"], 1)
                if s.of(BLOCKS):
                    dve.wait_ge(gated[1], s.v + 1)
                    wait(dve, S["hidT_ps"], s.v)
                    nc.vector.tensor_tensor(hid[:], hb[:, :, 0:F], hb[:, :, F:2 * F], ALU.mult)\
                        .then_inc(S["hid_done"], 1)
                if (s - 2).of(BLOCKS):
                    j = s - 2
                    e = expert_of_block(dve, j)
                    dve.wait_ge(S["yb_ps"], j.v + 1)
                    wait(dve, y_stored[j.mod(2)], j.div(2) * 32)
                    nc.vector.tensor_tensor(yb[:, j.mod(2)], B_YB[:].rearrange("p (t c) -> p t c", t=2),
                                            row_of(y_bias, e).unsqueeze(1).broadcast_to((P, 2, C)), ALU.add)
                    nc.vector.tensor_tensor(dest_ring[:, j.mod(2)], row_of(dest, j.v), row_of(fill_row, j.v), ALU.max)\
                        .then_inc(S["yb_sb"], 1)

            steps_b(dve, step)

            steps_c(dve, shared_step, EARLY + 1)

        @block.tensor
        def _(pe):
            def mm(out_, lhsT, rhs, first, last):
                return nc.tensor.matmul(out_, lhsT, rhs, start=first, stop=last)

            def mm3(out_, lh, ll, rh, rl, first, last):
                mm(out_, ll, rh, first, False)
                mm(out_, lh, rl, False, False)
                return mm(out_, lh, rh, False, last)

            def add_bias(out_, e, c0, c1):
                mm(out_, sel[:, e, :], bias[:, c0:c1], True, False)

            pe.wait_ge(S["attn_w_loaded"], 32)
            pe.wait_ge(S["pool_made"], 4)
            for i, bank in ((0, B_XT), (1, B_CT)):
                for a in range(KC):
                    for k in range(KC):
                        last = nc.tensor.transpose(bank[:, k * C + a * P:k * C + (a + 1) * P],
                                                   wstage[:, i, a * C + k * P:a * C + (k + 1) * P], ident[:])
                last.then_inc(S["prep_ps"], 1)
            pe.wait_ge(S["prep_sb"], 2)
            for a in range(KC):
                for k in range(KC):
                    last = mm(B_TT[:, a * C:(a + 1) * C], tT[:, 0, k, a * P:(a + 1) * P], cT[:, 0, k, :],
                              k == 0, k == KC - 1)
            last.then_inc(S["prep_ps"], 1)

            def transposes(bank, src):
                for t in range(2):
                    for k in range(KC):
                        last = nc.tensor.transpose(bank[:, k * 2 * P + t * P:k * 2 * P + (t + 1) * P],
                                                   src[:, t, k * P:(k + 1) * P], ident[:])
                return last

            def step(s):
                b = s.mod(2)
                if (s - 1).of(PAIRS):
                    q = s - 1
                    pe.wait_ge(S["exp_done"], q.v + 1)
                    for t in range(2):
                        last = nc.tensor.transpose(B_S[:, (2 + t) * P:(3 + t) * P], prob[:, q.mod(2), t, :], ident[:])
                    last.then_inc(S["pT_ps"], 1)
                if s.of(PAIRS):
                    wait(pe, S["wqk_lo"], 1)
                    pe.wait_ge(S["xnT_lo"], s.v + 1)
                    wait(pe, S["tT_sb"], s.v)
                    for c in range(KC):
                        cols = slice(c * P, (c + 1) * P)
                        for k in range(KC):
                            last = mm3(B_TT[:, c * 2 * P:(c + 1) * 2 * P], wqkh[:, k, cols], wqkl[:, k, cols],
                                       xnTh[:, b, k, :], xnTl[:, k, :], k == 0, k == KC - 1)
                    last.then_inc(S["tT_ps"], 1)
                if (s + 1).of(PAIRS):
                    q = s + 1
                    pe.wait_ge(S["xn_done"], q.v + 1)
                    wait(pe, S["xn2T_sb"], s.v - 2)
                    transposes(B_XT, xn[:, q.mod(2)]).then_inc(S["xnT_ps"], 1)
                if (s - 1).of(PAIRS):
                    q = s - 1
                    pe.wait_ge(S["pT_sb"], q.v + 1)
                    pe.wait_ge(S["v_sb"], q.v + 1)
                    wait(pe, S["y_lo"], q.v)
                    for t in range(2):
                        last = mm(B_Y[:, t * C:(t + 1) * C], pT[:, q.mod(2), t * P:(t + 1) * P],
                                  v[:, q.mod(2), t, :], True, True)
                    last.then_inc(S["y_ps"], 1)
                if s.of(PAIRS):
                    wait(pe, S["small_loaded"], 48)
                    pe.wait_ge(S["cT_sb"], s.v + 1)
                    wait(pe, S["v_sb"], s.v)
                    for t in range(2):
                        for k in range(KC):
                            last = mm(B_V[:, t * C:(t + 1) * C], cT[:, b, k, t * P:(t + 1) * P], wv_s[:, k, :],
                                      k == 0, k == KC - 1)
                    last.then_inc(S["v_ps"], 1)
                if (s - 2).of(PAIRS):
                    q = s - 2
                    pe.wait_ge(S["xn2_done"], q.v + 1)
                    if (s + 1).of(PAIRS):
                        pe.wait_ge(S["xnT_lo"], s.v + 2)
                    transposes(B_XT, xn2[:, q.mod(4)]).then_inc(S["xn2T_ps"], 1)
                if (s - 3).of(PAIRS):
                    q = s - 3
                    pe.wait_ge(S["hot_done"], q.v + 1)
                    r0 = 64
                    mm(B_R[:, r0:r0 + E], below[:], both[:, 0, :], True, True)
                    mm(B_R[:, r0 + E:r0 + 2 * E], below[:], both[:, 1, :], True, False)
                    mm(B_R[:, r0 + E:r0 + 2 * E], ones[:], both[:, 0, :], False, True)
                    mm(B_R[:, r0 + 2 * E:r0 + 3 * E], ones[:], both[:, 0, :], True, False)
                    mm(B_R[:, r0 + 2 * E:r0 + 3 * E], ones[:], both[:, 1, :], False, True).then_inc(S["place_ps"], 1)
                if (s - 1).of(PAIRS):
                    q = s - 1
                    if s.r is None:
                        pe.wait_ge(S["bias_split"], 5)
                        pe.wait_ge(S["pool_made"], 11)
                        pe.wait_ge(S["wp_lo"], 1)
                    pe.wait_ge(S["y_lo"], q.v + 1)
                    wait(pe, S["x2_done"], q.v)
                    halves_h, halves_l = (t_[:, q.mod(2)].rearrange("p t (r h) -> p t h r", h=2) for t_ in (yh, yl))
                    for t in range(2):
                        add_bias(B_Z[:, t * C:(t + 1) * C], E + 1, 0, C)
                        for h in range(2):
                            last = mm3(B_Z[:, t * C:(t + 1) * C], halves_h[:, t, h, :], halves_l[:, t, h, :],
                                       wph[:, h, :], wpl[:, h, :], False, h == 1)
                    last.then_inc(S["z_ps"], 1)
                if s.of(PAIRS):
                    pe.wait_ge(S["tT_sb"], s.v + 1)
                    wait(pe, S["pT_sb"], s.v)
                    for t in range(2):
                        for k in range(KC):
                            last = mm(B_S[:, t * P:(t + 1) * P], tT[:, b, k, t * P:(t + 1) * P],
                                      cT[:, b, k, t * P:(t + 1) * P], k == 0, k == KC - 1)
                    last.then_inc(S["s_ps"], 1)
                if (s - 2).of(PAIRS):
                    q = s - 2
                    pe.wait_ge(S["xn2T_sb"], q.v + 1)
                    wait(pe, S["counts_added"], q.v)
                    for t in range(2):
                        add_bias(B_R[:, t * E:(t + 1) * E], E + 2, 0, E)
                        for k in range(KC):
                            last = mm(B_R[:, t * E:(t + 1) * E], xn2T[:, q.mod(2), k, t * P:(t + 1) * P],
                                      gw_s[:, k, :], False, k == KC - 1)
                    last.then_inc(S["gate_ps"], 1)
                if (s + 1).of(PAIRS):
                    q = s + 1
                    pe.wait_ge(ctx_loaded[q.mod(2)], q.div(2) * 16 + 16)
                    transposes(B_CT, cx[:, q.mod(2)]).then_inc(S["cT_ps"], 1)

            steps_a(pe, step)

            def shared_step(s, lo, hi):
                if (s + 1).of(hi, lo):
                    q = s + 1
                    pe.wait_ge(S["c_xn"], q.v + 1)
                    wait(pe, S["c_lo"], q.v)
                    transposes(C_XT, cxn[:, q.mod(2)]).then_inc(S["c_T_ps"], 1)
                if s.of(hi, lo):
                    b = s.mod(2)
                    pe.wait_ge(S["c_lo"], s.v + 1)
                    wait(pe, c_hid[1], s.v - 1)
                    for f in range(KF):
                        for half in range(2):
                            o = C_H[b][f][:, half * 2 * P:(half + 1) * 2 * P]
                            c0 = half * F + f * P
                            for k in range(KC):
                                last = mm3(o, sw1h[:, k, c0:c0 + P], sw1l[:, k, c0:c0 + P], cxh[:, b, k, :],
                                           cxl[:, b, k, :], k == 0, k == KC - 1)
                        last.then_inc(c_h_ps[f], 1)
                if (s - 1).of(hi, lo):
                    q = s - 1
                    b = q.mod(2)
                    pe.wait_ge(S["c_hid_lo"], q.v + 1)
                    if hi == EARLY:
                        pe.wait_ge(S["shared_lo2"], 1)
                    wait(pe, S["c_base"], q.v - 1)
                    if q.r is None and q.offset == EARLY + 1:
                        pe.wait_ge(S["yb_sb"], BLOCKS)
                    for t in range(2):
                        o = C_Y[b][:, t * C:(t + 1) * C]
                        if hi == EARLY:
                            add_bias(o, E, 2 * F, 2 * F + C)
                        for k in range(KF):
                            last = mm3(o, chidh[:, b, k, t * P:(t + 1) * P], chidl[:, b, k, t * P:(t + 1) * P],
                                       sw2h[:, k, :], sw2l[:, k, :], hi != EARLY and k == 0, k == KF - 1)
                    last.then_inc(S["c_y_ps"], 1)

            def h_biases(e0, e1):
                for e in range(e0, e1):
                    wait(pe, S["h_bias_sb"], e - 3)
                    mm(bias_bank(e)[:], sel[:, e, :], bias[:, 0:2 * F], True, True).then_inc(S["h_bias_ps"], 1)

            def y_biases(n0, n1):
                for n in range(n0, n1):
                    for i in range(2):
                        last = mm(y_bias_banks[n][:, i * C:(i + 1) * C], sel[:, 2 * n + i, :],
                                  bias[:, 2 * F:2 * F + C], True, True)
                    last.then_inc(S["y_bias_ps"], 1)

            pe.wait_ge(S["shared_lo"], KC)
            steps_early(shared_step, end=EARLY)
            pe.wait_ge(c_hid[1], EARLY)
            h_biases(0, 4)
            pe.wait_ge(S["c_lo"], EARLY)
            y_biases(0, 2)
            steps_early(shared_step, EARLY)
            h_biases(4, E)
            pe.wait_ge(S["c_base"], EARLY)
            y_biases(2, 4)
            pe.wait_ge(S["y_bias_sb"], 3)
            mm(y_bias_banks[2][:, 0:C], sel[:, E, :], bias[:, 2 * F:2 * F + C], True, True)\
                .then_inc(S["y_bias_ps"], 1)

            pe.wait_ge(S["table_done"], 1)
            pe.wait_ge(S["w_lo"], E * KC)
            pe.wait_ge(S["h_bias_sb"], E)
            pe.wait_ge(S["y_bias_sb"], 2)

            def step(s):
                if s.r is None and s.offset >= BLOCKS - 1:
                    shared_step(At(s.offset - BLOCKS + 1), EARLY, PAIRS)
                if (s + 1).of(BLOCKS):
                    j = s + 1
                    i = j.mod(2)
                    pe.wait_ge(rows_loaded[i], j.div(2) * 16 + 16)
                    wait(pe, S["rows_lo"], j.v - 1)
                    transposes(B_ROWS[i], xg[:, i]).then_inc(S["rowsT_ps"], 1)
                if s.of(BLOCKS):
                    i = s.mod(2)
                    e = expert_of_block(pe, s)
                    pe.wait_ge(S["rows_lo"], s.v + 1)
                    wait(pe, h_sb[1], s.v - 1)
                    for a in range(2):
                        rows = slice(a * P, (a + 1) * P)
                        for k in range(KC):
                            last = mm3(B_H[i][a][:], xgh[:, i, k, rows], xgl[:, i, k, rows],
                                       row_of(rw1h, e * KC + k), row_of(rw1l, e * KC + k), k == 0, k == KC - 1)
                        last.then_inc(h_ps[a], 1)
                if (s - 1).of(BLOCKS):
                    j = s - 1
                    if s.r is None and j.offset == 0:
                        pe.wait_ge(S["y_bias_sb"], E // 2 + 1)
                    pe.wait_ge(S["hid_done"], j.v + 1)
                    wait(pe, S["hid_lo"], j.v)
                    transposes(B_HT, hid).then_inc(S["hidT_ps"], 1)
                if (s - 2).of(BLOCKS):
                    j = s - 2
                    i = j.mod(2)
                    e = expert_of_block(pe, j)
                    pe.wait_ge(S["hid_lo"], j.v + 1)
                    wait(pe, S["yb_sb"], j.v)
                    for a in range(2):
                        rows, o = slice(a * P, (a + 1) * P), B_YB[:, a * C:(a + 1) * C]
                        for k in range(KF):
                            last = mm3(o, hidh[:, i, k, rows], hidl[:, i, k, rows], row_of(rw2h, e * KF + k),
                                       row_of(rw2l, e * KF + k), k == 0, k == KF - 1)
                    last.then_inc(S["yb_ps"], 1)

            steps_b(pe, step)

            steps_c(pe, shared_step, EARLY + 1)


_INS = ['x', 'ctx_1024', 'L0_xattn_Wq', 'L0_xattn_Wk', 'L0_xattn_Wv', 'L0_xattn_Wp', 'L0_xattn_bp',
        'L0_ffn_gate_w', 'L0_ffn_gate_b', 'L0_ffn_sw1', 'L0_ffn_sb1', 'L0_ffn_sw2', 'L0_ffn_sb2',
        'L0_ffn_rw1', 'L0_ffn_rb1', 'L0_ffn_rw2', 'L0_ffn_rb2']


def kernel(**inputs):
    import numpy as _np
    import concourse.bacc as _bacc
    from concourse import mybir as _mybir
    from concourse.bass_utils import run_bass_kernel_spmd as _run

    nc = _bacc.Bacc("TRN2", target_bir_lowering=False, num_devices=1)
    arrays, args = {}, []
    for name in _INS:
        a = _np.ascontiguousarray(inputs[name])
        arrays[f"in_{name}"] = a
        args.append(nc.dram_tensor(f"in_{name}", a.shape, _mybir.dt.from_np(a.dtype), kind="ExternalInput").ap())
    shape = tuple(inputs['x'].shape)
    args.append(nc.dram_tensor("out_0", shape, _mybir.dt.float32, kind="ExternalOutput").ap())
    cross_attention_moe_kernel(nc, *args)
    r = _run(nc, [arrays], core_ids=[0])
    return r.results[0]["out_0"]
```
